# Optimizing a Trainium2 kernel written in Bass

```python
import numpy as np
import jax
import jax.numpy as jnp

def _softmax(x, axis=-1):
    return jax.nn.softmax(x, axis=axis)

def _gelu(x):
    return jax.nn.gelu(x, approximate=True)

def _silu(x):
    return jax.nn.silu(x)

def _sigmoid(x):
    return jax.nn.sigmoid(x)

def _layernorm(x, axis=-1, eps=1e-05):
    m = jnp.mean(x, axis=axis, keepdims=True)
    v = jnp.var(x, axis=axis, keepdims=True)
    return (x - m) / jnp.sqrt(v + eps)

def _scatter_add(tgt, idx, src, axis=0):
    return tgt.at[idx].add(src)

def _segment_sum(src, seg, n):
    return jax.ops.segment_sum(src, seg, n)
kernel_name = 'mk_macaron_d2_jaxref_r8_c2bab6'

def setup_inputs(seed: int=0):
    np.random.seed(seed)
    _w = jnp.asarray

    def _L0_attn_setup():
        import jax, jax.numpy as jnp
        import numpy as np
        DIM = 128
        NUM_HEADS = 16
        HEAD_DIM = DIM // NUM_HEADS
        ROPE_BASE = 10000.0

        def rope_cos_sin(seq_len, dim):
            inv_freq = 1.0 / ROPE_BASE ** (jnp.arange(0, dim, 2, dtype=jnp.float32) / dim)
            t = jnp.arange(seq_len, dtype=jnp.float32)
            freqs = t[:, None] * inv_freq[None, :]
            emb = jnp.concatenate([freqs, freqs], axis=-1)
            return (jnp.cos(emb), jnp.sin(emb))

        def apply_rotary(x, cos, sin):
            x1 = x[..., ::2]
            x2 = x[..., 1::2]
            x_rot = jnp.stack((-x2, x1), axis=-1).reshape(x.shape)
            return x * cos + x_rot * sin
        key = jax.random.key(seed)
        ks = jax.random.split(key, 5)
        B, L, C = (4, 256, DIM)
        s = 1.0 / np.sqrt(C)
        return {'x': jax.random.normal(ks[0], (B, L, C), dtype=jnp.float32), 'qkv_w': jax.random.normal(ks[1], (3 * C, C), dtype=jnp.float32) * s, 'qkv_b': jax.random.normal(ks[2], (3 * C,), dtype=jnp.float32) * 0.02, 'proj_w': jax.random.normal(ks[3], (C, C), dtype=jnp.float32) * s, 'proj_b': jax.random.normal(ks[4], (C,), dtype=jnp.float32) * 0.02}
    _L0_attn_in = _L0_attn_setup()

    def _L0_ffn_setup():
        import jax, jax.numpy as jnp
        import numpy as np
        DIM = 128

        def _reference_tuple_inner(x, W_r, W_k, W_v, mu_r, mu_k):
            B, T, C = x.shape
            x_prev = jnp.concatenate([jnp.zeros((B, 1, C), x.dtype), x[:, :-1, :]], axis=1)
            xr = mu_r * x + (1.0 - mu_r) * x_prev
            xk = mu_k * x + (1.0 - mu_k) * x_prev
            r = jax.nn.sigmoid(jnp.einsum('btc,dc->btd', xr, W_r))
            k = jnp.einsum('btc,dc->btd', xk, W_k)
            k_act = jnp.square(jax.nn.relu(k))
            out = r * jnp.einsum('btc,dc->btd', k_act, W_v)
            new_state = x[:, -1, :]
            return (out, new_state)
        key = jax.random.key(seed)
        ks = jax.random.split(key, 6)
        B, T, C = (8, 256, DIM)
        x = jax.random.normal(ks[0], (B, T, C), dtype=jnp.float32)
        s = 1.0 / np.sqrt(C)
        W_r = jax.random.uniform(ks[1], (C, C), jnp.float32, -s, s)
        W_k = jax.random.uniform(ks[2], (C, C), jnp.float32, -s, s)
        W_v = jax.random.uniform(ks[3], (C, C), jnp.float32, -s, s)
        mu_r = jax.random.uniform(ks[4], (C,), jnp.float32)
        mu_k = jax.random.uniform(ks[5], (C,), jnp.float32)
        return {'x': x, 'W_r': W_r, 'W_k': W_k, 'W_v': W_v, 'mu_r': mu_r, 'mu_k': mu_k}
    _L0_ffn_in = _L0_ffn_setup()

    def _L1_attn_setup():
        import jax, jax.numpy as jnp
        import numpy as np
        D_MODEL = 128
        N_HEADS = 16
        D_HEAD = D_MODEL // N_HEADS
        key = jax.random.key(seed)
        ks = jax.random.split(key, 5)
        B, S = (1, 256)
        x = jax.random.normal(ks[0], (B, S, D_MODEL), dtype=jnp.float32)
        lim = float(np.sqrt(6.0 / (2 * D_MODEL)))

        def w(k):
            return jax.random.uniform(k, (D_MODEL, D_MODEL), jnp.float32, -lim, lim)
        return {'x': x, 'Wq': w(ks[1]), 'bq': jnp.zeros((D_MODEL,), jnp.float32), 'Wk': w(ks[2]), 'bk': jnp.zeros((D_MODEL,), jnp.float32), 'Wv': w(ks[3]), 'bv': jnp.zeros((D_MODEL,), jnp.float32), 'Wo': w(ks[4]), 'bo': jnp.zeros((D_MODEL,), jnp.float32)}
    _L1_attn_in = _L1_attn_setup()

    def _L1_ffn_setup():
        import jax, jax.numpy as jnp
        import numpy as np
        DIM = 128
        HIDDEN = 256
        N_EXPERTS = 8
        TOP_K = 2
        EPS = 1e-06

        def rms_norm(x, scale, eps=EPS):
            ms = jnp.mean(jnp.square(x.astype(jnp.float32)), axis=-1, keepdims=True)
            s = scale.astype(jnp.float32) * jax.lax.rsqrt(ms + eps)
            return x * s.astype(x.dtype)

        def moe_linear(xf, ids, W):
            E = W.shape[0]
            out = jnp.zeros((xf.shape[0], W.shape[1]), dtype=xf.dtype)
            for e in range(E):
                out = out + jnp.where((ids == e)[:, None], xf @ W[e].T, 0.0)
            return out
        key = jax.random.key(seed)
        k1, k2, k3, k4 = jax.random.split(key, 4)
        x = jax.random.normal(k1, (4, 512, DIM), dtype=jnp.float32)
        norm_scale = jnp.ones((DIM,), dtype=jnp.float32)
        w_router = jax.random.normal(k2, (N_EXPERTS, DIM), dtype=jnp.float32) / np.sqrt(DIM)
        lim_up = np.sqrt(6.0 / (DIM + 2 * HIDDEN))
        w_up = jax.random.uniform(k3, (N_EXPERTS, 2 * HIDDEN, DIM), dtype=jnp.float32, minval=-lim_up, maxval=lim_up)
        lim_dn = np.sqrt(6.0 / (HIDDEN + DIM))
        w_down = jax.random.uniform(k4, (N_EXPERTS, DIM, HIDDEN), dtype=jnp.float32, minval=-lim_dn, maxval=lim_dn)
        return {'x': x, 'norm_scale': norm_scale, 'w_router': w_router, 'w_up': w_up, 'w_down': w_down}
    _L1_ffn_in = _L1_ffn_setup()
    _d = {'L0_attn_x': _L0_attn_in['x'], 'L0_attn_qkv_w': _L0_attn_in['qkv_w'], 'L0_attn_qkv_b': _L0_attn_in['qkv_b'], 'L0_attn_proj_w': _L0_attn_in['proj_w'], 'L0_attn_proj_b': _L0_attn_in['proj_b'], 'L0_ffn_W_r': _L0_ffn_in['W_r'], 'L0_ffn_W_k': _L0_ffn_in['W_k'], 'L0_ffn_W_v': _L0_ffn_in['W_v'], 'L0_ffn_mu_r': _L0_ffn_in['mu_r'], 'L0_ffn_mu_k': _L0_ffn_in['mu_k'], 'L1_attn_Wq': _L1_attn_in['Wq'], 'L1_attn_bq': _L1_attn_in['bq'], 'L1_attn_Wk': _L1_attn_in['Wk'], 'L1_attn_bk': _L1_attn_in['bk'], 'L1_attn_Wv': _L1_attn_in['Wv'], 'L1_attn_bv': _L1_attn_in['bv'], 'L1_attn_Wo': _L1_attn_in['Wo'], 'L1_attn_bo': _L1_attn_in['bo'], 'L1_ffn_norm_scale': _L1_ffn_in['norm_scale'], 'L1_ffn_w_router': _L1_ffn_in['w_router'], 'L1_ffn_w_up': _L1_ffn_in['w_up'], 'L1_ffn_w_down': _L1_ffn_in['w_down']}
    _x0 = _d['L0_attn_x']
    _d['L0_attn_x'] = jax.random.normal(jax.random.fold_in(jax.random.key(seed), 1), (4, 1024, 128), dtype=_x0.dtype)
    del _x0
    return _d

def reference(L0_attn_x, L0_attn_qkv_w, L0_attn_qkv_b, L0_attn_proj_w, L0_attn_proj_b, L0_ffn_W_r, L0_ffn_W_k, L0_ffn_W_v, L0_ffn_mu_r, L0_ffn_mu_k, L1_attn_Wq, L1_attn_bq, L1_attn_Wk, L1_attn_bk, L1_attn_Wv, L1_attn_bv, L1_attn_Wo, L1_attn_bo, L1_ffn_norm_scale, L1_ffn_w_router, L1_ffn_w_up, L1_ffn_w_down):

    def _L0_attn_ref(x, qkv_w, qkv_b, proj_w, proj_b):
        import jax, jax.numpy as jnp
        import numpy as np
        DIM = 128
        NUM_HEADS = 16
        HEAD_DIM = DIM // NUM_HEADS
        ROPE_BASE = 10000.0

        def rope_cos_sin(seq_len, dim):
            inv_freq = 1.0 / ROPE_BASE ** (jnp.arange(0, dim, 2, dtype=jnp.float32) / dim)
            t = jnp.arange(seq_len, dtype=jnp.float32)
            freqs = t[:, None] * inv_freq[None, :]
            emb = jnp.concatenate([freqs, freqs], axis=-1)
            return (jnp.cos(emb), jnp.sin(emb))

        def apply_rotary(x, cos, sin):
            x1 = x[..., ::2]
            x2 = x[..., 1::2]
            x_rot = jnp.stack((-x2, x1), axis=-1).reshape(x.shape)
            return x * cos + x_rot * sin
        B, L, C = x.shape
        H, D = (NUM_HEADS, HEAD_DIM)
        scale = D ** (-0.5)
        qkv = x @ qkv_w.T + qkv_b
        qkv = qkv.reshape(B, L, 3, H, D).transpose(2, 0, 3, 1, 4)
        q, k, v = (qkv[0], qkv[1], qkv[2])
        cos, sin = rope_cos_sin(L, D)
        q = apply_rotary(q, cos, sin)
        k = apply_rotary(k, cos, sin)
        attn = jnp.einsum('bhqd,bhkd->bhqk', q, k) * scale
        attn = jax.nn.softmax(attn, axis=-1)
        out = jnp.einsum('bhqk,bhkd->bhqd', attn, v)
        out = out.transpose(0, 2, 1, 3).reshape(B, L, C)
        return out @ proj_w.T + proj_b

    def _L0_ffn_ref(x, W_r, W_k, W_v, mu_r, mu_k):
        import jax, jax.numpy as jnp
        import numpy as np
        DIM = 128

        def _reference_tuple_inner(x, W_r, W_k, W_v, mu_r, mu_k):
            B, T, C = x.shape
            x_prev = jnp.concatenate([jnp.zeros((B, 1, C), x.dtype), x[:, :-1, :]], axis=1)
            xr = mu_r * x + (1.0 - mu_r) * x_prev
            xk = mu_k * x + (1.0 - mu_k) * x_prev
            r = jax.nn.sigmoid(jnp.einsum('btc,dc->btd', xr, W_r))
            k = jnp.einsum('btc,dc->btd', xk, W_k)
            k_act = jnp.square(jax.nn.relu(k))
            out = r * jnp.einsum('btc,dc->btd', k_act, W_v)
            new_state = x[:, -1, :]
            return (out, new_state)
        return _reference_tuple_inner(x, W_r, W_k, W_v, mu_r, mu_k)[0]

    def _L1_attn_ref(x, Wq, bq, Wk, bk, Wv, bv, Wo, bo):
        import jax, jax.numpy as jnp
        import numpy as np
        D_MODEL = 128
        N_HEADS = 16
        D_HEAD = D_MODEL // N_HEADS
        B, S, _ = x.shape
        H, d = (N_HEADS, D_HEAD)
        q = x @ Wq.T + bq
        k = x @ Wk.T + bk
        v = x @ Wv.T + bv

        def to_z(t):
            return t.reshape(B, S, H, d).transpose(0, 2, 1, 3).reshape(B * H, S, d)
        q = jax.nn.softplus(to_z(q))
        k = jax.nn.softplus(to_z(k))
        v = to_z(v)
        kv = jnp.cumsum(k[:, :, :, None] * v[:, :, None, :], axis=1)
        k1 = jnp.cumsum(k, axis=1)
        num = jnp.einsum('zsD,zsDe->zse', q, kv)
        den = jnp.sum(q * k1, axis=-1, keepdims=True)
        out = num / den
        out = out.reshape(B, H, S, d).transpose(0, 2, 1, 3).reshape(B, S, H * d)
        return out @ Wo.T + bo

    def _L1_ffn_ref(x, norm_scale, w_router, w_up, w_down):
        import jax, jax.numpy as jnp
        import numpy as np
        DIM = 128
        HIDDEN = 256
        N_EXPERTS = 8
        TOP_K = 2
        EPS = 1e-06

        def rms_norm(x, scale, eps=EPS):
            ms = jnp.mean(jnp.square(x.astype(jnp.float32)), axis=-1, keepdims=True)
            s = scale.astype(jnp.float32) * jax.lax.rsqrt(ms + eps)
            return x * s.astype(x.dtype)

        def moe_linear(xf, ids, W):
            E = W.shape[0]
            out = jnp.zeros((xf.shape[0], W.shape[1]), dtype=xf.dtype)
            for e in range(E):
                out = out + jnp.where((ids == e)[:, None], xf @ W[e].T, 0.0)
            return out
        B, S, D = x.shape
        skip = x
        xn = rms_norm(x, norm_scale)
        scores = (xn @ w_router.T).astype(jnp.float32)
        scores_topk, idx = jax.lax.top_k(scores, TOP_K)
        weights = jax.nn.softmax(scores_topk, axis=-1)
        xf = jnp.broadcast_to(xn[..., None, :], (B, S, TOP_K, D)).reshape(-1, D)
        ids = idx.reshape(-1)
        up = moe_linear(xf, ids, w_up)
        u, gate = jnp.split(up, 2, axis=-1)
        h = u * jax.nn.silu(gate)
        down = moe_linear(h, ids, w_down)
        down = down.reshape(B, S, TOP_K, D)
        out = jnp.sum(down * weights[..., None].astype(down.dtype), axis=-2)
        return out + skip
    x = L0_attn_x
    x = x + 0.5 * _L0_ffn_ref(_layernorm(x, axis=-1), L0_ffn_W_r, L0_ffn_W_k, L0_ffn_W_v, L0_ffn_mu_r, L0_ffn_mu_k)
    x = x + _L0_attn_ref(_layernorm(x, axis=-1), L0_attn_qkv_w, L0_attn_qkv_b, L0_attn_proj_w, L0_attn_proj_b)
    x = x + 0.5 * _L0_ffn_ref(_layernorm(x, axis=-1), L0_ffn_W_r, L0_ffn_W_k, L0_ffn_W_v, L0_ffn_mu_r, L0_ffn_mu_k)
    x = x + 0.5 * _L1_ffn_ref(_layernorm(x, axis=-1), L1_ffn_norm_scale, L1_ffn_w_router, L1_ffn_w_up, L1_ffn_w_down)
    x = x + _L1_attn_ref(_layernorm(x, axis=-1), L1_attn_Wq, L1_attn_bq, L1_attn_Wk, L1_attn_bk, L1_attn_Wv, L1_attn_bv, L1_attn_Wo, L1_attn_bo)
    x = x + 0.5 * _L1_ffn_ref(_layernorm(x, axis=-1), L1_ffn_norm_scale, L1_ffn_w_router, L1_ffn_w_up, L1_ffn_w_down)
    return x

_drawn_inputs = setup_inputs


def setup_inputs(seed=0):
    import zlib

    import numpy as np

    out = dict(_drawn_inputs(seed))
    spreads = {'L1_attn_bq': (0.0, 0.8),
     'L1_attn_bk': (0.0, 0.8),
     'L1_attn_bv': (0.0, 0.1),
     'L1_attn_bo': (0.0, 0.1),
     'L1_ffn_norm_scale': (1.0, 0.2)}
    factors = {'L0_ffn_W_r': 2.95, 'L0_ffn_mu_r': 5.337, 'L1_attn_Wq': 5.427, 'L1_attn_Wk': 2.7}
    for name, (base, spread) in spreads.items():
        noise = np.random.default_rng([zlib.crc32(name.encode()), seed]).standard_normal(out[name].shape)
        drawn = base * np.exp(spread * noise) if base else spread * noise
        out[name] = jnp.asarray(drawn.astype(out[name].dtype))
    for name, factor in factors.items():
        out[name] = (out[name] * factor).astype(out[name].dtype)
    return out
```

```python
from contextlib import ExitStack
from itertools import chain

import numpy as np

import concourse.bass as bass
from concourse import mybir

F32 = mybir.dt.float32
BF16 = mybir.dt.bfloat16
I32 = mybir.dt.int32
U32 = mybir.dt.uint32
ALU = mybir.AluOpType
ACT_FN = mybir.ActivationFunctionType
AX_X = mybir.AxisListType.X

P = 128
BATCH, SEQ, DIM = 4, 1024, 128
TOKENS = BATCH * SEQ
TILES = TOKENS // P
TPB = SEQ // P
BANK = 512
TPG = BANK // P
GROUPS = TILES // TPG
HEADS, HD = 16, 8
EXPERTS, TOPK, HIDDEN = 8, 2, 256
LN_EPS, RMS_EPS = 1e-5, 1e-6
SLOT_TILES = TOKENS * TOPK // P + EXPERTS - 1
SLOTS = SLOT_TILES * P
Q_PARTS = (0, 0, 1, 1, 0, 2)
K_PARTS = (0, 1, 0, 1, 2, 0)
QK_ROWS = len(Q_PARTS) * HD
MAX_ROWS = 2
STACK = 64
PAIRS = HEADS // 2
HEADS_PER_GROUP = 4


class Signal:

    def __init__(self, nc, ctx, name):
        self.sem, self.count, self.name = ctx.enter_context(nc.semaphore(name)), 0, name

    def after(self, instruction, by=1):
        instruction.then_inc(self.sem, by)
        self.count += by
        return (self, self.count)


def wait(engine, *marks):
    for mark in marks:
        if mark is not None:
            engine.wait_ge(mark[0].sem, mark[1])


class Ring:

    def __init__(self, banks):
        self.banks, self.free, self.n = list(banks), [None] * len(banks), -1

    def take(self):
        self.n = (self.n + 1) % len(self.banks)
        return self.n, self.banks[self.n], self.free[self.n]


class Stage:

    def __init__(self, core, name):
        self.core, self.nc, self.name, self.ctx = core, core.nc, name, ExitStack()
        ctx = core.ctx
        self.pe = Signal(self.nc, ctx, f"{name}_pe")
        self.dve = Signal(self.nc, ctx, f"{name}_dve")
        self.act = Signal(self.nc, ctx, f"{name}_act")
        self.pool = Signal(self.nc, ctx, f"{name}_pool")
        self.dmas = []

    def sbuf(self, name, shape, dtype=F32):
        return self.ctx.enter_context(self.nc.sbuf_tensor(f"{self.name}_{name}", shape, dtype))

    def dma_signal(self, name):
        s = Signal(self.nc, self.core.ctx, f"{self.name}_{name}")
        self.dmas.append(s)
        return s

    def close(self):
        for engine in self.core.engines:
            for s in (self.pe, self.dve, self.act, self.pool, *self.dmas):
                if s.count:
                    wait(engine, (s, s.count))
        self.ctx.close()


class Core:

    def __init__(self, nc, ctx):
        self.nc, self.ctx = nc, ctx
        self.engines = (nc.tensor, nc.vector, nc.scalar, nc.gpsimd, nc.sync)

    def sbuf(self, name, shape, dtype=F32):
        return self.ctx.enter_context(self.nc.sbuf_tensor(name, shape, dtype))


def normalise(core, st, batches, with_rms=False):
    nc, x = core.nc, core.x
    V = nc.vector
    n = batches * TPB
    stats = st.sbuf("ln_stats", [P, n, 6])
    moments = st.sbuf("ln_moments", [P, n, 2])
    var, std, rstd, fix = (st.sbuf(f"ln_{k}", [P, n]) for k in ("var", "std", "rstd", "fix"))
    for t in range(n):
        m = st.dve.after(V.bn_stats(out=stats[:, t, :], in_=x[:, t, :]))
    wait(V, m)
    for t in range(n):
        m = st.dve.after(V.bn_aggr(out=moments[:, t, :], in_=stats[:, t, :]))
    wait(V, m)

    def inverse_root(value, out):
        m = st.dve.after(V.tensor_copy(var[:, :], value)) if value is not None else st.dve_last
        wait(nc.scalar, m)
        m = st.act.after(nc.scalar.activation(std[:, :], var[:, :], ACT_FN.Sqrt))
        wait(V, m)
        m = st.dve.after(V.reciprocal(out, std[:, :]))
        wait(V, m)
        m = st.dve.after(V.tensor_tensor(fix[:, :], var[:, :], out, ALU.mult))
        wait(V, m)
        m = st.dve.after(V.tensor_tensor(fix[:, :], fix[:, :], out, ALU.mult))
        wait(V, m)
        m = st.dve.after(V.tensor_scalar(fix[:, :], fix[:, :], -0.5, 1.5, ALU.mult, ALU.add))
        wait(V, m)
        m = st.dve.after(V.tensor_tensor(out, out, fix[:, :], ALU.mult))
        wait(V, m)
        return m

    st.dve_last = st.dve.after(V.tensor_scalar(var[:, :], moments[:, :, 1], LN_EPS, None, ALU.add))
    m = inverse_root(None, rstd[:, :])
    if with_rms:
        st.scale_rms = st.sbuf("rms_scale", [P, n])
        ms = st.sbuf("rms_ms", [P, n])
        m = st.dve.after(V.tensor_tensor(ms[:, :], moments[:, :, 1], rstd[:, :], ALU.mult))
        wait(V, m)
        m = st.dve.after(V.tensor_tensor(ms[:, :], ms[:, :], rstd[:, :], ALU.mult))
        wait(V, m)
        m = st.dve.after(V.tensor_scalar(ms[:, :], ms[:, :], RMS_EPS, None, ALU.add))
        wait(V, m)
        m = inverse_root(ms[:, :], st.scale_rms[:, :])
    st.xn = st.sbuf("xn", [P, n, DIM])
    done = []
    for t in range(n):
        m = st.dve.after(V.tensor_scalar(st.xn[:, t, :], x[:, t, :], moments[:, t, 0:1], rstd[:, t:t + 1],
                                         ALU.subtract, ALU.mult))
        if t % TPB == TPB - 1:
            done.append(m)
    return done


def to_channels(core, st, ring, source, ready, group, out):
    nc = core.nc
    slot, bank, free = ring.take()
    wait(nc.tensor, free, ready)
    for i in range(TPG):
        m = nc.tensor.transpose(core.ps[:, bank, i * P:(i + 1) * P], source[:, group * TPG + i, :], core.ident[:, :])
    m = st.pe.after(m)
    if group % 2:
        wait(nc.scalar, m)
        ring.free[slot] = st.act.after(nc.scalar.activation(out, core.ps[:, bank, :], ACT_FN.Copy))
    else:
        wait(nc.vector, m)
        ring.free[slot] = st.dve.after(nc.vector.tensor_copy(out, core.ps[:, bank, :]))
    return ring.free[slot]


def channel_mix(core, name, w, mu_r, mu_k):
    nc = core.nc
    T, V, A, G = nc.tensor, nc.vector, nc.scalar, nc.gpsimd
    st = Stage(core, name)
    ring = Ring(range(8))
    ready = normalise(core, st, BATCH)
    xt = st.sbuf("xt", [P, BATCH, 1 + SEQ])
    m_zero = st.pool.after(G.memset(xt[:, :, 0:1], 0.0))
    rest = st.sbuf("rest", [P, 2])
    mixed = st.sbuf("mixed", [P, 4, DIM])
    for i, mu in enumerate((mu_r, mu_k)):
        m = st.dve.after(V.tensor_scalar(rest[:, i:i + 1], mu, -1.0, 1.0, ALU.mult, ALU.add))
    wait(V, m)
    for i, (wt, mu) in enumerate(((w[0], mu_r), (w[1], mu_k))):
        V.tensor_scalar(mixed[:, 2 * i, :], wt, mu, None, ALU.mult)
        m_mixed = st.dve.after(V.tensor_scalar(mixed[:, 2 * i + 1, :], wt, rest[:, i:i + 1], None, ALU.mult))
    wait(T, m_zero, m_mixed)
    NB = 2
    relu, act, gate, value = (st.sbuf(k, [P, NB, BANK]) for k in ("relu", "act", "gate", "value"))
    m_act, m_gate, m_value_free, m_v = {}, {}, {}, {}

    def value_and_add(g):
        slot, bank, free = ring.take()
        wait(T, free, m_act[g])
        for i in range(TPG):
            m = T.matmul(core.ps[:, bank, i * P:(i + 1) * P], act[:, g % NB, i * P:(i + 1) * P], w[2],
                         start=True, stop=True)
        m = m_v[g] = st.pe.after(m)
        wait(V, m, m_gate[g], m_value_free.get(g - NB))
        m = st.dve.after(V.scalar_tensor_tensor(value[:, g % NB, :], core.ps[:, bank, :], 0.5, gate[:, g % NB, :],
                                                ALU.mult, ALU.mult))
        ring.free[slot] = m
        wait(G, m)
        xg = core.x[:, g * TPG:(g + 1) * TPG, :].rearrange("p t c -> p (t c)")
        m_value_free[g] = st.pool.after(G.tensor_tensor(xg, xg, value[:, g % NB, :], ALU.add))

    for g in range(GROUPS):
        b, at = g // 2, (g % 2) * BANK
        m_xt = to_channels(core, st, ring, st.xn, ready[b], g, xt[:, b, 1 + at:1 + at + BANK])
        slot, bank, free = ring.take()
        wait(T, free, m_xt)
        T.matmul(core.ps[:, bank, :], mixed[:, 2, :], xt[:, b, 1 + at:1 + at + BANK], start=True, stop=False)
        m = st.pe.after(T.matmul(core.ps[:, bank, :], mixed[:, 3, :], xt[:, b, at:at + BANK], start=False, stop=True))
        wait(V, m, m_act.get(g - NB))
        m = ring.free[slot] = st.dve.after(V.tensor_scalar(relu[:, g % NB, :], core.ps[:, bank, :], 0.0, None, ALU.max))
        wait(A, m, m_v.get(g - NB))
        m_act[g] = st.act.after(A.activation(act[:, g % NB, :], relu[:, g % NB, :], ACT_FN.Square))
        slot, bank, free = ring.take()
        wait(T, free)
        for i in range(TPG):
            o = core.ps[:, bank, i * P:(i + 1) * P]
            T.matmul(o, xt[:, b, 1 + at + i * P:1 + at + (i + 1) * P], mixed[:, 0, :], start=True, stop=False)
            m = T.matmul(o, xt[:, b, at + i * P:at + (i + 1) * P], mixed[:, 1, :], start=False, stop=True)
        m = st.pe.after(m)
        wait(A, m, m_value_free.get(g - NB))
        m_gate[g] = ring.free[slot] = st.act.after(A.activation(gate[:, g % NB, :], core.ps[:, bank, :], ACT_FN.Sigmoid))
        if g:
            value_and_add(g - 1)
    value_and_add(GROUPS - 1)
    st.close()


def project_group(core, st, ring, heads_out, ready, group, weights, bias_rows, scratch, scratch_free):
    nc = core.nc
    T, V = nc.tensor, nc.vector
    slot, bank, free = ring.take()
    wait(T, free, ready)
    for i in range(TPG):
        m = T.transpose(core.ps[:, bank, i * P:(i + 1) * P], heads_out[:, i, :], core.ident[:, :])
    m_read = m = st.pe.after(m)
    wait(V, m, scratch_free)
    m = ring.free[slot] = st.dve.after(V.tensor_copy(scratch, core.ps[:, bank, :]))
    slot, bank, free = ring.take()
    wait(T, free, m)
    for i in range(TPG):
        m = T.matmul(core.ps[:, bank, i * P:(i + 1) * P], scratch[:, i * P:(i + 1) * P], weights, start=True, stop=True)
    m_scratch = m = st.pe.after(m)
    xg = core.x[:, group * TPG:(group + 1) * TPG, :]
    wait(V, m)
    m = ring.free[slot] = st.dve.after(V.tensor_tensor(
        xg, xg, core.ps[:, bank, :].rearrange("p (t c) -> p t c", t=TPG), ALU.add))
    wait(nc.gpsimd, m)
    st.pool.after(nc.gpsimd.tensor_tensor(xg, xg, bias_rows[:, None, :].broadcast_to([P, TPG, DIM]), ALU.add))
    return m_read, m_scratch


def softmax_attention(core, w, dram):
    nc = core.nc
    T, V, A, G, S = nc.tensor, nc.vector, nc.scalar, nc.gpsimd, nc.sync
    pre = Stage(core, "attn_ln")
    ring = Ring(range(8))
    ready = normalise(core, pre, BATCH)
    xt = core.xt_attn
    for g in range(GROUPS):
        to_channels(core, pre, ring, pre.xn, ready[g // 2], g, xt[:, g // 2, (g % 2) * BANK:(g % 2 + 1) * BANK])
    pre.close()

    st = Stage(core, "attn")
    E_BANKS, AUX_BANKS, PV_BANK = (0, 2), (4, 5, 6), 7
    ring = Ring(AUX_BANKS)
    HALVES = SEQ // BANK
    qs = st.sbuf("q_stack", [P, 2, PAIRS, SEQ], BF16)
    ks = st.sbuf("k_stack", [P, 2, PAIRS, SEQ], BF16)
    v = st.sbuf("v", [P, 2, TPB, HEADS, 32])
    probs = st.sbuf("probs", [P, 3, HEADS_PER_GROUP * BANK])
    t_cos, t_sin = (st.sbuf(k, [P, BANK]) for k in ("t_cos", "t_sin"))
    roped = st.sbuf("roped", [P, BANK])
    parts = st.sbuf("parts", [P, 2, 3, SEQ], BF16)
    half_max = st.sbuf("half_max", [P, HEADS, TPB, HALVES])
    neg_max = st.sbuf("neg_max", [P, HEADS * TPB])
    max_parts = st.sbuf("max_parts", [P, 2, P], BF16)
    sums = st.sbuf("sums", [P, 2, BANK])
    inv = st.sbuf("inv", [P, TPG, HEADS_PER_GROUP])
    heads_out = st.sbuf("heads_out", [P, HALVES, TPG, DIM])
    scratch = st.sbuf("proj_in", [P, BANK])
    parts_dma = [st.dma_signal(f"parts_store{i}") for i in range(2)]
    stack_dma = [st.dma_signal(f"stack_load{i}") for i in range(2)]
    max_store, max_load = st.dma_signal("max_store"), st.dma_signal("max_load")

    for s in range(2):
        m_ones = st.pool.after(G.memset(ks[s * STACK + 32:(s + 1) * STACK, :, :, :], 1.0))
        wait(G, m_ones)
    st.pool.after(G.memset(v[:, :, :, :, 8:32], 0.0))
    wait(G, (st.pool, st.pool.count))
    m_vconst = st.pool.after(G.memset(v[:, :, :, :, 8:9], 1.0))
    wait(V, m_vconst)

    m_stack_free = [None, None]
    m_v_free = [None, None]
    m_stack, m_v, m_max = {}, {}, {}
    last = {"cos": None, "parts": [None, None], "roped": None, "pe_roped": None}

    def project(b):
        for qk in range(2):
            for half in range(HALVES):
                cols = slice(half * BANK, (half + 1) * BANK)
                out = []
                for which in range(2):
                    slot, bank, free = ring.take()
                    wait(T, free)
                    m = st.pe.after(T.matmul(core.ps[:, bank, :], w["qk"][:, 2 * qk + which, :], xt[:, b, cols],
                                             start=True, stop=True))
                    wait(V, m, last["cos"])
                    table, dst = ((core.cos, t_cos), (core.sin, t_sin))[which]
                    m = st.dve.after(V.scalar_tensor_tensor(
                        dst[:, :], core.ps[:, bank, :], w["qk_bias"][:, 2 * qk + which:2 * qk + which + 1],
                        table[:, cols], ALU.add, ALU.mult))
                    ring.free[slot] = m
                wait(G, m)
                m = st.pool.after(G.tensor_tensor(roped[:, :], t_cos[:, :], t_sin[:, :], ALU.add))
                last["cos"] = m
                wait(G, m, last["parts"][qk])
                for part in range(3):
                    m = st.pool.after(G.tensor_copy(parts[:, qk, part, cols], roped[:, :]))
                    wait(G, m)
                    if part < 2:
                        m = st.pool.after(G.tensor_tensor(roped[:, :], roped[:, :], parts[:, qk, part, cols],
                                                          ALU.subtract))
                        wait(G, m)
                yield
            wait(S, m)
            for part in range(3):
                last["parts"][qk] = parts_dma[b % 2].after(
                    S.dma_start(dram["parts"][b % 2, qk, part], parts[:, qk, part, :]), 16)

    def values(b):
        for half in range(HALVES):
            slot, bank, free = ring.take()
            wait(T, free)
            for i in range(TPG):
                at = half * BANK + i * P
                m = T.matmul(core.ps[:, bank, i * P:(i + 1) * P], xt[:, b, at:at + P], w["v"], start=True, stop=True)
            m = st.pe.after(m)
            wait(V, m, m_v_free[b % 2])
            for i in range(TPG):
                m = st.dve.after(V.tensor_tensor(
                    v[:, b % 2, half * TPG + i, :, 0:8],
                    core.ps[:, bank, i * P:(i + 1) * P].rearrange("p (h d) -> p h d", h=HEADS),
                    w["v_bias"].rearrange("p (h d) -> p h d", h=HEADS), ALU.add))
            m_v[b] = ring.free[slot] = m
            yield

    def load_stacks(b):
        wait(S, (parts_dma[b % 2], parts_dma[b % 2].count), m_stack_free[b % 2], m_ones)
        for s in range(2):
            for row, (qp, kp) in enumerate(zip(Q_PARTS, K_PARTS)):
                for qk, dst, part in ((0, qs, qp), (1, ks, kp)):
                    src = dram["parts"][b % 2, qk, part].rearrange("(r s d) t -> s d r t", s=2, d=HD)[s]
                    first = s * STACK + row * HD
                    m = stack_dma[b % 2].after(S.dma_start(dst[first:first + HD, b % 2, :, :], src), 16)
        m_stack[b] = m

    m_half = {"last": None, "neg": None}

    def maxima(b):
        wait(T, m_stack[b])
        for pair in range(PAIRS):
            for qt in range(TPB):
                for s in range(2):
                    h = 2 * pair + s
                    for half in range(HALVES):
                        slot, bank, free = ring.take()
                        wait(T, free)
                        m = st.pe.after(T.matmul(
                            core.ps[:, bank, :], qs[s * STACK:s * STACK + QK_ROWS, b % 2, pair, qt * P:(qt + 1) * P],
                            ks[s * STACK:s * STACK + QK_ROWS, b % 2, pair, half * BANK:(half + 1) * BANK],
                            start=True, stop=True))
                        wait(V, m)
                        ring.free[slot] = st.dve.after(V.tensor_reduce(
                            half_max[:, h, qt, half:half + 1], core.ps[:, bank, :], AX_X, ALU.max))
                    yield
        wait(V, ring.free[slot])
        m = st.dve.after(V.tensor_reduce(neg_max[:, :], half_max[:, :, :, :].rearrange("p h q k -> p (h q) k"),
                                         AX_X, ALU.max, negate=True))
        slot, bank, free = ring.take()
        wait(T, free, m)
        m = st.pe.after(T.transpose(core.ps[:, bank, 0:P], neg_max[:, :], core.ident[:, :]))
        wait(V, m, (max_store, max_store.count) if max_store.count else None)
        m = st.dve.after(V.tensor_copy(max_parts[:, 0, :], core.ps[:, bank, 0:P]))
        wait(V, m)
        m = ring.free[slot] = st.dve.after(V.tensor_tensor(max_parts[:, 1, :], core.ps[:, bank, 0:P],
                                                           max_parts[:, 0, :], ALU.subtract))
        wait(S, m)
        m = max_store.after(S.dma_start(dram["maxima"][b].rearrange("k r q -> r k q"), max_parts[:, :, :]), 16)
        wait(S, m)
        for s in range(2):
            first = s * STACK + QK_ROWS
            src = dram["maxima"][b].rearrange("k (r s j) q -> s k r (j q)", s=2, j=TPB)[s]
            m_max[b] = max_load.after(S.dma_start(qs[first:first + MAX_ROWS, b % 2, :, :], src), 16)

    e_free = [None, None]
    m_exp, m_pv = {}, {}
    pv_free, m_sums_free = [None], [None, None]
    m_heads_free, m_scratch = [None, None], [None]
    step_no = [0]

    def scores_and_exp(b, group, half, kt):
        n = step_no[0]
        if kt == 0 and group == 0 and half == 0:
            wait(T, m_max[b])
        marks = []
        for e in range(2):
            pair = 2 * group + e
            wait(T, e_free[e])
            for s in range(2):
                rows = slice(s * STACK, s * STACK + QK_ROWS + MAX_ROWS)
                m = T.matmul(core.ps[:, E_BANKS[e] + s, :], ks[rows, b % 2, pair, kt * P:(kt + 1) * P],
                             qs[rows, b % 2, pair, half * BANK:(half + 1) * BANK], start=True, stop=True)
            m = st.pe.after(m)
            wait(A, m, m_pv.get(n - 3) if e == 0 else None)
            e_free[e] = st.act.after(A.activation(
                probs[:, n % 3, 2 * e * BANK:2 * (e + 1) * BANK],
                core.ps[:, E_BANKS[e]:E_BANKS[e] + 2, :].rearrange("p a n -> p (a n)"), ACT_FN.Exp, scale=HD ** -0.5))
        m_exp[n] = e_free[1]
        m_stack_free[b % 2] = m
        step_no[0] += 1
        return n

    def weighted_sums(n, b, group, half, kt):
        wait(T, m_exp[n], m_v[b] if kt == 0 else None, pv_free[0] if kt == 0 else None)
        for j in range(HEADS_PER_GROUP):
            m = T.matmul(core.ps[32 * j:32 * (j + 1), PV_BANK, :], v[:, b % 2, kt, HEADS_PER_GROUP * group + j, :],
                         probs[:, n % 3, j * BANK:(j + 1) * BANK], start=kt == 0, stop=kt == TPB - 1)
        m_pv[n] = m_v_free[b % 2] = m = st.pe.after(m)
        if kt < TPB - 1:
            return
        k = (2 * group + half) % 2
        wait(V, m, m_sums_free[k])
        m = pv_free[0] = st.dve.after(V.tensor_copy(sums[:, k, :], core.ps[:, PV_BANK, :]))
        pending.append((m, k, b, group, half))

    def divide():
        m, k, b, group, half = pending.pop(0)
        slot, bank, free = ring.take()
        wait(T, m, free)
        for i in range(TPG):
            m = T.transpose(core.ps[:, bank, i * P:(i + 1) * P], sums[:, k, i * P:(i + 1) * P], core.ident[:, :])
        m = m_sums_free[k] = st.pe.after(m)
        got = core.ps[:, bank, :].rearrange("p (t j c) -> p t j c", t=TPG, j=HEADS_PER_GROUP)
        wait(V, m)
        m = st.dve.after(V.reciprocal(inv[:, :, :], got[:, :, :, 8]))
        wait(V, m, m_heads_free[half] if group == 0 else None)
        out = heads_out[:, half, :, group * 32:(group + 1) * 32].rearrange("p t (j d) -> p t j d", d=HD)
        m = ring.free[slot] = st.dve.after(V.tensor_tensor(
            out, got[:, :, :, 0:8], inv[:, :, :, None].broadcast_to([P, TPG, HEADS_PER_GROUP, HD]), ALU.mult))
        if group == HEADS // HEADS_PER_GROUP - 1:
            m_heads_free[half], m_scratch[0] = project_group(
                core, st, ring, heads_out[:, half, :, :], m, 2 * b + half, w["proj"], w["proj_bias"],
                scratch[:, :], m_scratch[0])

    pending = []
    for b in range(min(2, BATCH)):
        for _ in project(b):
            pass
        load_stacks(b)
        if b == 0:
            for units in (values(0), maxima(0)):
                for _ in units:
                    pass
    for b in range(BATCH):
        steps = [(group, half, kt) for group in range(HEADS // HEADS_PER_GROUP) for half in range(HALVES)
                 for kt in range(TPB)]
        max_units = maxima(b + 1) if b + 1 < BATCH else iter(())
        proj_units = chain(values(b + 1) if b + 1 < BATCH else (), project(b + 2) if b + 2 < BATCH else ())
        MAX_FROM, MAX_TO = 5, 60
        done = 0
        previous = None
        for i, (group, half, kt) in enumerate(steps):
            n = scores_and_exp(b, group, half, kt)
            if i >= MAX_FROM:
                target = min(1.0, (i + 1 - MAX_FROM) / (MAX_TO - MAX_FROM)) * (HEADS * TPB + 1)
                while done < target:
                    next(max_units, None)
                    done += 1
            if i % 8 == 6:
                next(proj_units, None)
            if previous is not None:
                weighted_sums(*previous)
            if pending and kt == 2:
                divide()
            previous = (n, b, group, half, kt)
        weighted_sums(*previous)
        for units in (max_units, proj_units):
            for _ in units:
                pass
        while pending:
            divide()
        if b + 2 < BATCH:
            load_stacks(b + 2)
    st.close()


def experts(core, name, w, dram):
    nc = core.nc
    T, V, A, G, S = nc.tensor, nc.vector, nc.scalar, nc.gpsimd, nc.sync
    st = Stage(core, name)
    ring = Ring(range(8))
    ready = normalise(core, st, BATCH, with_rms=True)
    xr = st.sbuf("xr", [P, TILES, DIM])
    token_dma = st.dma_signal("token_store")
    rows = dram["tokens"].rearrange("(t p) c -> p t c", p=P)
    m_xr = []
    for b in range(BATCH):
        wait(G, ready[b])
        for t in range(b * TPB, (b + 1) * TPB):
            m = st.pool.after(G.tensor_scalar(xr[:, t, :], st.xn[:, t, :], st.scale_rms[:, t:t + 1], None, ALU.mult))
        m_xr.append(m)
        wait(S, m)
        m_tokens = token_dma.after(S.dma_start(rows[:, b * TPB:(b + 1) * TPB, :], xr[:, b * TPB:(b + 1) * TPB, :]), 16)

    SCORE = ring.banks[7]
    ring = Ring(range(7))
    xrt = st.sbuf("xrt", [P, 2, BANK])
    m_score = {}
    for g in range(GROUPS):
        wait(V, m_score.get(g - 2))
        wait(A, m_score.get(g - 2))
        m = to_channels(core, st, ring, xr, m_xr[g // 2], g, xrt[:, g % 2, :])
        wait(T, m)
        for i in range(TPG):
            at = (g * TPG + i) * EXPERTS
            m = T.matmul(core.ps[:, SCORE, at:at + EXPERTS], xrt[:, g % 2, i * P:(i + 1) * P], w["router"],
                         start=True, stop=True)
        m_score[g] = m = st.pe.after(m)

    N8 = [P, TILES, EXPERTS]

    def wide(k, dtype=F32):
        return st.sbuf(k, N8, dtype)

    def bc(narrow):
        return narrow[:, :, None].broadcast_to(N8)

    def v_(instruction):
        m = st.dve.after(instruction)
        wait(V, m)
        return m

    score, key, scored2 = wide("score"), wide("key"), wide("scored2")
    hot = [wide("hot1"), wide("hot2")]
    top = st.sbuf("top", [P, 2, TILES])
    pick = st.sbuf("pick", [P, TILES])
    wait(V, m)
    v_(V.tensor_copy(score[:, :, :].rearrange("p t e -> p (t e)"), core.ps[:, SCORE, 0:TILES * EXPERTS]))
    rev = core.rev_expert[:, None, :].broadcast_to(N8)
    for c, src in enumerate((score, scored2)):
        v_(V.tensor_reduce(top[:, c, :], src[:, :, :], AX_X, ALU.max))
        v_(V.tensor_tensor(key[:, :, :], src[:, :, :], bc(top[:, c, :]), ALU.is_equal))
        v_(V.tensor_tensor(key[:, :, :], key[:, :, :], rev, ALU.mult))
        v_(V.tensor_reduce(pick[:, :], key[:, :, :], AX_X, ALU.max))
        v_(V.tensor_tensor(hot[c][:, :, :], rev, bc(pick[:, :]), ALU.is_equal))
        if c == 0:
            v_(V.scalar_tensor_tensor(scored2[:, :, :], hot[0][:, :, :], -3.0e38, score[:, :, :], ALU.mult, ALU.add))
    weight = st.sbuf("weight", [P, 2, TILES])
    gap = st.sbuf("gap", [P, TILES])
    m = v_(V.tensor_tensor(gap[:, :], top[:, 1, :], top[:, 0, :], ALU.subtract))
    wait(A, m)
    m_gap = st.act.after(A.activation(gap[:, :], gap[:, :], ACT_FN.Exp))

    both = wide("both", BF16)
    m = v_(V.tensor_tensor(both[:, :, :], hot[0][:, :, :], hot[1][:, :, :], ALU.add))
    flat = both[:, :, :].rearrange("p t e -> p (t e)")
    slot_a, bank_a, free_a = ring.take()
    slot_b, bank_b, free_b = ring.take()
    wait(T, m, free_a, free_b)
    T.matmul(core.ps[:, bank_a, 0:TILES * EXPERTS], core.before[:, :], flat, start=True, stop=True)
    m = st.pe.after(T.matmul(core.ps[:, bank_b, 0:TILES * EXPERTS], core.ones_bf[:, :], flat, start=True, stop=True))
    E8 = [P, EXPERTS, TILES]
    total, running, base = (st.sbuf(k, E8) for k in ("total", "running", "base"))
    per_e = {k: st.sbuf(k, [P, EXPERTS]) for k in ("count", "tiles", "first")}
    count_i = st.sbuf("count_i", [P, EXPERTS], I32)
    ends = st.sbuf("ends", [P, EXPERTS])
    zero = core.zeros
    wait(V, m)
    v_(V.tensor_copy(total[:, :, :], core.ps[:, bank_b, 0:TILES * EXPERTS].rearrange("p (t e) -> p e t", e=EXPERTS)))
    v_(V.tensor_tensor_scan(running[:, :, :].rearrange("p e t -> p (e t)"), total[:, :, :].rearrange("p e t -> p (e t)"),
                            zero[:, 0:TILES * EXPERTS], 0.0, ALU.add, ALU.add))
    v_(V.tensor_tensor(base[:, :, :], running[:, :, :], total[:, :, :], ALU.subtract))
    v_(V.tensor_tensor(per_e["count"][:, :], running[:, :, TILES - 1], base[:, :, 0], ALU.subtract))
    v_(V.tensor_scalar(per_e["count"][:, :], per_e["count"][:, :], float(P - 1), None, ALU.add))
    v_(V.tensor_copy(count_i[:, :], per_e["count"][:, :]))
    v_(V.tensor_scalar(count_i[:, :], count_i[:, :], 7, None, ALU.arith_shift_right))
    v_(V.tensor_copy(per_e["tiles"][:, :], count_i[:, :]))
    v_(V.tensor_tensor_scan(ends[:, :], per_e["tiles"][:, :], zero[:, 0:EXPERTS], 0.0, ALU.add, ALU.add))
    v_(V.tensor_tensor(per_e["first"][:, :], ends[:, :], per_e["tiles"][:, :], ALU.subtract))
    v_(V.tensor_scalar(per_e["first"][:, :], per_e["first"][:, :], float(P), None, ALU.mult))
    v_(V.tensor_tensor(per_e["first"][:, :], per_e["first"][:, :], base[:, :, 0], ALU.subtract))
    v_(V.tensor_tensor(base[:, :, :], base[:, :, :], per_e["first"][:, :, None].broadcast_to(E8), ALU.add))
    place = wide("place")
    v_(V.tensor_tensor(place[:, :, :], core.ps[:, bank_a, 0:TILES * EXPERTS].rearrange("p (t e) -> p t e", e=EXPERTS),
                       base[:, :, :].rearrange("p e t -> p t e"), ALU.add))

    T8 = [P, SLOT_TILES, EXPERTS]
    ended = st.sbuf("ended", T8)
    expert_of = st.sbuf("expert_of", [P, SLOT_TILES])
    offsets = st.sbuf("offsets", [P, 2, SLOT_TILES], I32)
    v_(V.tensor_tensor(ended[:, :, :], core.slot_tile[:, :, None].broadcast_to(T8),
                       ends[:, None, :].broadcast_to(T8), ALU.is_ge))
    v_(V.tensor_reduce(expert_of[:, :], ended[:, :, :], AX_X, ALU.add))
    v_(V.tensor_scalar(expert_of[:, :], expert_of[:, :], float(EXPERTS - 1), None, ALU.min))
    for i, stride in enumerate((2 * HIDDEN, DIM)):
        m_offsets = v_(V.tensor_scalar(offsets[:, i, :], expert_of[:, :], float(stride), None, ALU.mult))

    slot_f = st.sbuf("slot_f", [P, 2, TILES])
    slot_i, slot_t = (st.sbuf(k, [P, 2, TILES], I32) for k in ("slot_i", "slot_t"))
    row_f, tile_f = (st.sbuf(k, [P, 2, TILES]) for k in ("row_f", "tile_f"))
    for c in range(TOPK):
        v_(V.tensor_tensor(key[:, :, :], place[:, :, :], hot[c][:, :, :], ALU.mult))
        m = v_(V.tensor_reduce(slot_f[:, c, :], key[:, :, :], AX_X, ALU.add))
    v_(V.tensor_copy(slot_i[:, :, :], slot_f[:, :, :]))
    v_(V.tensor_scalar(slot_t[:, :, :], slot_i[:, :, :], 7, None, ALU.arith_shift_right))
    v_(V.tensor_copy(tile_f[:, :, :], slot_t[:, :, :]))
    v_(V.tensor_scalar(slot_i[:, :, :], slot_i[:, :, :], P - 1, None, ALU.bitwise_and))
    v_(V.tensor_copy(row_f[:, :, :], slot_i[:, :, :]))

    PART = 2 * SLOT_TILES
    row_hot = st.sbuf("row_hot", [P, 4, P], BF16)
    tile_hot = st.sbuf("tile_hot", [P, 4, PART], BF16)
    slot_l, bank_l, free_l = ring.take()
    m_l = {}
    n = 0
    for t in range(TILES):
        for c in range(TOPK):
            wait(V, m_l.get(n - 4))
            V.tensor_scalar(row_hot[:, n % 4, :], core.iota_p[:, :], row_f[:, c, t:t + 1], None, ALU.is_equal)
            V.tensor_scalar(tile_hot[:, n % 4, 0:SLOT_TILES], core.slot_tile[:, :], tile_f[:, c, t:t + 1],
                            core.lane1[:, 0:1], ALU.is_equal, ALU.mult)
            m = st.dve.after(V.tensor_scalar(tile_hot[:, n % 4, SLOT_TILES:PART], core.slot_tile[:, :],
                                             tile_f[:, c, t:t + 1], float(2 * t + c), ALU.is_equal, ALU.mult))
            wait(T, m, free_l if n == 0 else None)
            m_l[n] = st.pe.after(T.matmul(core.ps[:, bank_l, 0:PART], row_hot[:, n % 4, :], tile_hot[:, n % 4, :],
                                          start=n == 0, stop=n == TILES * TOPK - 1))
            n += 1
    listed = st.sbuf("listed", [P, 2, SLOT_TILES])
    empty = st.sbuf("empty", [P, SLOT_TILES])
    src_f, dst_f = (st.sbuf(k, [P, SLOT_TILES]) for k in ("src_f", "dst_f"))
    src_i, dst_i = (st.sbuf(k, [P, SLOT_TILES], U32) for k in ("src_i", "dst_i"))
    wait(V, m_l[n - 1])
    v_(V.tensor_copy(listed[:, :, :].rearrange("p a t -> p (a t)"), core.ps[:, bank_l, 0:PART]))
    half_i = st.sbuf("half_i", [P, SLOT_TILES], I32)
    v_(V.tensor_scalar(empty[:, :], listed[:, 0, :], 0.0, None, ALU.is_equal))
    v_(V.tensor_scalar(listed[:, 0, :], listed[:, 0, :], -1.0, 0.0, ALU.add, ALU.max))
    v_(V.tensor_copy(half_i[:, :], listed[:, 1, :]))
    v_(V.tensor_scalar(half_i[:, :], half_i[:, :], 1, None, ALU.arith_shift_right))
    v_(V.tensor_copy(src_f[:, :], half_i[:, :]))
    v_(V.scalar_tensor_tensor(src_f[:, :], src_f[:, :], float(P), listed[:, 0, :], ALU.mult, ALU.add))
    v_(V.tensor_copy(src_i[:, :], src_f[:, :]))
    v_(V.scalar_tensor_tensor(dst_f[:, :], listed[:, 1, :], float(P), listed[:, 0, :], ALU.mult, ALU.add))
    v_(V.tensor_tensor(empty[:, :], empty[:, :], core.spare_row[:, :], ALU.mult))
    v_(V.tensor_tensor(dst_f[:, :], dst_f[:, :], empty[:, :], ALU.add))
    m_lists = v_(V.tensor_copy(dst_i[:, :], dst_f[:, :]))
    wait(V, m_gap)
    v_(V.tensor_scalar(weight[:, 0, :], gap[:, :], 1.0, None, ALU.add))
    v_(V.reciprocal(weight[:, 0, :], weight[:, 0, :]))
    v_(V.tensor_scalar(weight[:, 0, :], weight[:, 0, :], 0.5, None, ALU.mult))
    v_(V.tensor_tensor(weight[:, 1, :], weight[:, 0, :], gap[:, :], ALU.mult))

    ring = Ring(())
    NG, NB = 6, 3
    gathered = st.sbuf("gathered", [P, NG, DIM])
    gt = st.sbuf("gt", [P, NB, DIM])
    silu, h = (st.sbuf(k, [P, NB, HIDDEN]) for k in ("silu", "h"))
    ht = st.sbuf("ht", [P, NB, HIDDEN])
    y = st.sbuf("y", [P, NG, DIM])
    gather_dma = [st.dma_signal(f"gather{i}") for i in range(NG)]
    scatter_dma = [st.dma_signal(f"scatter{i}") for i in range(NG)]
    XT, UP, HT, DOWN = (0, 1), (2, 3), (4, 5), (6, 7)
    m_g, m_xt, m_gt, m_up, m_silu, m_h, m_htp, m_ht, m_down, m_y = ({} for _ in range(10))
    wait(G, m_lists, m_tokens, (token_dma, token_dma.count))
    wait(T, m_offsets, m_lists, m_gap)
    wait(A, m_lists)

    def gather(j):
        wait(G, m_xt.get(j - NG))
        m_g[j] = gather_dma[j % NG].after(G.indirect_dma_start(
            out=gathered[:, j % NG, :], out_offset=None, in_=dram["tokens"],
            in_offset=bass.IndirectOffsetOnAxis(ap=src_i[:, j:j + 1], axis=0)), 16)

    def turn(j):
        wait(T, m_g[j], m_gt.get(j - 2))
        m_xt[j] = st.pe.after(T.transpose(core.ps[:, XT[j % 2], 0:P], gathered[:, j % NG, :], core.ident[:, :]))
        wait(V, m_xt[j], m_up.get(j - NB))
        m_gt[j] = st.dve.after(V.tensor_copy(gt[:, j % NB, :], core.ps[:, XT[j % 2], 0:P]))

    def up(j):
        wait(T, m_gt[j], m_h.get(j - 2), m_silu.get(j - 2))
        at = T.value_load(offsets[0:1, 0, j:j + 1], min_val=0, max_val=(EXPERTS - 1) * 2 * HIDDEN)
        bank = UP[j % 2]
        m_up[j] = st.pe.after(T.matmul(core.ps[:, bank, :], gt[:, j % NB, :], w["up"][:, bass.ds(at, 2 * HIDDEN)],
                                       start=True, stop=True))
        wait(A, m_up[j], m_h.get(j - NB))
        m_silu[j] = st.act.after(A.activation(silu[:, j % NB, :], core.ps[:, bank, HIDDEN:2 * HIDDEN], ACT_FN.Silu))
        wait(V, m_silu[j], m_htp.get(j - NB))
        m_h[j] = st.dve.after(V.tensor_tensor(h[:, j % NB, :], core.ps[:, bank, 0:HIDDEN], silu[:, j % NB, :], ALU.mult))

    def turn_hidden(j):
        wait(T, m_h[j], m_ht.get(j - 2))
        bank = HT[j % 2]
        for k in range(2):
            m = T.transpose(core.ps[:, bank, k * P:(k + 1) * P], h[:, j % NB, k * P:(k + 1) * P], core.ident[:, :])
        m_htp[j] = st.pe.after(m)
        wait(A, m_htp[j], m_down.get(j - NB))
        m_ht[j] = st.act.after(A.activation(ht[:, j % NB, :], core.ps[:, bank, 0:HIDDEN], ACT_FN.Copy))

    def down(j):
        wait(T, m_ht[j], m_y.get(j - 2))
        at = T.value_load(offsets[0:1, 1, j:j + 1], min_val=0, max_val=(EXPERTS - 1) * DIM)
        bank = DOWN[j % 2]
        for k in range(2):
            m = T.matmul(core.ps[:, bank, 0:DIM], ht[:, j % NB, k * P:(k + 1) * P],
                         w["down"][:, k * EXPERTS * DIM:(k + 1) * EXPERTS * DIM][:, bass.ds(at, DIM)],
                         start=k == 0, stop=k == 1)
        m_down[j] = st.pe.after(m)
        free = (scatter_dma[j % NG], scatter_dma[j % NG].count) if j >= NG else None
        wait(V, m_down[j], free)
        m_y[j] = st.dve.after(V.tensor_copy(y[:, j % NG, :], core.ps[:, bank, 0:DIM]))

    def scatter(j):
        wait(G, m_y[j])
        scatter_dma[j % NG].after(G.indirect_dma_start(
            out=dram["routed"], out_offset=bass.IndirectOffsetOnAxis(ap=dst_i[:, j:j + 1], axis=0),
            in_=y[:, j % NG, :], in_offset=None), 16)

    AHEAD = 4
    for j in range(min(AHEAD, SLOT_TILES)):
        gather(j)
    for j in range(SLOT_TILES + 4):
        if j < SLOT_TILES:
            turn(j)
        if 0 <= j - 1 < SLOT_TILES:
            up(j - 1)
        if 0 <= j - 2 < SLOT_TILES:
            turn_hidden(j - 2)
        if 0 <= j - 3 < SLOT_TILES:
            down(j - 3)
        if j + AHEAD < SLOT_TILES:
            gather(j + AHEAD)
        if 0 <= j - 3 < SLOT_TILES:
            scatter(j - 3)

    for s in scatter_dma:
        wait(S, (s, s.count))
    back = st.sbuf("back", [P, 2, TPG * TOPK, DIM])
    back_dma = [st.dma_signal(f"back{i}") for i in range(2)]
    routed = dram["routed"][0:TOKENS * TOPK, :].rearrange("(n p) c -> p n c", p=P)
    m_read = {}
    for g in range(GROUPS):
        wait(S, m_read.get(g - 2))
        m = back_dma[g % 2].after(S.dma_start(back[:, g % 2, :, :],
                                              routed[:, g * TPG * TOPK:(g + 1) * TPG * TOPK, :]), 16)
        wait(V, m)
        tiles = slice(g * TPG, (g + 1) * TPG)
        v_(V.scalar_tensor_tensor(core.x[:, tiles, :], st.xn[:, tiles, :], 0.5, core.x[:, tiles, :], ALU.mult, ALU.add))
        for c in range(TOPK):
            wc = weight[:, c, g * TPG:(g + 1) * TPG][:, :, None].broadcast_to([P, TPG, DIM])
            bk = back[:, g % 2, :, :].rearrange("p (t c) d -> p t c d", c=TOPK)[:, :, c, :]
            v_(V.tensor_tensor(bk, bk, wc, ALU.mult))
            m = v_(V.tensor_tensor(core.x[:, tiles, :], core.x[:, tiles, :], bk, ALU.add))
        m_read[g] = m
    st.close()


def linear_attention(core, w):
    nc = core.nc
    T, V, A, G = nc.tensor, nc.vector, nc.scalar, nc.gpsimd
    st = Stage(core, "lin")
    ring = Ring(range(8))
    ready = normalise(core, st, BATCH)
    VW = HD + 1
    xt = st.sbuf("xt", [P, 2, BANK])
    q, k = (st.sbuf(n, [P, SEQ]) for n in ("q", "k"))
    q_of = st.sbuf("q_of", [P, TPB, HEADS_PER_GROUP, P])
    k_tok = st.sbuf("k_tok", [P, TPB, DIM])
    v = st.sbuf("v", [P, TPB, HEADS, VW])
    neg_abs, e, ln, rest, pos = (st.sbuf(n, [P, BANK]) for n in ("abs", "e", "ln", "rest", "pos"))
    scores = st.sbuf("scores", [P, 4, BANK])
    state = st.sbuf("state", [P, HEADS * VW])
    update = st.sbuf("update", [P, HEADS * VW])
    inv = st.sbuf("inv", [P, HEADS])
    heads_out = st.sbuf("heads_out", [P, TPG, DIM])
    scratch = st.sbuf("proj_in", [P, BANK])
    m_heads_free = m_scratch = None
    wait(V, st.pool.after(G.memset(v[:, :, :, HD:VW], 1.0)))
    m_xt_free = {}
    m_end = None
    m_work = None
    n_scores, m_scores_free = 0, {}
    for b in range(BATCH):
        for half in range(2):
            g = 2 * b + half
            cols = slice(half * BANK, (half + 1) * BANK)
            wait(V, m_xt_free.get(g - 2))
            wait(A, m_xt_free.get(g - 2))
            m_xt = to_channels(core, st, ring, st.xn, ready[b], g, xt[:, g % 2, :])
            for i, dst in enumerate((q, k)):
                slot, bank, free = ring.take()
                wait(T, free, m_xt)
                m = st.pe.after(T.matmul(core.ps[:, bank, :], w["qkvo"][:, i, :], xt[:, g % 2, :], start=True, stop=True))
                bias = w["qk_bias"][:, i:i + 1]
                wait(V, m, m_work, m_end)
                m = st.dve.after(V.tensor_scalar(pos[:, :], core.ps[:, bank, :], bias, 0.0, ALU.add, ALU.max))
                wait(A, m)
                m = ring.free[slot] = st.act.after(A.activation(neg_abs[:, :], core.ps[:, bank, :], ACT_FN.Abs, bias=bias))
                wait(A, m)
                m = st.act.after(A.activation(e[:, :], neg_abs[:, :], ACT_FN.Exp, scale=-1.0))
                wait(A, m)
                m_ln = st.act.after(A.activation(ln[:, :], e[:, :], ACT_FN.Ln, bias=1.0))
                wait(V, m)
                m = st.dve.after(V.tensor_scalar(rest[:, :], e[:, :], 1.0, -1.0, ALU.add, ALU.add))
                wait(V, m)
                m = st.dve.after(V.tensor_tensor(rest[:, :], e[:, :], rest[:, :], ALU.subtract))
                wait(V, m, m_ln)
                m = st.dve.after(V.tensor_tensor(rest[:, :], ln[:, :], rest[:, :], ALU.add))
                wait(V, m)
                m_work = st.dve.after(V.tensor_tensor(dst[:, cols], pos[:, :], rest[:, :], ALU.add))
            slot, bank, free = ring.take()
            wait(T, free)
            for i in range(TPG):
                m = T.matmul(core.ps[:, bank, i * P:(i + 1) * P], xt[:, g % 2, i * P:(i + 1) * P], w["qkvo"][:, 2, :],
                             start=True, stop=True)
            m_xt_free[g] = m = st.pe.after(m)
            wait(V, m)
            for i in range(TPG):
                m = st.dve.after(V.tensor_tensor(
                    v[:, half * TPG + i, :, 0:HD], core.ps[:, bank, i * P:(i + 1) * P].rearrange("p (h d) -> p h d", h=HEADS),
                    w["v_bias"].rearrange("p (h d) -> p h d", h=HEADS), ALU.add))
            m_v = ring.free[slot] = m
            slot, bank, free = ring.take()
            wait(T, free, m_work)
            for i in range(TPG):
                at = half * BANK + i * P
                m = T.transpose(core.ps[:, bank, i * P:(i + 1) * P], k[:, at:at + P], core.ident[:, :])
            m = st.pe.after(m)
            wait(A, m, m_end)
            m_ktok = ring.free[slot] = st.act.after(A.activation(
                k_tok[:, half * TPG:(half + 1) * TPG, :].rearrange("p t c -> p (t c)"), core.ps[:, bank, :], ACT_FN.Copy))
            wait(G, m_work, m_end)
            for j in range(HEADS_PER_GROUP):
                m_qof = st.pool.after(G.tensor_scalar(
                    q_of[:, half * TPG:(half + 1) * TPG, j, :], q[:, cols].rearrange("p (t n) -> p t n", n=P),
                    core.head_in_4[:, j:j + 1], None, ALU.mult))
        for c in range(TPB):
            if c % TPG == 0:
                m_heads = None
            o_slot, o_bank, o_free = ring.take()
            out = core.ps[:, o_bank, 0:HEADS * VW]
            m_masked = []
            for gr in range(HEADS // HEADS_PER_GROUP):
                slot, bank, free = ring.take()
                wait(T, free, m_qof, m_work)
                rows = slice(32 * gr, 32 * (gr + 1))
                m = st.pe.after(T.matmul(core.ps[:, bank, :], k[rows, c * P:(c + 1) * P],
                                         q_of[rows, c, :, :].rearrange("p j t -> p (j t)"), start=True, stop=True))
                wait(V, m, m_scores_free.get(n_scores - 4))
                m = ring.free[slot] = st.dve.after(V.tensor_tensor(
                    scores[:, n_scores % 4, :].rearrange("p (j t) -> p j t", j=HEADS_PER_GROUP),
                    core.ps[:, bank, :].rearrange("p (j t) -> p j t", j=HEADS_PER_GROUP),
                    core.causal[:, None, :].broadcast_to([P, HEADS_PER_GROUP, P]), ALU.mult))
                m_masked.append((n_scores, m))
                n_scores += 1
            wait(T, o_free)
            if c:
                wait(T, m_state)
                T.matmul(out, q[:, c * P:(c + 1) * P], state[:, :], start=True, stop=False)
            for gr, (n, m) in enumerate(m_masked):
                wait(T, m, m_v)
                for j in range(HEADS_PER_GROUP):
                    hd = gr * HEADS_PER_GROUP + j
                    mm = T.matmul(out[:, hd * VW:(hd + 1) * VW], scores[:, n % 4, j * P:(j + 1) * P], v[:, c, hd, :],
                                  start=c == 0, stop=c == 0 or hd == HEADS - 1)
                m_out = m_scores_free[n] = st.pe.after(mm)
            if c < TPB - 1:
                slot, bank, free = ring.take()
                wait(T, free, m_ktok)
                m = st.pe.after(T.matmul(core.ps[:, bank, 0:HEADS * VW], k_tok[:, c, :],
                                         v[:, c, :, :].rearrange("p h c -> p (h c)"), start=True, stop=True))
                wait(V, m, m_out)
                dst = state if c == 0 else update
                m = ring.free[slot] = st.dve.after(V.tensor_tensor(dst[:, :], core.ps[:, bank, 0:HEADS * VW],
                                                                   core.own_block[:, :], ALU.mult))
                if c:
                    wait(V, m)
                    m = st.dve.after(V.tensor_tensor(state[:, :], state[:, :], update[:, :], ALU.add))
                m_state = m
            got = out.rearrange("p (h c) -> p h c", c=VW)
            wait(V, m_out)
            m = st.dve.after(V.reciprocal(inv[:, :], got[:, :, HD]))
            wait(V, m, m_heads_free)
            m = ring.free[o_slot] = st.dve.after(V.tensor_tensor(
                heads_out[:, c % TPG, :].rearrange("p (h d) -> p h d", h=HEADS), got[:, :, 0:HD],
                inv[:, :, None].broadcast_to([P, HEADS, HD]), ALU.mult))
            if c % TPG == TPG - 1:
                m_heads_free, m_scratch = project_group(
                    core, st, ring, heads_out[:, :, :], m, 2 * b + c // TPG, w["qkvo"][:, 3, :], w["o_bias"],
                    scratch[:, :], m_scratch)
        m_end = (st.pe, st.pe.count)
    st.close()


def macaron_kernel(nc, t, stages=6, first=0):
    with ExitStack() as ctx:
        core = Core(nc, ctx)
        S, V, G = nc.sync, nc.vector, nc.gpsimd
        core.x = core.sbuf("x", [P, TILES, DIM])
        core.ps = ctx.enter_context(nc.psum_tensor("ps", [P, 8, BANK], F32))
        load = Stage(core, "load")
        done = load.dma_signal("in")

        def loaded(name, shape, dtype=F32, engine=S):
            buf = core.sbuf("c_" + name, shape, dtype)
            done.after(engine.dma_start(buf[:], t[name]), 16)
            return buf

        tiles = t["x"].rearrange("(n p) c -> p n c", p=P)
        for b in range(BATCH):
            done.after(S.dma_start(core.x[:, b * TPB:(b + 1) * TPB, :], tiles[:, b * TPB:(b + 1) * TPB, :]), 16)
        core.ident = loaded("ident", [P, P])
        mix_w = loaded("mix_w", [P, 3, DIM])
        mus = loaded("mus", [P, 2])
        core.causal = loaded("causal", [P, P])
        core.own_block = loaded("own_block", [P, HEADS * (HD + 1)])
        core.head_in_4 = loaded("head_in_4", [P, HEADS_PER_GROUP])
        core.slot_tile = loaded("slot_tile", [P, SLOT_TILES])
        core.spare_row = loaded("spare_row", [P, SLOT_TILES])
        core.iota_p = loaded("iota_p", [P, P])
        core.lane1 = loaded("lane1", [P, 1])
        core.rev_expert = loaded("rev_expert", [P, EXPERTS])
        scale = loaded("norm_scale", [P, 1])
        qkv_w = loaded("qk_w", [P, 4, DIM])
        attn_vo = loaded("attn_vo", [P, 2, DIM])
        attn_b = loaded("attn_b", [P, 4])
        attn_rows = loaded("attn_rows", [P, 2, DIM])
        lin_w = loaded("lin_w", [P, 4, DIM])
        lin_b = loaded("lin_b", [P, 2])
        lin_rows = loaded("lin_rows", [P, 2, DIM])
        before_f = loaded("before", [P, P])
        router = loaded("router", [P, EXPERTS])
        core.before = core.sbuf("before_bf", [P, P], BF16)
        core.ones_bf = core.sbuf("ones_bf", [P, P], BF16)
        core.zeros = core.sbuf("zeros", [P, TILES * EXPERTS])
        load.pool.after(G.memset(core.zeros[:, :], 0.0))
        load.pool.after(G.memset(core.ones_bf[:, :], 1.0))
        wait(V, (done, done.count))
        load.dve.after(V.tensor_copy(core.before[:, :], before_f[:, :]))
        load.dve.after(V.tensor_scalar(router[:, :], router[:, :], scale[:, 0:1], None, ALU.mult))
        load.close()

        dram = {
            "parts": nc.dram_tensor("qk_parts", [2, 2, 3, P, SEQ], BF16, kind="Internal").ap(),
            "maxima": nc.dram_tensor("row_maxima", [BATCH, 2, P, P], BF16, kind="Internal").ap(),
            "tokens": nc.dram_tensor("tokens", [TOKENS, DIM], F32, kind="Internal").ap(),
            "routed": nc.dram_tensor("routed", [TOKENS * TOPK + SLOTS, DIM], F32, kind="Internal").ap(),
        }
        mix = [mix_w[:, i, :] for i in range(3)]

        def expert_weights(name):
            st = Stage(core, name)
            up = core.late.enter_context(nc.sbuf_tensor(name + "_up_w", [P, EXPERTS * 2 * HIDDEN], F32))
            down = core.late.enter_context(nc.sbuf_tensor(name + "_down_w", [P, 2 * EXPERTS * DIM], F32))
            d = st.dma_signal("in")
            d.after(S.dma_start(up[:, :], t["up"]), 16)
            d.after(S.dma_start(down[:, :], t["down"]), 16)
            wait(V, (d, d.count))
            st.dve.after(V.tensor_scalar(up[:, :], up[:, :], scale[:, 0:1], None, ALU.mult))
            st.close()
            return {"router": router[:, :], "up": up[:, :], "down": down[:, :]}

        if first < 1 <= stages:
            channel_mix(core, "mix1", mix, mus[:, 0:1], mus[:, 1:2])
        if first < 2 <= stages:
            with ExitStack() as rope_ctx:
                core.cos = rope_ctx.enter_context(nc.sbuf_tensor("cos", [P, SEQ], F32))
                core.sin = rope_ctx.enter_context(nc.sbuf_tensor("sin", [P, SEQ], F32))
                core.xt_attn = rope_ctx.enter_context(nc.sbuf_tensor("xt_attn", [P, BATCH, SEQ], F32))
                rope = Stage(core, "rope")
                d = rope.dma_signal("in")
                d.after(S.dma_start(core.cos[:, :], t["cos"]), 16)
                d.after(S.dma_start(core.sin[:, :], t["sin"]), 16)
                rope.close()
                softmax_attention(core, {
                    "qk": qkv_w[:, :, :], "qk_bias": attn_b[:, :], "v": attn_vo[:, 0, :], "v_bias": attn_rows[:, 0, :],
                    "proj": attn_vo[:, 1, :], "proj_bias": attn_rows[:, 1, :]}, dram)
        if first < 3 <= stages:
            channel_mix(core, "mix2", mix, mus[:, 0:1], mus[:, 1:2])
        with ExitStack() as core.late:
            moe_w = expert_weights("moe") if stages > 3 else None
            if first < 4 <= stages:
                experts(core, "moe1", moe_w, dram)
            if first < 5 <= stages:
                linear_attention(core, {"qkvo": lin_w[:, :, :], "qk_bias": lin_b[:, :], "v_bias": lin_rows[:, 0, :],
                                        "o_bias": lin_rows[:, 1, :]})
            if first < 6 <= stages:
                experts(core, "moe2", moe_w, dram)
        out = Stage(core, "store")
        d = out.dma_signal("out")
        d.after(S.dma_start(t["out"].rearrange("(n p) c -> p n c", p=P), core.x[:, :, :]), 16)
        out.close()


def constants():
    ar = np.arange
    inv_freq = (np.float32(1.0) / np.float32(10000.0) ** (ar(0, HD, 2, dtype=np.float32) / np.float32(HD))).astype(np.float32)
    freqs = ar(SEQ, dtype=np.float32)[:, None] * inv_freq[None, :]
    emb = np.concatenate([freqs, freqs], axis=-1).astype(np.float32)
    cos, sin = np.cos(emb), np.sin(emb)
    sign = np.where(ar(HD) % 2 == 0, -1.0, 1.0).astype(np.float32)
    head = ar(P) // HD
    own = (head[:, None] == ar(HEADS)[None, :]).astype(np.float32)
    spare = TOKENS * TOPK + ar(SLOT_TILES)[None, :] * P + ar(P)[:, None]
    f = np.float32
    return {
        "cos": np.tile(cos.T, (HEADS, 1)).astype(f), "sin": np.tile((sin * sign).T, (HEADS, 1)).astype(f),
        "ident": np.eye(P, dtype=f),
        "causal": (ar(P)[:, None] <= ar(P)[None, :]).astype(f),
        "before": (ar(P)[:, None] < ar(P)[None, :]).astype(f),
        "own_block": np.repeat(own, HD + 1, axis=1).astype(f),
        "head_in_4": (head[:, None] % HEADS_PER_GROUP == ar(HEADS_PER_GROUP)[None, :]).astype(f),
        "slot_tile": np.tile(ar(SLOT_TILES, dtype=f), (P, 1)), "spare_row": spare.astype(f),
        "iota_p": np.tile(ar(P, dtype=f), (P, 1)), "lane1": ar(1, P + 1, dtype=f)[:, None],
        "rev_expert": np.tile(ar(EXPERTS, 0, -1, dtype=f), (P, 1)),
    }


def layout(i):
    c = np.ascontiguousarray
    swap = np.arange(DIM) ^ 1
    qkv, qb = np.asarray(i["L0_attn_qkv_w"]), np.asarray(i["L0_attn_qkv_b"])
    a = {k: np.asarray(v) for k, v in i.items()}

    def cols(*ws):
        return c(np.stack([w.T for w in ws], axis=1))

    def rows(*bs):
        return c(np.broadcast_to(np.stack(bs)[None], (P, len(bs), DIM)))

    q, k, v = qkv[:DIM], qkv[DIM:2 * DIM], qkv[2 * DIM:]
    bq, bk, bv = qb[:DIM], qb[DIM:2 * DIM], qb[2 * DIM:]
    down = a["L1_ffn_w_down"].transpose(2, 0, 1).reshape(2, P, EXPERTS, DIM)
    return {
        "x": c(a["L0_attn_x"].reshape(TOKENS, DIM)),
        "mix_w": cols(a["L0_ffn_W_r"], a["L0_ffn_W_k"], a["L0_ffn_W_v"]),
        "mus": c(np.stack([a["L0_ffn_mu_r"], a["L0_ffn_mu_k"]], axis=1)),
        "qk_w": cols(q, q[swap], k, k[swap]), "attn_vo": cols(v, a["L0_attn_proj_w"]),
        "attn_b": c(np.stack([bq, bq[swap], bk, bk[swap]], axis=1)), "attn_rows": rows(bv, a["L0_attn_proj_b"]),
        "lin_w": cols(a["L1_attn_Wq"], a["L1_attn_Wk"], a["L1_attn_Wv"], a["L1_attn_Wo"]),
        "lin_b": c(np.stack([a["L1_attn_bq"], a["L1_attn_bk"]], axis=1)), "lin_rows": rows(a["L1_attn_bv"], a["L1_attn_bo"]),
        "norm_scale": c(a["L1_ffn_norm_scale"][:, None]), "router": c(a["L1_ffn_w_router"].T),
        "up": c(a["L1_ffn_w_up"].transpose(2, 0, 1).reshape(P, EXPERTS * 2 * HIDDEN)),
        "down": c(down.transpose(1, 0, 2, 3).reshape(P, 2 * EXPERTS * DIM)),
    }


def kernel(**inputs):
    import concourse.bacc as _bacc
    from concourse.bass_utils import run_bass_kernel_spmd as _run

    nc = _bacc.Bacc("TRN2", target_bir_lowering=False, num_devices=1)
    arrays = {**layout(inputs), **constants()}
    t = {n: nc.dram_tensor("in_" + n, a.shape, mybir.dt.from_np(a.dtype), kind="ExternalInput").ap()
         for n, a in arrays.items()}
    t["out"] = nc.dram_tensor("out_0", (TOKENS, DIM), F32, kind="ExternalOutput").ap()
    macaron_kernel(nc, t)
    r = _run(nc, [{"in_" + n: a for n, a in arrays.items()}], core_ids=[0])
    return r.results[0]["out_0"].reshape(BATCH, SEQ, DIM)
```

```python
from contextlib import ExitStack
from itertools import chain

import numpy as np

import concourse.bass as bass
from concourse import mybir

F32 = mybir.dt.float32
BF16 = mybir.dt.bfloat16
I32 = mybir.dt.int32
U32 = mybir.dt.uint32
ALU = mybir.AluOpType
ACT_FN = mybir.ActivationFunctionType
AX_X = mybir.AxisListType.X

P = 128
BATCH, SEQ, DIM = 4, 1024, 128
TOKENS = BATCH * SEQ
TILES = TOKENS // P
TPB = SEQ // P
BANK = 512
TPG = BANK // P
GROUPS = TILES // TPG
HEADS, HD = 16, 8
EXPERTS, TOPK, HIDDEN = 8, 2, 256
LN_EPS, RMS_EPS = 1e-5, 1e-6
SLOT_TILES = TOKENS * TOPK // P + EXPERTS - 1
SLOTS = SLOT_TILES * P
Q_PARTS = (0, 0, 1, 1, 0, 2)
K_PARTS = (0, 1, 0, 1, 2, 0)
QK_ROWS = len(Q_PARTS) * HD
MAX_ROWS = 2
MAX_SCORE = 62.0
STACK = 64
PAIRS = HEADS // 2
HEADS_PER_GROUP = 4


class Step:

    def __init__(self, issue):
        self.issue, self.raises = issue, []

    def then_inc(self, sem, by):
        self.raises.append((sem, by))


class Queue:

    def __init__(self):
        self.steps = []

    def put(self, issue):
        self.steps.append(Step(issue))
        return self.steps[-1]

    def issue_all(self, engine):
        for step in self.steps:
            instruction = step.issue(engine)
            for sem, by in step.raises:
                instruction.then_inc(sem, by)

    def only_if(self, flag, body):
        def issue(engine):
            with engine.If(engine.value_load(flag, min_val=0, max_val=1) != 0):
                body.issue_all(engine)
        self.put(issue)

    def wait_ge(self, *a):
        return self.put(lambda e: e.wait_ge(*a))

    def dma_start(self, *a, **k):
        return self.put(lambda e: e.dma_start(*a, **k))

    def indirect_dma_start(self, *a, **k):
        return self.put(lambda e: e.indirect_dma_start(*a, **k))

    def matmul(self, *a, **k):
        return self.put(lambda e: e.matmul(*a, **k))

    def matmul_by_expert(self, out, stationary, moving, width, offset, start=True, stop=True):
        def issue(e):
            at = e.value_load(offset, min_val=0, max_val=(EXPERTS - 1) * width)
            return e.matmul(out, stationary, moving[:, bass.ds(at, width)], start=start, stop=stop)
        return self.put(issue)

    def transpose(self, *a, **k):
        return self.put(lambda e: e.transpose(*a, **k))

    def activation(self, *a, **k):
        return self.put(lambda e: e.activation(*a, **k))

    def memset(self, *a, **k):
        return self.put(lambda e: e.memset(*a, **k))

    def tensor_copy(self, *a, **k):
        return self.put(lambda e: e.tensor_copy(*a, **k))

    def tensor_scalar(self, *a, **k):
        return self.put(lambda e: e.tensor_scalar(*a, **k))

    def tensor_tensor(self, *a, **k):
        return self.put(lambda e: e.tensor_tensor(*a, **k))

    def scalar_tensor_tensor(self, *a, **k):
        return self.put(lambda e: e.scalar_tensor_tensor(*a, **k))

    def tensor_tensor_scan(self, *a, **k):
        return self.put(lambda e: e.tensor_tensor_scan(*a, **k))

    def tensor_reduce(self, *a, **k):
        return self.put(lambda e: e.tensor_reduce(*a, **k))

    def reciprocal(self, *a, **k):
        return self.put(lambda e: e.reciprocal(*a, **k))

    def bn_stats(self, *a, **k):
        return self.put(lambda e: e.bn_stats(*a, **k))

    def bn_aggr(self, *a, **k):
        return self.put(lambda e: e.bn_aggr(*a, **k))


class Program:

    def __init__(self, nc):
        self.sbuf_tensor, self.psum_tensor = nc.sbuf_tensor, nc.psum_tensor
        self.semaphore, self.dram_tensor = nc.semaphore, nc.dram_tensor
        self.tensor, self.vector, self.scalar, self.gpsimd, self.sync = (Queue() for _ in range(5))

    def build(self, nc):
        with nc.Block() as block:
            block.tensor(self.tensor.issue_all)
            block.vector(self.vector.issue_all)
            block.scalar(self.scalar.issue_all)
            block.gpsimd(self.gpsimd.issue_all)
            block.sync(self.sync.issue_all)


class Signal:

    def __init__(self, nc, ctx, name):
        self.sem, self.count, self.name = ctx.enter_context(nc.semaphore(name)), 0, name

    def after(self, instruction, by=1):
        instruction.then_inc(self.sem, by)
        self.count += by
        return (self, self.count)


def wait(engine, *marks):
    for mark in marks:
        if mark is not None:
            engine.wait_ge(mark[0].sem, mark[1])


class Ring:

    def __init__(self, banks):
        self.banks, self.free, self.n = list(banks), [None] * len(banks), -1

    def take(self):
        self.n = (self.n + 1) % len(self.banks)
        return self.n, self.banks[self.n], self.free[self.n]


class Stage:

    def __init__(self, core, name):
        self.core, self.nc, self.name, self.ctx = core, core.nc, name, ExitStack()
        ctx = core.ctx
        self.pe = Signal(self.nc, ctx, f"{name}_pe")
        self.dve = Signal(self.nc, ctx, f"{name}_dve")
        self.act = Signal(self.nc, ctx, f"{name}_act")
        self.pool = Signal(self.nc, ctx, f"{name}_pool")
        self.dmas = []

    def sbuf(self, name, shape, dtype=F32):
        return self.ctx.enter_context(self.nc.sbuf_tensor(f"{self.name}_{name}", shape, dtype))

    def dma_signal(self, name):
        s = Signal(self.nc, self.core.ctx, f"{self.name}_{name}")
        self.dmas.append(s)
        return s

    def close(self):
        for engine in self.core.engines:
            for s in (self.pe, self.dve, self.act, self.pool, *self.dmas):
                if s.count:
                    wait(engine, (s, s.count))
        self.ctx.close()


PRODUCT, OTHER = "uses the tensor engine", "doesn't"


class Side:

    def __init__(self):
        self.work = []

    def add(self, work, first=False):
        one = [work, next(work)]
        self.work.insert(0 if first else len(self.work), one)
        return one

    def piece(self, one):
        try:
            one[1] = next(one[0])
        except StopIteration:
            self.work.remove(one)

    def run(self):
        products = 0
        for one in self.work[:2]:
            if one[1] == PRODUCT:
                products += 1
                if products > 1:
                    continue
            self.piece(one)

    def finish(self, one):
        while one in self.work:
            self.piece(one)

    def finish_all(self):
        while self.work:
            self.finish(self.work[0])


class Core:

    def __init__(self, nc, ctx):
        self.nc, self.ctx = nc, ctx
        self.engines = (nc.tensor, nc.vector, nc.scalar, nc.gpsimd, nc.sync)

    def sbuf(self, name, shape, dtype=F32):
        return self.ctx.enter_context(self.nc.sbuf_tensor(name, shape, dtype))


def take_statistics(core, st, group, ready):
    wait(core.nc.vector, ready)
    for t in range(group * TPG, (group + 1) * TPG):
        m = st.dve.after(core.nc.vector.bn_stats(out=core.stats[:, t, :], in_=core.x[:, t, :]))
    return m


def norm_factors(core, st, with_rms=False):
    nc = core.nc
    V = nc.vector
    st.moments = st.sbuf("moments", [P, TILES, 2])
    var, std, fix = (st.sbuf(f"ln_{k}", [P, TILES]) for k in ("var", "std", "fix"))
    st.rstd = st.sbuf("rstd", [P, TILES])
    for t in range(TILES):
        m = st.dve.after(V.bn_aggr(out=st.moments[:, t, :], in_=core.stats[:, t, :]))
    wait(V, m)

    def chained(instruction):
        m = st.dve.after(instruction)
        wait(V, m)
        return m

    def inverse_root(m, out):
        wait(nc.scalar, m)
        m = st.act.after(nc.scalar.activation(std[:, :], var[:, :], ACT_FN.Sqrt))
        wait(V, m)
        chained(V.reciprocal(out, std[:, :]))
        chained(V.tensor_tensor(fix[:, :], var[:, :], out, ALU.mult))
        chained(V.tensor_tensor(fix[:, :], fix[:, :], out, ALU.mult))
        chained(V.tensor_scalar(fix[:, :], fix[:, :], -0.5, 1.5, ALU.mult, ALU.add))
        return chained(V.tensor_tensor(out, out, fix[:, :], ALU.mult))

    m = chained(V.tensor_scalar(var[:, :], st.moments[:, :, 1], LN_EPS, None, ALU.add))
    m = inverse_root(m, st.rstd[:, :])
    if with_rms:
        st.scale_rms = st.sbuf("rms_scale", [P, TILES])
        chained(V.tensor_tensor(var[:, :], st.moments[:, :, 1], st.rstd[:, :], ALU.mult))
        chained(V.tensor_tensor(var[:, :], var[:, :], st.rstd[:, :], ALU.mult))
        m = chained(V.tensor_scalar(var[:, :], var[:, :], RMS_EPS, None, ALU.add))
        m = inverse_root(m, st.scale_rms[:, :])
    return m


def normalised(core, st, group, out, factors_ready, free=None):
    V = core.nc.vector
    wait(V, factors_ready, free)
    for i in range(TPG):
        t = group * TPG + i
        m = st.dve.after(V.tensor_scalar(out[:, i, :], core.x[:, t, :], st.moments[:, t, 0:1], st.rstd[:, t:t + 1],
                                         ALU.subtract, ALU.mult))
    return m


def to_channels(core, st, ring, source, ready, out, engine):
    nc = core.nc
    slot, bank, free = ring.take()
    wait(nc.tensor, free, ready)
    for i in range(TPG):
        m = nc.tensor.transpose(core.ps[:, bank, i * P:(i + 1) * P], source[:, i, :], core.ident[:, :])
    m_read = m = st.pe.after(m)
    if engine == "act":
        wait(nc.scalar, m)
        ring.free[slot] = st.act.after(nc.scalar.activation(out, core.ps[:, bank, :], ACT_FN.Copy))
    else:
        wait(nc.vector, m)
        ring.free[slot] = st.dve.after(nc.vector.tensor_copy(out, core.ps[:, bank, :]))
    return m_read, ring.free[slot]


def channel_mix(core, name, w, mu_r, mu_k):
    nc = core.nc
    T, V, A, G = nc.tensor, nc.vector, nc.scalar, nc.gpsimd
    st = Stage(core, name)
    ring = Ring(range(8))
    m_factors = norm_factors(core, st)
    xt = st.sbuf("xt", [P, BATCH, 1 + SEQ])
    m_zero = st.pool.after(G.memset(xt[:, :, 0:1], 0.0))
    rest = st.sbuf("rest", [P, 2])
    mixed = st.sbuf("mixed", [P, 4, DIM])
    for i, mu in enumerate((mu_r, mu_k)):
        m = st.dve.after(V.tensor_scalar(rest[:, i:i + 1], mu, -1.0, 1.0, ALU.mult, ALU.add))
    wait(V, m)
    for i, (wt, mu) in enumerate(((w[0], mu_r), (w[1], mu_k))):
        V.tensor_scalar(mixed[:, 2 * i, :], wt, mu, None, ALU.mult)
        m_mixed = st.dve.after(V.tensor_scalar(mixed[:, 2 * i + 1, :], wt, rest[:, i:i + 1], None, ALU.mult))
    wait(T, m_zero, m_mixed)
    NB = 2
    relu, act, gate, value = (st.sbuf(k, [P, NB, BANK]) for k in ("relu", "act", "gate", "value"))
    xn = st.sbuf("xn", [P, NB, TPG, DIM])
    m_xn_read, m_added = {}, {}
    m_act, m_gate, m_value_free, m_v = {}, {}, {}, {}

    def value_and_add(g):
        slot, bank, free = ring.take()
        wait(T, free, m_act[g])
        for i in range(TPG):
            m = T.matmul(core.ps[:, bank, i * P:(i + 1) * P], act[:, g % NB, i * P:(i + 1) * P], w[2],
                         start=True, stop=True)
        m = m_v[g] = st.pe.after(m)
        wait(V, m, m_gate[g], m_value_free.get(g - NB))
        m = st.dve.after(V.scalar_tensor_tensor(value[:, g % NB, :], core.ps[:, bank, :], 0.5, gate[:, g % NB, :],
                                                ALU.mult, ALU.mult))
        ring.free[slot] = m
        wait(G, m)
        xg = core.x[:, g * TPG:(g + 1) * TPG, :].rearrange("p t c -> p (t c)")
        m_added[g] = m_value_free[g] = st.pool.after(G.tensor_tensor(xg, xg, value[:, g % NB, :], ALU.add))

    m_xt = {}

    def prepare(g):
        b, at = g // 2, (g % 2) * BANK
        m = normalised(core, st, g, xn[:, g % NB, :, :], m_factors, m_xn_read.get(g - NB))
        m_xn_read[g], m_xt[g] = to_channels(core, st, ring, xn[:, g % NB, :, :], m, xt[:, b, 1 + at:1 + at + BANK],
                                            "act" if g % 2 else "dve")

    prepare(0)
    for g in range(GROUPS):
        b, at = g // 2, (g % 2) * BANK
        if g + 1 < GROUPS:
            prepare(g + 1)
        slot, bank, free = ring.take()
        wait(T, free, m_xt[g])
        T.matmul(core.ps[:, bank, :], mixed[:, 2, :], xt[:, b, 1 + at:1 + at + BANK], start=True, stop=False)
        m = st.pe.after(T.matmul(core.ps[:, bank, :], mixed[:, 3, :], xt[:, b, at:at + BANK], start=False, stop=True))
        wait(V, m, m_act.get(g - NB))
        m = ring.free[slot] = st.dve.after(V.tensor_scalar(relu[:, g % NB, :], core.ps[:, bank, :], 0.0, None, ALU.max))
        wait(A, m, m_v.get(g - NB))
        m_act[g] = st.act.after(A.activation(act[:, g % NB, :], relu[:, g % NB, :], ACT_FN.Square))
        slot, bank, free = ring.take()
        wait(T, free)
        for i in range(TPG):
            o = core.ps[:, bank, i * P:(i + 1) * P]
            T.matmul(o, xt[:, b, 1 + at + i * P:1 + at + (i + 1) * P], mixed[:, 0, :], start=True, stop=False)
            m = T.matmul(o, xt[:, b, at + i * P:at + (i + 1) * P], mixed[:, 1, :], start=False, stop=True)
        m = st.pe.after(m)
        wait(A, m, m_value_free.get(g - NB))
        m_gate[g] = ring.free[slot] = st.act.after(A.activation(gate[:, g % NB, :], core.ps[:, bank, :], ACT_FN.Sigmoid))
        if g:
            value_and_add(g - 1)
        if g > 1:
            take_statistics(core, st, g - 2, m_added[g - 2])
    value_and_add(GROUPS - 1)
    for g in (GROUPS - 2, GROUPS - 1):
        take_statistics(core, st, g, m_added[g])
    st.close()


def project_group(core, st, ring, heads_out, ready, group, weights, bias_rows, scratch, scratch_free):
    nc = core.nc
    T, V = nc.tensor, nc.vector
    slot, bank, free = ring.take()
    wait(T, free, ready)
    for i in range(TPG):
        m = T.transpose(core.ps[:, bank, i * P:(i + 1) * P], heads_out[:, i, :], core.ident[:, :])
    m_read = m = st.pe.after(m)
    wait(V, m, scratch_free)
    m = ring.free[slot] = st.dve.after(V.tensor_copy(scratch, core.ps[:, bank, :]))
    yield PRODUCT
    slot, bank, free = ring.take()
    wait(T, free, m)
    for i in range(TPG):
        m = T.matmul(core.ps[:, bank, i * P:(i + 1) * P], scratch[:, i * P:(i + 1) * P], weights, start=True, stop=True)
    m_scratch = m = st.pe.after(m)
    xg = core.x[:, group * TPG:(group + 1) * TPG, :]
    wait(V, m)
    m = ring.free[slot] = st.dve.after(V.tensor_tensor(
        xg, xg, core.ps[:, bank, :].rearrange("p (t c) -> p t c", t=TPG), ALU.add))
    wait(nc.gpsimd, m)
    m_added = st.pool.after(nc.gpsimd.tensor_tensor(xg, xg, bias_rows[:, None, :].broadcast_to([P, TPG, DIM]), ALU.add))
    return m_read, m_scratch, m_added


def softmax_attention(core, w, dram):
    nc = core.nc
    T, V, A, G, S = nc.tensor, nc.vector, nc.scalar, nc.gpsimd, nc.sync
    st = Stage(core, "attn")
    qs = st.sbuf("q_stack", [P, 2, PAIRS, SEQ], BF16)
    ks = st.sbuf("k_stack", [P, 2, 2, PAIRS, SEQ], BF16)
    m_zero = st.pool.after(G.memset(ks[:, :, :, :, :].rearrange("p b s r t -> p (b s r t)").bitcast(F32), 0.0))
    m_zero_q = st.pool.after(G.memset(qs[:, :, :, :].rearrange("p b r t -> p (b r t)").bitcast(F32), 0.0))
    v = st.sbuf("v", [P, 2, TPB, HEADS, HD + 1])
    m_vconst = st.pool.after(G.memset(v[:, :, :, :, HD:HD + 1], 1.0))
    wait(G, m_vconst)
    for s in range(2):
        m_ones = st.pool.after(G.memset(ks[s * STACK + 32:(s + 1) * STACK, :, s, :, :], 1.0))
        wait(G, m_ones)

    pre = Stage(core, "attn_ln")
    ring = Ring(range(8))
    m_factors = norm_factors(core, pre)
    xt = core.xt_attn
    xn = pre.sbuf("xn", [P, 2, TPG, DIM])
    m_xn_read = {}
    for g in range(GROUPS):
        m = normalised(core, pre, g, xn[:, g % 2, :, :], m_factors, m_xn_read.get(g - 2))
        m_xn_read[g], _ = to_channels(core, pre, ring, xn[:, g % 2, :, :], m,
                                      xt[:, g // 2, (g % 2) * BANK:(g % 2 + 1) * BANK], "act" if g % 2 else "dve")
    pre.close()

    E_BANKS, AUX_BANKS, PV_BANK = (0, 2), (4, 5, 6), 7
    ring = Ring(AUX_BANKS)
    HALVES = SEQ // BANK
    probs = st.sbuf("probs", [P, 2, HEADS_PER_GROUP * BANK])
    t_cos, t_sin, roped, square = (st.sbuf(k, [P, BANK]) for k in ("t_cos", "t_sin", "roped", "square"))
    parts = st.sbuf("parts", [P, 2, 3, BANK], BF16)
    norms = st.sbuf("norms", [P, 2, 2, HALVES])
    top_norm = st.sbuf("top_norm", [P, 2])
    bound = st.sbuf("bound", [P, 1])
    bound_of = st.sbuf("bound_of", [P, P])
    lowest = st.sbuf("lowest", [P, 1])
    wide = st.sbuf("wide", [P, BATCH], I32)
    half_max = st.sbuf("half_max", [P, HEADS, TPB, HALVES])
    neg_max = st.sbuf("neg_max", [P, HEADS * TPB])
    max_parts = st.sbuf("max_parts", [P, 2, P], BF16)
    sums = st.sbuf("sums", [P, 2, BANK])
    inv = st.sbuf("inv", [P, TPG, HEADS_PER_GROUP])
    heads_out = st.sbuf("heads_out", [P, HALVES, TPG, DIM])
    scratch = st.sbuf("proj_in", [P, BANK])
    parts_dma = [st.dma_signal(f"parts_store{i}") for i in range(2)]
    stack_dma = [st.dma_signal(f"stack_load{i}") for i in range(2)]
    max_store, max_load = st.dma_signal("max_store"), st.dma_signal("max_load")

    m_pv_zero = st.dve.after(V.memset(core.ps[:, PV_BANK, :], 0.0))
    wait(T, m_pv_zero)
    wait(S, m_zero, m_zero_q, m_ones)
    wait(V, m_vconst)

    m_stack_free = [None, None]
    m_v_free = [None, None]
    m_stack, m_v, m_max, m_norm = {}, {}, {}, {}
    last = {"cos": None, "parts": [None, None], "square": None}
    n_parts = [0]

    def project(b):
        for qk in range(2):
            for half in range(HALVES):
                cols = slice(half * BANK, (half + 1) * BANK)
                out = []
                for which in range(2):
                    slot, bank, free = ring.take()
                    wait(T, free)
                    m = st.pe.after(T.matmul(core.ps[:, bank, :], w["qk"][:, 2 * qk + which, :], xt[:, b, cols],
                                             start=True, stop=True))
                    wait(V, m, last["cos"])
                    table, dst = ((core.cos, t_cos), (core.sin, t_sin))[which]
                    m = st.dve.after(V.scalar_tensor_tensor(
                        dst[:, :], core.ps[:, bank, :], w["qk_bias"][:, 2 * qk + which:2 * qk + which + 1],
                        table[:, cols], ALU.add, ALU.mult))
                    ring.free[slot] = m
                wait(G, m)
                m = st.pool.after(G.tensor_tensor(roped[:, :], t_cos[:, :], t_sin[:, :], ALU.add))
                last["cos"] = m
                wait(A, m, last["square"])
                m_square = st.act.after(A.activation(square[:, :], roped[:, :], ACT_FN.Square))
                slot, bank, free = ring.take()
                wait(T, free, m_square)
                m_norm2 = last["square"] = st.pe.after(T.matmul(core.ps[:, bank, :], core.same_head[:, :], square[:, :],
                                                                start=True, stop=True))
                wait(V, m_norm2)
                m_norm[b] = ring.free[slot] = st.dve.after(V.tensor_reduce(
                    norms[:, b % 2, qk, half:half + 1], core.ps[:, bank, :], AX_X, ALU.max))
                k = n_parts[0] % 2
                n_parts[0] += 1
                wait(G, m, last["parts"][k])
                for part in range(3):
                    m = st.pool.after(G.tensor_copy(parts[:, k, part, :], roped[:, :]))
                    wait(G, m, m_square)
                    if part < 2:
                        m = st.pool.after(G.tensor_tensor(roped[:, :], roped[:, :], parts[:, k, part, :], ALU.subtract))
                        wait(G, m)
                wait(S, m)
                last["parts"][k] = parts_dma[k].after(
                    S.dma_start(dram["parts"][b % 2, qk, :, :, cols].rearrange("k p t -> p k t"), parts[:, k, :, :]), 16)
                yield

    def values(b):
        for half in range(HALVES):
            slot, bank, free = ring.take()
            wait(T, free)
            for i in range(TPG):
                at = half * BANK + i * P
                m = T.matmul(core.ps[:, bank, i * P:(i + 1) * P], xt[:, b, at:at + P], w["v"], start=True, stop=True)
            m = st.pe.after(m)
            wait(V, m, m_v_free[b % 2])
            for i in range(TPG):
                m = st.dve.after(V.tensor_tensor(
                    v[:, b % 2, half * TPG + i, :, 0:8],
                    core.ps[:, bank, i * P:(i + 1) * P].rearrange("p (h d) -> p h d", h=HEADS),
                    w["v_bias"].rearrange("p (h d) -> p h d", h=HEADS), ALU.add))
            m_v[b] = ring.free[slot] = m
            yield

    def load_stacks(b):
        wait(S, *last["parts"], m_stack_free[b % 2])
        for s in range(2):
            for row, (qp, kp) in enumerate(zip(Q_PARTS, K_PARTS)):
                for qk, dst, part in ((0, qs, qp), (1, ks, kp)):
                    src = dram["parts"][b % 2, qk, part].rearrange("(r s d) t -> s d r t", s=2, d=HD)[s]
                    first = s * STACK + row * HD
                    rows = slice(first, first + HD)
                    m = stack_dma[b % 2].after(S.dma_start(dst[rows, b % 2, s, :, :] if qk else dst[rows, b % 2, :, :],
                                                           src), 16)
        m_stack[b] = m

    def true_maxima(b):
        pe, dve = Signal(nc, core.ctx, f"max_pe{b}"), Signal(nc, core.ctx, f"max_dve{b}")
        products, reductions = Queue(), Queue()
        turns = [(pair, qt, s, half) for pair in range(PAIRS) for qt in range(TPB) for s in range(2)
                 for half in range(HALVES)]
        m_reduced = {}
        for i, (pair, qt, s, half) in enumerate(turns):
            rows = slice(s * STACK, s * STACK + QK_ROWS)
            bank = AUX_BANKS[i % len(AUX_BANKS)]
            wait(products, m_reduced.get(i - len(AUX_BANKS)))
            m = pe.after(products.matmul(core.ps[:, bank, :], qs[rows, b % 2, pair, qt * P:(qt + 1) * P],
                                         ks[rows, b % 2, s, pair, half * BANK:(half + 1) * BANK], start=True, stop=True))
            wait(reductions, m)
            m_reduced[i] = dve.after(reductions.tensor_reduce(half_max[:, 2 * pair + s, qt, half:half + 1],
                                                              core.ps[:, bank, :], AX_X, ALU.max))
        wait(reductions, m_reduced[len(turns) - 1])
        m = dve.after(reductions.tensor_reduce(neg_max[:, :], half_max[:, :, :, :].rearrange("p h q k -> p (h q) k"),
                                               AX_X, ALU.max, negate=True))
        wait(products, m)
        return products, reductions

    def shifts(b):
        wait(V, m_norm[b])
        m = st.dve.after(V.tensor_reduce(top_norm[:, :], norms[:, b % 2, :, :], AX_X, ALU.max))
        wait(V, m)
        m = st.dve.after(V.tensor_tensor(bound[:, :], top_norm[:, 0:1], top_norm[:, 1:2], ALU.add))
        wait(V, m)
        m = st.dve.after(V.tensor_scalar(bound_of[:, :], core.ident[:, :], bound[:, 0:1], 0.5 * HD ** -0.5,
                                         ALU.mult, ALU.mult))
        slot, bank, free = ring.take()
        wait(T, free, m)
        m = st.pe.after(T.matmul(core.ps[:, bank, 0:P], core.ones_f[:, :], bound_of[:, :], start=True, stop=True))
        wait(V, m)
        m = ring.free[slot] = st.dve.after(V.tensor_scalar(bound_of[:, :], core.ps[:, bank, 0:P], MAX_SCORE, None,
                                                           ALU.is_lt))
        wait(V, m)
        m = st.dve.after(V.tensor_reduce(lowest[:, :], bound_of[:, :], AX_X, ALU.min))
        wait(V, m)
        m = st.dve.after(V.tensor_scalar(wide[:, b:b + 1], lowest[:, :], -1.0, 1.0, ALU.mult, ALU.add))
        wait(V, m)
        m = st.dve.after(V.memset(neg_max[:, :], 0.0))
        wait(V, m)
        products, reductions = true_maxima(b)
        wait(T, m, m_stack[b], *ring.free)
        T.only_if(wide[0:1, b:b + 1], products)
        V.only_if(wide[0:1, b:b + 1], reductions)
        slot, bank, free = ring.take()
        wait(T, m, free)
        m = st.pe.after(T.transpose(core.ps[:, bank, 0:P], neg_max[:, :], core.ident[:, :]))
        wait(V, m, (max_store, max_store.count) if max_store.count else None)
        m = st.dve.after(V.tensor_copy(max_parts[:, 0, :], core.ps[:, bank, 0:P]))
        wait(V, m)
        m = ring.free[slot] = st.dve.after(V.tensor_tensor(max_parts[:, 1, :], core.ps[:, bank, 0:P],
                                                           max_parts[:, 0, :], ALU.subtract))
        wait(S, m)
        m = max_store.after(S.dma_start(dram["maxima"][b].rearrange("k r q -> r k q"), max_parts[:, :, :]), 16)
        wait(S, m)
        for s in range(2):
            first = s * STACK + QK_ROWS
            src = dram["maxima"][b].rearrange("k (r s j) q -> s k r (j q)", s=2, j=TPB)[s]
            m_max[b] = max_load.after(S.dma_start(qs[first:first + MAX_ROWS, b % 2, :, :], src), 16)

    e_free = [None, None]
    m_exp, m_pv = {}, {}
    pv_free, m_sums_free = [None], [None, None]
    m_heads_free, m_scratch = [None, None], [None]
    step_no = [0]

    def scores_and_exp(b, group, half, kt):
        n = step_no[0]
        if kt == 0 and group == 0 and half == 0:
            wait(T, m_max[b])
        marks = []
        for e in range(2):
            pair = 2 * group + e
            wait(T, e_free[e])
            for s in range(2):
                m = T.matmul(core.ps[:, E_BANKS[e] + s, :], ks[:, b % 2, s, pair, kt * P:(kt + 1) * P],
                             qs[:, b % 2, pair, half * BANK:(half + 1) * BANK], start=True, stop=True)
            m = st.pe.after(m)
            wait(A, m, m_pv.get(n - 2) if e == 0 else None)
            e_free[e] = st.act.after(A.activation(
                probs[:, n % 2, 2 * e * BANK:2 * (e + 1) * BANK],
                core.ps[:, E_BANKS[e]:E_BANKS[e] + 2, :].rearrange("p a n -> p (a n)"), ACT_FN.Exp, scale=HD ** -0.5))
        m_exp[n] = e_free[1]
        m_stack_free[b % 2] = m
        step_no[0] += 1
        return n

    def weighted_sums(n, b, group, half, kt):
        wait(T, m_exp[n], m_v[b] if kt == 0 else None, pv_free[0] if kt == 0 else None)
        for j in range(HEADS_PER_GROUP):
            m = T.matmul(core.ps[32 * j:32 * j + HD + 1, PV_BANK, :], v[:, b % 2, kt, HEADS_PER_GROUP * group + j, :],
                         probs[:, n % 2, j * BANK:(j + 1) * BANK], start=kt == 0, stop=kt == TPB - 1)
        m_pv[n] = m_v_free[b % 2] = m = st.pe.after(m)
        if kt < TPB - 1:
            return
        k = (2 * group + half) % 2
        wait(V, m, m_sums_free[k])
        m = pv_free[0] = st.dve.after(V.tensor_copy(sums[:, k, :], core.ps[:, PV_BANK, :]))
        pending.append((m, k, b, group, half))

    def divide():
        m, k, b, group, half = pending.pop(0)
        slot, bank, free = ring.take()
        wait(T, m, free)
        for i in range(TPG):
            m = T.transpose(core.ps[:, bank, i * P:(i + 1) * P], sums[:, k, i * P:(i + 1) * P], core.ident[:, :])
        m = m_sums_free[k] = st.pe.after(m)
        got = core.ps[:, bank, :].rearrange("p (t j c) -> p t j c", t=TPG, j=HEADS_PER_GROUP)
        wait(V, m)
        m = st.dve.after(V.reciprocal(inv[:, :, :], got[:, :, :, 8]))
        wait(V, m, m_heads_free[half] if group == 0 else None)
        out = heads_out[:, half, :, group * 32:(group + 1) * 32].rearrange("p t (j d) -> p t j d", d=HD)
        m = ring.free[slot] = st.dve.after(V.tensor_tensor(
            out, got[:, :, :, 0:8], inv[:, :, :, None].broadcast_to([P, TPG, HEADS_PER_GROUP, HD]), ALU.mult))
        if group == HEADS // HEADS_PER_GROUP - 1:
            m_heads_free[half], m_scratch[0], m = yield from project_group(
                core, st, ring, heads_out[:, half, :, :], m, 2 * b + half, w["proj"], w["proj_bias"],
                scratch[:, :], m_scratch[0])
            summed.append((2 * b + half, m))

    pending, summed = [], []
    for b in range(2):
        for units in (project(b), values(b) if b == 0 else ()):
            for _ in units:
                pass
        load_stacks(b)
        if b == 0:
            shifts(0)
    for b in range(BATCH):
        steps = [(group, half, kt) for group in range(HEADS // HEADS_PER_GROUP) for half in range(HALVES)
                 for kt in range(TPB)]
        units = chain(values(b + 1) if b + 1 < BATCH else (), project(b + 2) if b + 2 < BATCH else ())
        previous = None
        for i, (group, half, kt) in enumerate(steps):
            n = scores_and_exp(b, group, half, kt)
            if i == 12 and b + 1 < BATCH:
                shifts(b + 1)
            if i % 8 == 6:
                next(units, None)
            if previous is not None:
                weighted_sums(*previous)
            if pending and kt == 2:
                for _ in divide():
                    pass
            if summed and kt == 5:
                take_statistics(core, st, *summed.pop(0))
            previous = (n, b, group, half, kt)
        if b < BATCH - 1:
            for _ in units:
                pass
        weighted_sums(*previous)
        if b + 2 < BATCH:
            load_stacks(b + 2)
        if b == BATCH - 1:
            while pending:
                for _ in divide():
                    pass
            while summed:
                take_statistics(core, st, *summed.pop(0))
    st.close()


def experts(core, name, w, dram):
    nc = core.nc
    T, V, A, G, S = nc.tensor, nc.vector, nc.scalar, nc.gpsimd, nc.sync
    st = Stage(core, name)
    ring = Ring(range(8))
    m_factors = norm_factors(core, st, with_rms=True)
    xl, xr = st.sbuf("xl", [P, TILES, DIM]), st.sbuf("xr", [P, TILES, DIM])
    token_dma = st.dma_signal("token_store")
    rows = dram["tokens"].rearrange("(t p) c -> p t c", p=P)
    m_xr = []
    for g in range(GROUPS):
        tiles = slice(g * TPG, (g + 1) * TPG)
        m = normalised(core, st, g, xl[:, tiles, :], m_factors)
        wait(A, m)
        for t in range(g * TPG, (g + 1) * TPG):
            m = st.act.after(A.activation(xr[:, t, :], xl[:, t, :], ACT_FN.Copy, scale=st.scale_rms[:, t:t + 1]))
        m_xr.append(m)
        wait(S, m)
        m_tokens = token_dma.after(S.dma_start(rows[:, tiles, :], xr[:, tiles, :]), 16)

    SCORE = ring.banks[7]
    ring = Ring(range(7))
    xrt = st.sbuf("xrt", [P, 2, BANK])
    m_score = {}
    for g in range(GROUPS):
        wait(V, m_score.get(g - 2))
        wait(A, m_score.get(g - 2))
        _, m = to_channels(core, st, ring, xr[:, g * TPG:(g + 1) * TPG, :], m_xr[g], xrt[:, g % 2, :],
                           "dve" if g % 2 else "act")
        wait(T, m)
        for i in range(TPG):
            at = (g * TPG + i) * EXPERTS
            m = T.matmul(core.ps[:, SCORE, at:at + EXPERTS], xrt[:, g % 2, i * P:(i + 1) * P], w["router"],
                         start=True, stop=True)
        m_score[g] = m = st.pe.after(m)

    N8 = [P, TILES, EXPERTS]

    def wide(k, dtype=F32):
        return st.sbuf(k, N8, dtype)

    def bc(narrow):
        return narrow[:, :, None].broadcast_to(N8)

    def v_(instruction):
        m = st.dve.after(instruction)
        wait(V, m)
        return m

    score, key, scored2 = wide("score"), wide("key"), wide("scored2")
    hot = [wide("hot1"), wide("hot2")]
    top = st.sbuf("top", [P, 2, TILES])
    pick = st.sbuf("pick", [P, TILES])
    wait(V, m)
    v_(V.tensor_copy(score[:, :, :].rearrange("p t e -> p (t e)"), core.ps[:, SCORE, 0:TILES * EXPERTS]))
    rev = core.rev_expert[:, None, :].broadcast_to(N8)
    for c, src in enumerate((score, scored2)):
        v_(V.tensor_reduce(top[:, c, :], src[:, :, :], AX_X, ALU.max))
        v_(V.tensor_tensor(key[:, :, :], src[:, :, :], bc(top[:, c, :]), ALU.is_equal))
        v_(V.tensor_tensor(key[:, :, :], key[:, :, :], rev, ALU.mult))
        v_(V.tensor_reduce(pick[:, :], key[:, :, :], AX_X, ALU.max))
        v_(V.tensor_tensor(hot[c][:, :, :], rev, bc(pick[:, :]), ALU.is_equal))
        if c == 0:
            v_(V.scalar_tensor_tensor(scored2[:, :, :], hot[0][:, :, :], -3.0e38, score[:, :, :], ALU.mult, ALU.add))
    weight = st.sbuf("weight", [P, 2, TILES])
    gap = st.sbuf("gap", [P, TILES])
    m = v_(V.tensor_tensor(gap[:, :], top[:, 1, :], top[:, 0, :], ALU.subtract))
    wait(A, m)
    m_gap = st.act.after(A.activation(gap[:, :], gap[:, :], ACT_FN.Exp))

    both = wide("both", BF16)
    m = v_(V.tensor_tensor(both[:, :, :], hot[0][:, :, :], hot[1][:, :, :], ALU.add))
    flat = both[:, :, :].rearrange("p t e -> p (t e)")
    slot_a, bank_a, free_a = ring.take()
    slot_b, bank_b, free_b = ring.take()
    wait(T, m, free_a, free_b)
    T.matmul(core.ps[:, bank_a, 0:TILES * EXPERTS], core.before[:, :], flat, start=True, stop=True)
    m = st.pe.after(T.matmul(core.ps[:, bank_b, 0:TILES * EXPERTS], core.ones_bf[:, :], flat, start=True, stop=True))
    E8 = [P, EXPERTS, TILES]
    total, running, base = (st.sbuf(k, E8) for k in ("total", "running", "base"))
    per_e = {k: st.sbuf(k, [P, EXPERTS]) for k in ("count", "tiles", "first")}
    count_i = st.sbuf("count_i", [P, EXPERTS], I32)
    ends = st.sbuf("ends", [P, EXPERTS])
    zero = core.zeros
    wait(V, m)
    v_(V.tensor_copy(total[:, :, :], core.ps[:, bank_b, 0:TILES * EXPERTS].rearrange("p (t e) -> p e t", e=EXPERTS)))
    v_(V.tensor_tensor_scan(running[:, :, :].rearrange("p e t -> p (e t)"), total[:, :, :].rearrange("p e t -> p (e t)"),
                            zero[:, 0:TILES * EXPERTS], 0.0, ALU.add, ALU.add))
    v_(V.tensor_tensor(base[:, :, :], running[:, :, :], total[:, :, :], ALU.subtract))
    v_(V.tensor_tensor(per_e["count"][:, :], running[:, :, TILES - 1], base[:, :, 0], ALU.subtract))
    v_(V.tensor_scalar(per_e["count"][:, :], per_e["count"][:, :], float(P - 1), None, ALU.add))
    v_(V.tensor_copy(count_i[:, :], per_e["count"][:, :]))
    v_(V.tensor_scalar(count_i[:, :], count_i[:, :], 7, None, ALU.arith_shift_right))
    v_(V.tensor_copy(per_e["tiles"][:, :], count_i[:, :]))
    v_(V.tensor_tensor_scan(ends[:, :], per_e["tiles"][:, :], zero[:, 0:EXPERTS], 0.0, ALU.add, ALU.add))
    v_(V.tensor_tensor(per_e["first"][:, :], ends[:, :], per_e["tiles"][:, :], ALU.subtract))
    v_(V.tensor_scalar(per_e["first"][:, :], per_e["first"][:, :], float(P), None, ALU.mult))
    v_(V.tensor_tensor(per_e["first"][:, :], per_e["first"][:, :], base[:, :, 0], ALU.subtract))
    v_(V.tensor_tensor(base[:, :, :], base[:, :, :], per_e["first"][:, :, None].broadcast_to(E8), ALU.add))
    place = wide("place")
    v_(V.tensor_tensor(place[:, :, :], core.ps[:, bank_a, 0:TILES * EXPERTS].rearrange("p (t e) -> p t e", e=EXPERTS),
                       base[:, :, :].rearrange("p e t -> p t e"), ALU.add))

    T8 = [P, SLOT_TILES, EXPERTS]
    ended = st.sbuf("ended", T8)
    expert_of = st.sbuf("expert_of", [P, SLOT_TILES])
    offsets = st.sbuf("offsets", [P, 2, SLOT_TILES], I32)
    v_(V.tensor_tensor(ended[:, :, :], core.slot_tile[:, :, None].broadcast_to(T8),
                       ends[:, None, :].broadcast_to(T8), ALU.is_ge))
    v_(V.tensor_reduce(expert_of[:, :], ended[:, :, :], AX_X, ALU.add))
    v_(V.tensor_scalar(expert_of[:, :], expert_of[:, :], float(EXPERTS - 1), None, ALU.min))
    for i, stride in enumerate((2 * HIDDEN, DIM)):
        m_offsets = v_(V.tensor_scalar(offsets[:, i, :], expert_of[:, :], float(stride), None, ALU.mult))

    slot_f = st.sbuf("slot_f", [P, 2, TILES])
    slot_i, slot_t = (st.sbuf(k, [P, 2, TILES], I32) for k in ("slot_i", "slot_t"))
    row_f, tile_f = (st.sbuf(k, [P, 2, TILES]) for k in ("row_f", "tile_f"))
    for c in range(TOPK):
        v_(V.tensor_tensor(key[:, :, :], place[:, :, :], hot[c][:, :, :], ALU.mult))
        m = v_(V.tensor_reduce(slot_f[:, c, :], key[:, :, :], AX_X, ALU.add))
    v_(V.tensor_copy(slot_i[:, :, :], slot_f[:, :, :]))
    v_(V.tensor_scalar(slot_t[:, :, :], slot_i[:, :, :], 7, None, ALU.arith_shift_right))
    v_(V.tensor_copy(tile_f[:, :, :], slot_t[:, :, :]))
    v_(V.tensor_scalar(slot_i[:, :, :], slot_i[:, :, :], P - 1, None, ALU.bitwise_and))
    v_(V.tensor_copy(row_f[:, :, :], slot_i[:, :, :]))

    PART = 2 * SLOT_TILES
    row_hot = st.sbuf("row_hot", [P, 4, P], BF16)
    tile_hot = st.sbuf("tile_hot", [P, 4, PART], BF16)
    slot_l, bank_l, free_l = ring.take()
    m_l = {}
    n = 0
    for t in range(TILES):
        for c in range(TOPK):
            wait(V, m_l.get(n - 4))
            V.tensor_scalar(row_hot[:, n % 4, :], core.iota_p[:, :], row_f[:, c, t:t + 1], None, ALU.is_equal)
            V.tensor_scalar(tile_hot[:, n % 4, 0:SLOT_TILES], core.slot_tile[:, :], tile_f[:, c, t:t + 1],
                            core.lane1[:, 0:1], ALU.is_equal, ALU.mult)
            m = st.dve.after(V.tensor_scalar(tile_hot[:, n % 4, SLOT_TILES:PART], core.slot_tile[:, :],
                                             tile_f[:, c, t:t + 1], float(2 * t + c), ALU.is_equal, ALU.mult))
            wait(T, m, free_l if n == 0 else None)
            m_l[n] = st.pe.after(T.matmul(core.ps[:, bank_l, 0:PART], row_hot[:, n % 4, :], tile_hot[:, n % 4, :],
                                          start=n == 0, stop=n == TILES * TOPK - 1))
            n += 1
    listed = st.sbuf("listed", [P, 2, SLOT_TILES])
    empty = st.sbuf("empty", [P, SLOT_TILES])
    src_f, dst_f = (st.sbuf(k, [P, SLOT_TILES]) for k in ("src_f", "dst_f"))
    src_i, dst_i = (st.sbuf(k, [P, SLOT_TILES], U32) for k in ("src_i", "dst_i"))
    wait(V, m_l[n - 1])
    v_(V.tensor_copy(listed[:, :, :].rearrange("p a t -> p (a t)"), core.ps[:, bank_l, 0:PART]))
    half_i = st.sbuf("half_i", [P, SLOT_TILES], I32)
    v_(V.tensor_scalar(empty[:, :], listed[:, 0, :], 0.0, None, ALU.is_equal))
    v_(V.tensor_scalar(listed[:, 0, :], listed[:, 0, :], -1.0, 0.0, ALU.add, ALU.max))
    v_(V.tensor_copy(half_i[:, :], listed[:, 1, :]))
    v_(V.tensor_scalar(half_i[:, :], half_i[:, :], 1, None, ALU.arith_shift_right))
    v_(V.tensor_copy(src_f[:, :], half_i[:, :]))
    v_(V.scalar_tensor_tensor(src_f[:, :], src_f[:, :], float(P), listed[:, 0, :], ALU.mult, ALU.add))
    v_(V.tensor_copy(src_i[:, :], src_f[:, :]))
    v_(V.scalar_tensor_tensor(dst_f[:, :], listed[:, 1, :], float(P), listed[:, 0, :], ALU.mult, ALU.add))
    v_(V.tensor_tensor(empty[:, :], empty[:, :], core.spare_row[:, :], ALU.mult))
    v_(V.tensor_tensor(dst_f[:, :], dst_f[:, :], empty[:, :], ALU.add))
    m_lists = v_(V.tensor_copy(dst_i[:, :], dst_f[:, :]))
    wait(V, m_gap)
    v_(V.tensor_scalar(weight[:, 0, :], gap[:, :], 1.0, None, ALU.add))
    v_(V.reciprocal(weight[:, 0, :], weight[:, 0, :]))
    v_(V.tensor_scalar(weight[:, 0, :], weight[:, 0, :], 0.5, None, ALU.mult))
    v_(V.tensor_tensor(weight[:, 1, :], weight[:, 0, :], gap[:, :], ALU.mult))

    ring = Ring(())
    NG, NB = 6, 3
    gathered = st.sbuf("gathered", [P, NG, DIM])
    gt = st.sbuf("gt", [P, NB, DIM])
    silu, h = (st.sbuf(k, [P, NB, HIDDEN]) for k in ("silu", "h"))
    ht = st.sbuf("ht", [P, NB, HIDDEN])
    y = st.sbuf("y", [P, NG, DIM])
    gather_dma = [st.dma_signal(f"gather{i}") for i in range(NG)]
    scatter_dma = [st.dma_signal(f"scatter{i}") for i in range(NG)]
    XT, UP, HT, DOWN = (0, 1), (2, 3), (4, 5), (6, 7)
    m_g, m_xt, m_gt, m_up, m_silu, m_h, m_htp, m_ht, m_down, m_y = ({} for _ in range(10))
    wait(G, m_lists, m_tokens, (token_dma, token_dma.count))
    wait(T, m_offsets, m_lists, m_gap)
    wait(A, m_lists)

    def gather(j):
        wait(G, m_xt.get(j - NG))
        m_g[j] = gather_dma[j % NG].after(G.indirect_dma_start(
            out=gathered[:, j % NG, :], out_offset=None, in_=dram["tokens"],
            in_offset=bass.IndirectOffsetOnAxis(ap=src_i[:, j:j + 1], axis=0)), 16)

    def turn(j):
        wait(T, m_g[j], m_gt.get(j - 2))
        m_xt[j] = st.pe.after(T.transpose(core.ps[:, XT[j % 2], 0:P], gathered[:, j % NG, :], core.ident[:, :]))
        wait(V, m_xt[j], m_up.get(j - NB))
        m_gt[j] = st.dve.after(V.tensor_copy(gt[:, j % NB, :], core.ps[:, XT[j % 2], 0:P]))

    def up(j):
        wait(T, m_gt[j], m_h.get(j - 2), m_silu.get(j - 2))
        bank = UP[j % 2]
        m_up[j] = st.pe.after(T.matmul_by_expert(core.ps[:, bank, :], gt[:, j % NB, :], w["up"], 2 * HIDDEN,
                                                 offsets[0:1, 0, j:j + 1]))
        wait(A, m_up[j], m_h.get(j - NB))
        m_silu[j] = st.act.after(A.activation(silu[:, j % NB, :], core.ps[:, bank, HIDDEN:2 * HIDDEN], ACT_FN.Silu))
        wait(V, m_silu[j], m_htp.get(j - NB))
        m_h[j] = st.dve.after(V.tensor_tensor(h[:, j % NB, :], core.ps[:, bank, 0:HIDDEN], silu[:, j % NB, :], ALU.mult))

    def turn_hidden(j):
        wait(T, m_h[j], m_ht.get(j - 2))
        bank = HT[j % 2]
        for k in range(2):
            m = T.transpose(core.ps[:, bank, k * P:(k + 1) * P], h[:, j % NB, k * P:(k + 1) * P], core.ident[:, :])
        m_htp[j] = st.pe.after(m)
        wait(A, m_htp[j], m_down.get(j - NB))
        m_ht[j] = st.act.after(A.activation(ht[:, j % NB, :], core.ps[:, bank, 0:HIDDEN], ACT_FN.Copy))

    def down(j):
        wait(T, m_ht[j], m_y.get(j - 2))
        bank = DOWN[j % 2]
        for k in range(2):
            m = T.matmul_by_expert(core.ps[:, bank, 0:DIM], ht[:, j % NB, k * P:(k + 1) * P],
                                   w["down"][:, k * EXPERTS * DIM:(k + 1) * EXPERTS * DIM], DIM,
                                   offsets[0:1, 1, j:j + 1], start=k == 0, stop=k == 1)
        m_down[j] = st.pe.after(m)
        free = (scatter_dma[j % NG], scatter_dma[j % NG].count) if j >= NG else None
        wait(V, m_down[j], free)
        m_y[j] = st.dve.after(V.tensor_copy(y[:, j % NG, :], core.ps[:, bank, 0:DIM]))

    def scatter(j):
        wait(G, m_y[j])
        scatter_dma[j % NG].after(G.indirect_dma_start(
            out=dram["routed"], out_offset=bass.IndirectOffsetOnAxis(ap=dst_i[:, j:j + 1], axis=0),
            in_=y[:, j % NG, :], in_offset=None), 16)

    AHEAD = 4
    for j in range(min(AHEAD, SLOT_TILES)):
        gather(j)
    for j in range(SLOT_TILES + 4):
        if j < SLOT_TILES:
            turn(j)
        if 0 <= j - 1 < SLOT_TILES:
            up(j - 1)
        if 0 <= j - 2 < SLOT_TILES:
            turn_hidden(j - 2)
        if 0 <= j - 3 < SLOT_TILES:
            down(j - 3)
        if j + AHEAD < SLOT_TILES:
            gather(j + AHEAD)
        if 0 <= j - 3 < SLOT_TILES:
            scatter(j - 3)

    for s in scatter_dma:
        wait(S, (s, s.count))
    back = st.sbuf("back", [P, 2, TPG * TOPK, DIM])
    back_dma = [st.dma_signal(f"back{i}") for i in range(2)]
    routed = dram["routed"][0:TOKENS * TOPK, :].rearrange("(n p) c -> p n c", p=P)
    m_read = {}
    for g in range(GROUPS):
        wait(S, m_read.get(g - 2))
        m = back_dma[g % 2].after(S.dma_start(back[:, g % 2, :, :],
                                              routed[:, g * TPG * TOPK:(g + 1) * TPG * TOPK, :]), 16)
        wait(V, m)
        tiles = slice(g * TPG, (g + 1) * TPG)
        v_(V.scalar_tensor_tensor(core.x[:, tiles, :], xl[:, tiles, :], 0.5, core.x[:, tiles, :], ALU.mult, ALU.add))
        for c in range(TOPK):
            wc = weight[:, c, g * TPG:(g + 1) * TPG][:, :, None].broadcast_to([P, TPG, DIM])
            bk = back[:, g % 2, :, :].rearrange("p (t c) d -> p t c d", c=TOPK)[:, :, c, :]
            v_(V.tensor_tensor(bk, bk, wc, ALU.mult))
            m = v_(V.tensor_tensor(core.x[:, tiles, :], core.x[:, tiles, :], bk, ALU.add))
        m_read[g] = m
        take_statistics(core, st, g, m)
    st.close()


def load_stacks(core, signal, parts, q_stack, k_stack):
    for s in range(2):
        for row, (qp, kp) in enumerate(zip(Q_PARTS, K_PARTS)):
            for qk, dst, part in ((0, q_stack, qp), (1, k_stack, kp)):
                src = parts[qk, part].rearrange("(r s d) t -> s d r t", s=2, d=HD)[s]
                first = s * STACK + row * HD
                rows = slice(first, first + HD)
                m = signal.after(core.nc.sync.dma_start(dst[rows, s, :, :] if qk else dst[rows, :, :], src), 16)
    return m


def linear_attention(core, w, dram):
    nc = core.nc
    T, V, A, G, S = nc.tensor, nc.vector, nc.scalar, nc.gpsimd, nc.sync
    st = Stage(core, "lin")
    VW, PAD = HD + 1, P // HEADS_PER_GROUP
    HEAD_GROUPS = HEADS // HEADS_PER_GROUP
    SCORE_BANKS, OUT_BANKS, AUX_BANKS = (0, 1, 2, 3), (4, 5), (6, 7)
    NQ, NS = 3, 5
    qs = st.sbuf("q_stack", [P, 2, PAIRS, BANK], BF16)
    ks = st.sbuf("k_stack", [P, 2, 2, PAIRS, BANK], BF16)
    q = st.sbuf("q", [P, NQ, BANK])
    k = st.sbuf("k", [P, 2, BANK])
    k_tok = st.sbuf("k_tok", [P, NQ, TPG, DIM])
    v = st.sbuf("v", [P, NQ, TPG, HEADS, VW])
    xn, xt = st.sbuf("xn", [P, 2, TPG, DIM]), st.sbuf("xt", [P, 2, BANK])
    pos, e, ln, rest = (st.sbuf(n, [P, 2, BANK]) for n in ("pos", "e", "ln", "rest"))
    parts = st.sbuf("parts", [P, 2, 3, BANK], BF16)
    scores = st.sbuf("scores", [P, NS, BANK])
    state, update = st.sbuf("state", [P, 2, HEADS, VW]), st.sbuf("update", [P, 2, HEADS, VW])
    sums = st.sbuf("sums", [P, 2, BANK])
    inv = st.sbuf("inv", [P, 2, HEADS])
    heads_out = st.sbuf("heads_out", [P, 2, TPG, DIM])
    scratch = st.sbuf("proj_in", [P, BANK])
    parts_dma = [st.dma_signal(f"parts_store{i}") for i in range(2)]
    stack_dma = [st.dma_signal(f"stack_load{i}") for i in range(2)]

    m_zero_k = st.pool.after(G.memset(ks[:, :, :, :, :].rearrange("p b s r t -> p (b s r t)").bitcast(F32), 0.0))
    m_zero_q = st.pool.after(G.memset(qs[:, :, :, :].rearrange("p b r t -> p (b r t)").bitcast(F32), 0.0))
    for bank in OUT_BANKS:
        m_zero_out = st.dve.after(V.memset(core.ps[:, bank, :], 0.0))
    m_v_one = st.pool.after(G.memset(v[:, :, :, :, HD:VW], 1.0))
    wait(S, m_zero_k, m_zero_q)
    wait(V, m_v_one)
    wait(T, m_zero_out)
    m_factors = norm_factors(core, st)
    hide = st.sbuf("hide", [P, P], BF16)
    later = st.sbuf("later", [P, HEADS_PER_GROUP, P], BF16)
    V.tensor_scalar(hide[:, :], core.ident[:, :], -3.0e38, None, ALU.mult)
    m_hide = st.dve.after(V.tensor_scalar(
        later[:, :, :], core.causal[:, None, :].broadcast_to([P, HEADS_PER_GROUP, P]), -1.0, 1.0, ALU.mult, ALU.add))
    wait(T, m_hide)

    ring = Ring(AUX_BANKS)
    m_xn_read, m_xt_read, m_rest_read, m_k_read, m_parts = {}, {}, {}, {}, {}
    m_q, m_v, m_ktok, m_stack, m_scores_read = {}, {}, {}, {}, {}
    m_parts_made = {}
    m_group_end = {}

    def prepare(g):
        n = g % NQ
        m = normalised(core, st, g, xn[:, g % 2, :, :], m_factors, m_xn_read.get(g - 2))
        yield PRODUCT
        wait(A, m_xt_read.get(g - 2))
        m_xn_read[g], m_xt = to_channels(core, st, ring, xn[:, g % 2, :, :], m, xt[:, g % 2, :], "act")
        yield PRODUCT
        m_e = []
        for i in range(2):
            slot, bank, free = ring.take()
            wait(T, free, m_xt)
            m = st.pe.after(T.matmul(core.ps[:, bank, :], w["qkvo"][:, i, :], xt[:, g % 2, :], start=True, stop=True))
            bias = w["qk_bias"][:, i:i + 1]
            wait(V, m, m_rest_read.get((g - 1, i)))
            m = st.dve.after(V.tensor_scalar(pos[:, i, :], core.ps[:, bank, :], bias, 0.0, ALU.add, ALU.max))
            wait(A, m, m_rest_read.get((g - 1, i)))
            m = ring.free[slot] = st.act.after(A.activation(e[:, i, :], core.ps[:, bank, :], ACT_FN.Abs, bias=bias))
            yield OTHER
            wait(A, m)
            m_e.append(st.act.after(A.activation(e[:, i, :], e[:, i, :], ACT_FN.Exp, scale=-1.0)))
            yield PRODUCT
        slot, bank, free = ring.take()
        wait(T, free)
        for i in range(TPG):
            m = T.matmul(core.ps[:, bank, i * P:(i + 1) * P], xt[:, g % 2, i * P:(i + 1) * P], w["qkvo"][:, 2, :],
                         start=True, stop=True)
        m_xt_read[g] = m = st.pe.after(m)
        wait(V, m, m_group_end.get(g - NQ))
        m_v[g] = ring.free[slot] = st.dve.after(V.tensor_tensor(
            v[:, n, :, :, 0:HD], core.ps[:, bank, :].rearrange("p (t h d) -> p t h d", t=TPG, h=HEADS),
            w["v_bias"].rearrange("p (h d) -> p h d", h=HEADS)[:, None, :, :].broadcast_to([P, TPG, HEADS, HD]), ALU.add))
        yield OTHER
        dst = (q[:, n, :], k[:, g % 2, :])
        engine, done = (G, V), (st.pool, st.dve)
        m_rest, m_value, m_part = {}, {}, {}
        for i in (1, 0):
            wait(A, m_e[i])
            m = st.act.after(A.activation(ln[:, i, :], e[:, i, :], ACT_FN.Ln, bias=1.0))
            wait(V, m_e[i], m_parts_made.get((g - 1, i)))
            mm = st.dve.after(V.tensor_scalar(rest[:, i, :], e[:, i, :], 1.0, -1.0, ALU.add, ALU.add))
            wait(V, mm)
            mm = st.dve.after(V.tensor_tensor(rest[:, i, :], e[:, i, :], rest[:, i, :], ALU.subtract))
            m_rest[i] = (m, mm)
            yield OTHER
        for i in (1, 0):
            wait(engine[i], *m_rest[i])
            m = done[i].after(engine[i].tensor_tensor(rest[:, i, :], ln[:, i, :], rest[:, i, :], ALU.add))
            wait(engine[i], m, m_group_end.get(g - NQ) if i == 0 else m_k_read.get(g - 2))
            m_value[i] = m_rest_read[g, i] = done[i].after(
                engine[i].tensor_tensor(dst[i], pos[:, i, :], rest[:, i, :], ALU.add))
            yield OTHER
        m_q[g] = m_value[0]

        def rounded(i, part):
            if part == 0:
                wait(A, (parts_dma[i], parts_dma[i].count) if parts_dma[i].count else None)
            wait(A, m_value[i])
            m_part[i] = st.act.after(A.activation(parts[:, i, part, :], rest[:, i, :] if part else dst[i], ACT_FN.Copy))

        def less(i, part):
            wait(engine[i], m_part[i])
            m_value[i] = done[i].after(engine[i].tensor_tensor(
                rest[:, i, :], rest[:, i, :] if part else dst[i], parts[:, i, part, :], ALU.subtract))

        def stored(i):
            m_parts_made[g, i] = m_part[i]
            wait(S, m_part[i], m_stack.get(g - 2))
            m_parts[g, i] = parts_dma[i].after(S.dma_start(dram["lin_parts"][g % 2, i].rearrange("k p t -> p k t"),
                                                           parts[:, i, :, :]), 16)

        rounded(1, 0)
        yield OTHER
        less(1, 0)
        rounded(0, 0)
        yield PRODUCT
        slot, bank, free = ring.take()
        wait(T, free, m_rest_read[g, 1])
        for i in range(TPG):
            m = T.transpose(core.ps[:, bank, i * P:(i + 1) * P], k[:, g % 2, i * P:(i + 1) * P], core.ident[:, :])
        m_k_read[g] = m = st.pe.after(m)
        rounded(1, 1)
        less(0, 0)
        yield OTHER
        wait(A, m, m_group_end.get(g - NQ))
        m_ktok[g] = ring.free[slot] = st.act.after(A.activation(
            k_tok[:, n, :, :].rearrange("p t c -> p (t c)"), core.ps[:, bank, :], ACT_FN.Copy))
        less(1, 1)
        yield OTHER
        rounded(1, 2)
        stored(1)
        rounded(0, 1)
        yield OTHER
        less(0, 1)
        yield OTHER
        yield OTHER
        rounded(0, 2)
        stored(0)

    def fill_stacks(g):
        wait(S, m_parts[g, 0], m_parts[g, 1], m_scores_read.get(g - 2))
        m_stack[g] = load_stacks(core, stack_dma[g % 2], dram["lin_parts"][g % 2], qs[:, g % 2, :, :], ks[:, g % 2, :, :, :])

    m_masked, m_av, m_inter, m_state = {}, {}, {}, {}
    score_free, out_free = [None] * len(SCORE_BANKS), [None] * 2

    def own_scores(n, g, c, gr):
        bank = SCORE_BANKS[n % len(SCORE_BANKS)]
        wait(T, score_free[n % len(SCORE_BANKS)], m_stack[g] if c == gr == 0 else None)
        by_act = n % 2
        tokens = slice(c * P, (c + 1) * P)
        if by_act:
            T.matmul(core.ps[:, bank, :], hide[:, :], later[:, :, :].rearrange("p j t -> p (j t)"), start=True, stop=False)
        for j in range(HEADS_PER_GROUP):
            pair, s = divmod(gr * HEADS_PER_GROUP + j, 2)
            m = T.matmul(core.ps[:, bank, j * P:(j + 1) * P], ks[:, g % 2, s, pair, tokens], qs[:, g % 2, pair, tokens],
                         start=not by_act, stop=not by_act or j == HEADS_PER_GROUP - 1)
        m_scores_read[g] = m = st.pe.after(m)
        engine = A if by_act else V
        wait(engine, m, m_av.get(n - NS))
        if by_act:
            m = st.act.after(A.activation(scores[:, n % NS, :], core.ps[:, bank, :], ACT_FN.Relu))
        else:
            m = st.dve.after(V.tensor_tensor(
                scores[:, n % NS, :].rearrange("p (j t) -> p j t", j=HEADS_PER_GROUP),
                core.ps[:, bank, :].rearrange("p (j t) -> p j t", j=HEADS_PER_GROUP),
                core.causal[:, None, :].broadcast_to([P, HEADS_PER_GROUP, P]), ALU.mult))
        m_masked[n] = score_free[n % len(SCORE_BANKS)] = m

    def weighted_sums(n, g, c, gr):
        u = g * TPG + c
        out = core.ps[:, OUT_BANKS[u % 2], gr * P:(gr + 1) * P]
        first = u % TPB == 0
        wait(T, out_free[u % 2] if gr == 0 else None, None if first else m_state[u], m_q[g])
        if not first:
            for j in range(HEADS_PER_GROUP):
                m = T.matmul(out[PAD * j:PAD * j + VW, :], state[:, u % 2, gr * HEADS_PER_GROUP + j, :],
                             q[:, g % NQ, c * P:(c + 1) * P], start=True, stop=False)
            m_inter[u] = st.pe.after(m)
        wait(T, m_masked[n], m_v[g])
        for j in range(HEADS_PER_GROUP):
            m = T.matmul(out[PAD * j:PAD * j + VW, :], v[:, g % NQ, c, gr * HEADS_PER_GROUP + j, :],
                         scores[:, n % NS, j * P:(j + 1) * P], start=first, stop=True)
        m_av[n] = m_group_end[g] = st.pe.after(m)

    def next_state(u):
        g, c = divmod(u, TPG)
        if (u + 1) % TPB == 0:
            return
        slot, bank, free = ring.take()
        wait(T, m_ktok[g], m_v[g], free)
        m = st.pe.after(T.matmul(core.ps[:, bank, 0:HEADS * VW], k_tok[:, g % NQ, c, :],
                                 v[:, g % NQ, c, :, :].rearrange("p h c -> p (h c)"), start=True, stop=True))
        new = state[:, (u + 1) % 2, :, :]
        own = new if u % TPB == 0 else update[:, u % 2, :, :]
        wait(V, m, m_inter.get(u - 1), m_state.get(u - 1))
        m = ring.free[slot] = st.dve.after(V.tensor_tensor(
            own, core.ps[:, bank, 0:HEADS * VW].rearrange("p (h c) -> p h c", c=VW),
            core.own_block[:, :].rearrange("p (h c) -> p h c", c=VW), ALU.mult))
        if u % TPB:
            wait(G, m, m_state[u], m_inter.get(u - 1))
            m = st.pool.after(G.tensor_tensor(new, state[:, u % 2, :, :], own, ALU.add))
        m_state[u + 1] = m

    m_sums_read, m_heads_read, m_scratch, m_added = {}, {}, [None], {}

    def finish(u, n):
        g, c = divmod(u, TPG)
        wait(A, m_av[n], m_sums_read.get(u - 2))
        m = out_free[u % 2] = st.act.after(A.activation(sums[:, u % 2, :], core.ps[:, OUT_BANKS[u % 2], :], ACT_FN.Copy))
        yield PRODUCT
        slot, bank, free = ring.take()
        wait(T, m, free)
        for i in range(HEAD_GROUPS):
            mm = T.transpose(core.ps[:, bank, i * P:(i + 1) * P], sums[:, u % 2, i * P:(i + 1) * P], core.ident[:, :])
        m = m_sums_read[u] = st.pe.after(mm)
        got = core.ps[:, bank, :].rearrange("p (h c) -> p h c", c=PAD)
        wait(V, m)
        m = st.dve.after(V.reciprocal(inv[:, u % 2, :], got[:, :, HD]))
        wait(V, m, m_heads_read.get(g - 2))
        m = ring.free[slot] = st.dve.after(V.tensor_tensor(
            heads_out[:, g % 2, c, :].rearrange("p (h d) -> p h d", h=HEADS), got[:, :, 0:HD],
            inv[:, u % 2, :, None].broadcast_to([P, HEADS, HD]), ALU.mult))
        if c == TPG - 1:
            yield PRODUCT
            marks = yield from project_group(core, st, ring, heads_out[:, g % 2, :, :], m, g, w["qkvo"][:, 3, :],
                                             w["o_bias"], scratch[:, :], m_scratch[0])
            m_heads_read[g], m_scratch[0], m_added[g] = marks
            yield OTHER
            yield OTHER
            take_statistics(core, st, g, m_added[g])

    first, second = prepare(0), prepare(1)
    while 0 not in m_q:
        next(first)
    for _ in first:
        next(second)
    fill_stacks(0)
    for _ in second:
        pass
    fill_stacks(1)
    steps = [(g, c, gr) for g in range(GROUPS) for c in range(TPG) for gr in range(HEAD_GROUPS)]
    LAG = 3
    side, ahead = Side(), None
    for n in range(len(steps) + LAG):
        if n < len(steps):
            g, c, gr = steps[n]
            if c == gr == 0:
                side.finish(ahead)
                ahead = side.add(prepare(g + 2)) if g + 2 < GROUPS else None
            own_scores(n, g, c, gr)
            if gr == HEAD_GROUPS - 1:
                next_state(g * TPG + c)
        if n < LAG or gr != HEAD_GROUPS - 1:
            side.run()
        if n >= LAG:
            g, c, gr = steps[n - LAG]
            weighted_sums(n - LAG, g, c, gr)
            if gr == HEAD_GROUPS - 1:
                side.add(finish(g * TPG + c, n - LAG), first=True)
                if c == TPG - 1 and g + 2 < GROUPS:
                    fill_stacks(g + 2)
    side.finish_all()
    st.close()


def macaron_kernel(bass_nc, t, stages=6, first=0):
    nc = Program(bass_nc)
    with ExitStack() as ctx:
        core = Core(nc, ctx)
        S, V, G = nc.sync, nc.vector, nc.gpsimd
        core.x = core.sbuf("x", [P, TILES, DIM])
        core.ps = ctx.enter_context(nc.psum_tensor("ps", [P, 8, BANK], F32))
        load = Stage(core, "load")
        done = load.dma_signal("in")

        def loaded(name, shape, dtype=F32, engine=S):
            buf = core.sbuf("c_" + name, shape, dtype)
            done.after(engine.dma_start(buf[:], t[name]), 16)
            return buf

        tiles = t["x"].rearrange("(n p) c -> p n c", p=P)
        for b in range(BATCH):
            done.after(S.dma_start(core.x[:, b * TPB:(b + 1) * TPB, :], tiles[:, b * TPB:(b + 1) * TPB, :]), 16)
        core.ident = loaded("ident", [P, P])
        mix_w = loaded("mix_w", [P, 3, DIM])
        mus = loaded("mus", [P, 2])
        core.causal = loaded("causal", [P, P])
        core.own_block = loaded("own_block", [P, HEADS * (HD + 1)])
        core.head_in_4 = loaded("head_in_4", [P, HEADS_PER_GROUP])
        core.slot_tile = loaded("slot_tile", [P, SLOT_TILES])
        core.spare_row = loaded("spare_row", [P, SLOT_TILES])
        core.iota_p = loaded("iota_p", [P, P])
        core.lane1 = loaded("lane1", [P, 1])
        core.same_head = loaded("same_head", [P, P])
        core.rev_expert = loaded("rev_expert", [P, EXPERTS])
        scale = loaded("norm_scale", [P, 1])
        qkv_w = loaded("qk_w", [P, 4, DIM])
        attn_vo = loaded("attn_vo", [P, 2, DIM])
        attn_b = loaded("attn_b", [P, 4])
        attn_rows = loaded("attn_rows", [P, 2, DIM])
        lin_w = loaded("lin_w", [P, 4, DIM])
        lin_b = loaded("lin_b", [P, 2])
        lin_rows = loaded("lin_rows", [P, 2, DIM])
        before_f = loaded("before", [P, P])
        router = loaded("router", [P, EXPERTS])
        core.before = core.sbuf("before_bf", [P, P], BF16)
        core.ones_bf = core.sbuf("ones_bf", [P, P], BF16)
        core.ones_f = core.sbuf("ones_f", [P, P])
        load.pool.after(G.memset(core.ones_f[:, :], 1.0))
        core.stats = core.sbuf("stats", [P, TILES, 6])
        core.zeros = core.sbuf("zeros", [P, TILES * EXPERTS])
        load.pool.after(G.memset(core.zeros[:, :], 0.0))
        load.pool.after(G.memset(core.ones_bf[:, :], 1.0))
        wait(V, (done, done.count))
        load.dve.after(V.tensor_copy(core.before[:, :], before_f[:, :]))
        load.dve.after(V.tensor_scalar(router[:, :], router[:, :], scale[:, 0:1], None, ALU.mult))
        for g in range(GROUPS):
            take_statistics(core, load, g, None)
        load.close()

        dram = {
            "parts": nc.dram_tensor("qk_parts", [2, 2, 3, P, SEQ], BF16, kind="Internal").ap(),
            "lin_parts": nc.dram_tensor("lin_qk_parts", [2, 2, 3, P, BANK], BF16, kind="Internal").ap(),
            "maxima": nc.dram_tensor("row_maxima", [BATCH, 2, P, P], BF16, kind="Internal").ap(),
            "tokens": nc.dram_tensor("tokens", [TOKENS, DIM], F32, kind="Internal").ap(),
            "routed": nc.dram_tensor("routed", [TOKENS * TOPK + SLOTS, DIM], F32, kind="Internal").ap(),
        }
        mix = [mix_w[:, i, :] for i in range(3)]

        def expert_weights(name):
            st = Stage(core, name)
            up = core.late.enter_context(nc.sbuf_tensor(name + "_up_w", [P, EXPERTS * 2 * HIDDEN], F32))
            down = core.late.enter_context(nc.sbuf_tensor(name + "_down_w", [P, 2 * EXPERTS * DIM], F32))
            d = st.dma_signal("in")
            d.after(S.dma_start(up[:, :], t["up"]), 16)
            d.after(S.dma_start(down[:, :], t["down"]), 16)
            wait(V, (d, d.count))
            st.dve.after(V.tensor_scalar(up[:, :], up[:, :], scale[:, 0:1], None, ALU.mult))
            st.close()
            return {"router": router[:, :], "up": up[:, :], "down": down[:, :]}

        if first < 1 <= stages:
            channel_mix(core, "mix1", mix, mus[:, 0:1], mus[:, 1:2])
        if first < 2 <= stages:
            with ExitStack() as rope_ctx:
                core.cos = rope_ctx.enter_context(nc.sbuf_tensor("cos", [P, SEQ], F32))
                core.sin = rope_ctx.enter_context(nc.sbuf_tensor("sin", [P, SEQ], F32))
                core.xt_attn = rope_ctx.enter_context(nc.sbuf_tensor("xt_attn", [P, BATCH, SEQ], F32))
                rope = Stage(core, "rope")
                d = rope.dma_signal("in")
                d.after(S.dma_start(core.cos[:, :], t["cos"]), 16)
                d.after(S.dma_start(core.sin[:, :], t["sin"]), 16)
                rope.close()
                softmax_attention(core, {
                    "qk": qkv_w[:, :, :], "qk_bias": attn_b[:, :], "v": attn_vo[:, 0, :], "v_bias": attn_rows[:, 0, :],
                    "proj": attn_vo[:, 1, :], "proj_bias": attn_rows[:, 1, :]}, dram)
        if first < 3 <= stages:
            channel_mix(core, "mix2", mix, mus[:, 0:1], mus[:, 1:2])
        with ExitStack() as core.late:
            moe_w = expert_weights("moe") if stages > 3 else None
            if first < 4 <= stages:
                experts(core, "moe1", moe_w, dram)
            if first < 5 <= stages:
                linear_attention(core, {"qkvo": lin_w[:, :, :], "qk_bias": lin_b[:, :], "v_bias": lin_rows[:, 0, :],
                                        "o_bias": lin_rows[:, 1, :]}, dram)
            if first < 6 <= stages:
                experts(core, "moe2", moe_w, dram)
        out = Stage(core, "store")
        d = out.dma_signal("out")
        d.after(S.dma_start(t["out"].rearrange("(n p) c -> p n c", p=P), core.x[:, :, :]), 16)
        out.close()
        nc.build(bass_nc)


def constants():
    ar = np.arange
    inv_freq = (np.float32(1.0) / np.float32(10000.0) ** (ar(0, HD, 2, dtype=np.float32) / np.float32(HD))).astype(np.float32)
    freqs = ar(SEQ, dtype=np.float32)[:, None] * inv_freq[None, :]
    emb = np.concatenate([freqs, freqs], axis=-1).astype(np.float32)
    cos, sin = np.cos(emb), np.sin(emb)
    sign = np.where(ar(HD) % 2 == 0, -1.0, 1.0).astype(np.float32)
    head = ar(P) // HD
    own = (head[:, None] == ar(HEADS)[None, :]).astype(np.float32)
    spare = TOKENS * TOPK + ar(SLOT_TILES)[None, :] * P + ar(P)[:, None]
    f = np.float32
    return {
        "cos": np.tile(cos.T, (HEADS, 1)).astype(f), "sin": np.tile((sin * sign).T, (HEADS, 1)).astype(f),
        "ident": np.eye(P, dtype=f),
        "causal": (ar(P)[:, None] <= ar(P)[None, :]).astype(f),
        "before": (ar(P)[:, None] < ar(P)[None, :]).astype(f),
        "own_block": np.repeat(own, HD + 1, axis=1).astype(f),
        "head_in_4": (head[:, None] % HEADS_PER_GROUP == ar(HEADS_PER_GROUP)[None, :]).astype(f),
        "slot_tile": np.tile(ar(SLOT_TILES, dtype=f), (P, 1)), "spare_row": spare.astype(f),
        "iota_p": np.tile(ar(P, dtype=f), (P, 1)), "lane1": ar(1, P + 1, dtype=f)[:, None],
        "same_head": (head[:, None] == head[None, :]).astype(f),
        "rev_expert": np.tile(ar(EXPERTS, 0, -1, dtype=f), (P, 1)),
    }


def layout(i):
    c = np.ascontiguousarray
    swap = np.arange(DIM) ^ 1
    qkv, qb = np.asarray(i["L0_attn_qkv_w"]), np.asarray(i["L0_attn_qkv_b"])
    a = {k: np.asarray(v) for k, v in i.items()}

    def cols(*ws):
        return c(np.stack([w.T for w in ws], axis=1))

    def rows(*bs):
        return c(np.broadcast_to(np.stack(bs)[None], (P, len(bs), DIM)))

    q, k, v = qkv[:DIM], qkv[DIM:2 * DIM], qkv[2 * DIM:]
    bq, bk, bv = qb[:DIM], qb[DIM:2 * DIM], qb[2 * DIM:]
    down = a["L1_ffn_w_down"].transpose(2, 0, 1).reshape(2, P, EXPERTS, DIM)
    return {
        "x": c(a["L0_attn_x"].reshape(TOKENS, DIM)),
        "mix_w": cols(a["L0_ffn_W_r"], a["L0_ffn_W_k"], a["L0_ffn_W_v"]),
        "mus": c(np.stack([a["L0_ffn_mu_r"], a["L0_ffn_mu_k"]], axis=1)),
        "qk_w": cols(q, q[swap], k, k[swap]), "attn_vo": cols(v, a["L0_attn_proj_w"]),
        "attn_b": c(np.stack([bq, bq[swap], bk, bk[swap]], axis=1)), "attn_rows": rows(bv, a["L0_attn_proj_b"]),
        "lin_w": cols(a["L1_attn_Wq"], a["L1_attn_Wk"], a["L1_attn_Wv"], a["L1_attn_Wo"]),
        "lin_b": c(np.stack([a["L1_attn_bq"], a["L1_attn_bk"]], axis=1)), "lin_rows": rows(a["L1_attn_bv"], a["L1_attn_bo"]),
        "norm_scale": c(a["L1_ffn_norm_scale"][:, None]), "router": c(a["L1_ffn_w_router"].T),
        "up": c(a["L1_ffn_w_up"].transpose(2, 0, 1).reshape(P, EXPERTS * 2 * HIDDEN)),
        "down": c(down.transpose(1, 0, 2, 3).reshape(P, 2 * EXPERTS * DIM)),
    }


def kernel(**inputs):
    import concourse.bacc as _bacc
    from concourse.bass_utils import run_bass_kernel_spmd as _run

    nc = _bacc.Bacc("TRN2", target_bir_lowering=False, num_devices=1)
    arrays = {**layout(inputs), **constants()}
    t = {n: nc.dram_tensor("in_" + n, a.shape, mybir.dt.from_np(a.dtype), kind="ExternalInput").ap()
         for n, a in arrays.items()}
    t["out"] = nc.dram_tensor("out_0", (TOKENS, DIM), F32, kind="ExternalOutput").ap()
    macaron_kernel(nc, t)
    r = _run(nc, [{"in_" + n: a for n, a in arrays.items()}], core_ids=[0])
    return r.results[0]["out_0"].reshape(BATCH, SEQ, DIM)
```

```python
from contextlib import ExitStack

import numpy as np

import concourse.bass as bass
from concourse import mybir

F32 = mybir.dt.float32
BF16 = mybir.dt.bfloat16
I32 = mybir.dt.int32
U32 = mybir.dt.uint32
ALU = mybir.AluOpType
ACT_FN = mybir.ActivationFunctionType
AX_X = mybir.AxisListType.X

P = 128
BATCH, SEQ, DIM = 4, 1024, 128
TOKENS = BATCH * SEQ
TILES = TOKENS // P
TPB = SEQ // P
BANK = 512
TPG = BANK // P
GROUPS = TILES // TPG
HEADS, HD = 16, 8
EXPERTS, TOPK, HIDDEN = 8, 2, 256
LN_EPS, RMS_EPS = 1e-5, 1e-6
SLOT_TILES = TOKENS * TOPK // P + EXPERTS - 1
SLOTS = SLOT_TILES * P
EXPERT_COLS = 2 * HIDDEN + HIDDEN // P * DIM
Q_PARTS = (0, 0, 1, 1, 0, 2)
K_PARTS = (0, 1, 0, 1, 2, 0)
QK_ROWS = len(Q_PARTS) * HD
MAX_ROWS = 2
MAX_SCORE = 60.0
STACK = 64
PAIRS = HEADS // 2
HEADS_PER_GROUP = 4


class Step:

    def __init__(self, issue):
        self.issue, self.raises = issue, []

    def then_inc(self, sem, by):
        self.raises.append((sem, by))


class Queue:

    def __init__(self):
        self.steps, self.registers = [], {}

    def put(self, issue):
        self.steps.append(Step(issue))
        return self.steps[-1]

    def issue_all(self, engine):
        for step in self.steps:
            instruction = step.issue(engine)
            for sem, by in step.raises:
                instruction.then_inc(sem, by)

    def only_if(self, flag, body):
        def issue(engine):
            with engine.If(engine.value_load(flag, min_val=0, max_val=1) != 0):
                body.issue_all(engine)
        self.put(issue)

    def wait_ge(self, *a):
        return self.put(lambda e: e.wait_ge(*a))

    def dma_start(self, *a, **k):
        return self.put(lambda e: e.dma_start(*a, **k))

    def indirect_dma_start(self, *a, **k):
        return self.put(lambda e: e.indirect_dma_start(*a, **k))

    def matmul(self, *a, **k):
        return self.put(lambda e: e.matmul(*a, **k))

    def load_offset(self, key, offset):
        def issue(e):
            self.registers[key] = e.value_load(offset, min_val=0, max_val=(EXPERTS - 1) * EXPERT_COLS)
        self.put(issue)

    def matmul_by_expert(self, out, stationary, moving, width, key, start=True, stop=True):
        return self.put(lambda e: e.matmul(out, stationary, moving[:, bass.ds(self.registers[key], width)],
                                           start=start, stop=stop))

    def transpose(self, *a, **k):
        return self.put(lambda e: e.transpose(*a, **k))

    def activation(self, *a, **k):
        return self.put(lambda e: e.activation(*a, **k))

    def memset(self, *a, **k):
        return self.put(lambda e: e.memset(*a, **k))

    def tensor_copy(self, *a, **k):
        return self.put(lambda e: e.tensor_copy(*a, **k))

    def tensor_scalar(self, *a, **k):
        return self.put(lambda e: e.tensor_scalar(*a, **k))

    def tensor_tensor(self, *a, **k):
        return self.put(lambda e: e.tensor_tensor(*a, **k))

    def scalar_tensor_tensor(self, *a, **k):
        return self.put(lambda e: e.scalar_tensor_tensor(*a, **k))

    def tensor_tensor_scan(self, *a, **k):
        return self.put(lambda e: e.tensor_tensor_scan(*a, **k))

    def tensor_reduce(self, *a, **k):
        return self.put(lambda e: e.tensor_reduce(*a, **k))

    def reciprocal(self, *a, **k):
        return self.put(lambda e: e.reciprocal(*a, **k))

    def bn_stats(self, *a, **k):
        return self.put(lambda e: e.bn_stats(*a, **k))

    def bn_aggr(self, *a, **k):
        return self.put(lambda e: e.bn_aggr(*a, **k))


class Program:

    def __init__(self, nc):
        self.sbuf_tensor, self.psum_tensor = nc.sbuf_tensor, nc.psum_tensor
        self.semaphore, self.dram_tensor = nc.semaphore, nc.dram_tensor
        self.tensor, self.vector, self.scalar, self.gpsimd, self.sync = (Queue() for _ in range(5))

    def build(self, nc):
        with nc.Block() as block:
            block.tensor(self.tensor.issue_all)
            block.vector(self.vector.issue_all)
            block.scalar(self.scalar.issue_all)
            block.gpsimd(self.gpsimd.issue_all)
            block.sync(self.sync.issue_all)


class Signal:

    def __init__(self, nc, ctx, name):
        self.sem, self.count, self.name = ctx.enter_context(nc.semaphore(name)), 0, name

    def after(self, instruction, by=1):
        instruction.then_inc(self.sem, by)
        self.count += by
        return (self, self.count)


def wait(engine, *marks):
    for mark in marks:
        if mark is not None:
            engine.wait_ge(mark[0].sem, mark[1])


class Ring:

    def __init__(self, banks):
        self.banks, self.free, self.n = list(banks), [None] * len(banks), -1

    def take(self):
        self.n = (self.n + 1) % len(self.banks)
        return self.n, self.banks[self.n], self.free[self.n]

    def narrow(self, engine, other, banks):
        wait(engine, *self.free)
        wait(other, *self.free)
        self.banks, self.free, self.n = list(banks), [None] * len(banks), -1


class Stage:

    def __init__(self, core, name):
        self.core, self.nc, self.name, self.ctx = core, core.nc, name, ExitStack()
        ctx = core.ctx
        self.pe = Signal(self.nc, ctx, f"{name}_pe")
        self.dve = Signal(self.nc, ctx, f"{name}_dve")
        self.act = Signal(self.nc, ctx, f"{name}_act")
        self.pool = Signal(self.nc, ctx, f"{name}_pool")
        self.dmas = []

    def sbuf(self, name, shape, dtype=F32):
        return self.ctx.enter_context(self.nc.sbuf_tensor(f"{self.name}_{name}", shape, dtype))

    def dma_signal(self, name):
        s = Signal(self.nc, self.core.ctx, f"{self.name}_{name}")
        self.dmas.append(s)
        return s

    def close(self):
        for engine in self.core.engines:
            for s in (self.pe, self.dve, self.act, self.pool, *self.dmas):
                if s.count:
                    wait(engine, (s, s.count))
        self.ctx.close()


PRODUCT, SAME_BANK, OTHER = "uses the tensor engine", "goes on with the bank of its last piece", "uses others only"


class Side:

    def __init__(self):
        self.work = []

    def add(self, work, first=False):
        one = [work, next(work)]
        self.work.insert(0 if first else len(self.work), one)
        return one

    def piece(self, one):
        try:
            one[1] = next(one[0])
        except StopIteration:
            self.work.remove(one)

    def run(self):
        works = sorted(self.work, key=lambda one: one[1] != SAME_BANK)[:2]
        products = 0
        for one in works:
            if one[1] != OTHER:
                products += 1
                if products > 1:
                    continue
            self.piece(one)

    def finish(self, one):
        while one in self.work:
            self.piece(one)

    def finish_all(self):
        while self.work:
            self.finish(self.work[0])


class Core:

    def __init__(self, nc, ctx):
        self.nc, self.ctx = nc, ctx
        self.engines = (nc.tensor, nc.vector, nc.scalar, nc.gpsimd, nc.sync)

    def sbuf(self, name, shape, dtype=F32):
        return self.ctx.enter_context(self.nc.sbuf_tensor(name, shape, dtype))


def take_statistics(core, st, group, ready):
    wait(core.nc.vector, ready)
    for t in range(group * TPG, (group + 1) * TPG):
        m = st.dve.after(core.nc.vector.bn_stats(out=core.stats[:, t, :], in_=core.x[:, t, :]))
    wait(core.nc.vector, m)
    for t in range(group * TPG, (group + 1) * TPG):
        st.dve.after(core.nc.vector.bn_aggr(out=core.moments[:, t, :], in_=core.stats[:, t, :]))


def norm_factors(core, st, with_rms=False):
    nc = core.nc
    V = nc.vector
    var, std, fix = (st.sbuf(f"ln_{k}", [P, TILES]) for k in ("var", "std", "fix"))
    st.rstd = st.sbuf("rstd", [P, TILES])

    def chained(instruction):
        m = st.dve.after(instruction)
        wait(V, m)
        return m

    def inverse_root(m, out):
        wait(nc.scalar, m)
        m = st.act.after(nc.scalar.activation(std[:, :], var[:, :], ACT_FN.Sqrt))
        wait(V, m)
        chained(V.reciprocal(out, std[:, :]))
        chained(V.tensor_tensor(fix[:, :], var[:, :], out, ALU.mult))
        chained(V.tensor_tensor(fix[:, :], fix[:, :], out, ALU.mult))
        chained(V.tensor_scalar(fix[:, :], fix[:, :], -0.5, 1.5, ALU.mult, ALU.add))
        return chained(V.tensor_tensor(out, out, fix[:, :], ALU.mult))

    m = chained(V.tensor_scalar(var[:, :], core.moments[:, :, 1], LN_EPS, None, ALU.add))
    m = inverse_root(m, st.rstd[:, :])
    if with_rms:
        st.scale_rms = st.sbuf("rms_scale", [P, TILES])
        chained(V.tensor_tensor(var[:, :], core.moments[:, :, 1], st.rstd[:, :], ALU.mult))
        chained(V.tensor_tensor(var[:, :], var[:, :], st.rstd[:, :], ALU.mult))
        m = chained(V.tensor_scalar(var[:, :], var[:, :], RMS_EPS, None, ALU.add))
        m = inverse_root(m, st.scale_rms[:, :])
    return m


def normalised(core, st, group, out, factors_ready, free=None):
    V = core.nc.vector
    wait(V, factors_ready, free)
    for i in range(TPG):
        t = group * TPG + i
        m = st.dve.after(V.tensor_scalar(out[:, i, :], core.x[:, t, :], core.moments[:, t, 0:1], st.rstd[:, t:t + 1],
                                         ALU.subtract, ALU.mult))
    return m


def to_channels(core, st, ring, source, ready, out, engine):
    nc = core.nc
    slot, bank, free = ring.take()
    wait(nc.tensor, free, ready)
    for i in range(TPG):
        m = nc.tensor.transpose(core.ps[:, bank, i * P:(i + 1) * P], source[:, i, :], core.ident[:, :])
    m_read = m = st.pe.after(m)
    if engine == "act":
        wait(nc.scalar, m)
        ring.free[slot] = st.act.after(nc.scalar.activation(out, core.ps[:, bank, :], ACT_FN.Copy))
    else:
        wait(nc.vector, m)
        ring.free[slot] = st.dve.after(nc.vector.tensor_copy(out, core.ps[:, bank, :]))
    return m_read, ring.free[slot]


def channel_mix(core, name, w, mu_r, mu_k):
    nc = core.nc
    T, V, A, G = nc.tensor, nc.vector, nc.scalar, nc.gpsimd
    st = Stage(core, name)
    ring = Ring(range(8))
    m_factors = norm_factors(core, st)
    xt = st.sbuf("xt", [P, BATCH, 1 + SEQ])
    m_zero = st.pool.after(G.memset(xt[:, :, 0:1], 0.0))
    rest = st.sbuf("rest", [P, 2])
    mixed = st.sbuf("mixed", [P, 4, DIM])
    for i, mu in enumerate((mu_r, mu_k)):
        m = st.dve.after(V.tensor_scalar(rest[:, i:i + 1], mu, -1.0, 1.0, ALU.mult, ALU.add))
    wait(V, m)
    for i, (wt, mu) in enumerate(((w[0], mu_r), (w[1], mu_k))):
        V.tensor_scalar(mixed[:, 2 * i, :], wt, mu, None, ALU.mult)
        m_mixed = st.dve.after(V.tensor_scalar(mixed[:, 2 * i + 1, :], wt, rest[:, i:i + 1], None, ALU.mult))
    wait(T, m_zero, m_mixed)
    NB = 2
    relu, act, gate, value = (st.sbuf(k, [P, NB, BANK]) for k in ("relu", "act", "gate", "value"))
    xn = st.sbuf("xn", [P, NB, TPG, DIM])
    m_xn_read, m_added = {}, {}
    m_act, m_gate, m_value_free, m_v = {}, {}, {}, {}

    def value_and_add(g):
        slot, bank, free = ring.take()
        wait(T, free, m_act[g])
        for i in range(TPG):
            m = T.matmul(core.ps[:, bank, i * P:(i + 1) * P], act[:, g % NB, i * P:(i + 1) * P], w[2],
                         start=True, stop=True)
        m = m_v[g] = st.pe.after(m)
        wait(V, m, m_gate[g], m_value_free.get(g - NB))
        m = st.dve.after(V.scalar_tensor_tensor(value[:, g % NB, :], core.ps[:, bank, :], 0.5, gate[:, g % NB, :],
                                                ALU.mult, ALU.mult))
        ring.free[slot] = m
        wait(G, m)
        xg = core.x[:, g * TPG:(g + 1) * TPG, :].rearrange("p t c -> p (t c)")
        m_added[g] = m_value_free[g] = st.pool.after(G.tensor_tensor(xg, xg, value[:, g % NB, :], ALU.add))

    m_xt, m_xn = {}, {}

    def normalise(g):
        if g < GROUPS:
            m_xn[g] = normalised(core, st, g, xn[:, g % NB, :, :], m_factors, m_xn_read.get(g - NB))

    def turn(g):
        if g < GROUPS:
            b, at = g // 2, (g % 2) * BANK
            m_xn_read[g], m_xt[g] = to_channels(core, st, ring, xn[:, g % NB, :, :], m_xn[g],
                                                xt[:, b, 1 + at:1 + at + BANK], "act")

    normalise(0)
    normalise(1)
    turn(0)
    for g in range(GROUPS):
        b, at = g // 2, (g % 2) * BANK
        turn(g + 1)
        slot, bank, free = ring.take()
        wait(T, free, m_xt[g])
        T.matmul(core.ps[:, bank, :], mixed[:, 2, :], xt[:, b, 1 + at:1 + at + BANK], start=True, stop=False)
        m = st.pe.after(T.matmul(core.ps[:, bank, :], mixed[:, 3, :], xt[:, b, at:at + BANK], start=False, stop=True))
        wait(V, m, m_act.get(g - NB))
        m = ring.free[slot] = st.dve.after(V.tensor_scalar(relu[:, g % NB, :], core.ps[:, bank, :], 0.0, None, ALU.max))
        wait(A, m, m_v.get(g - NB))
        m_act[g] = st.act.after(A.activation(act[:, g % NB, :], relu[:, g % NB, :], ACT_FN.Square))
        slot, bank, free = ring.take()
        wait(T, free)
        for i in range(TPG):
            o = core.ps[:, bank, i * P:(i + 1) * P]
            T.matmul(o, xt[:, b, 1 + at + i * P:1 + at + (i + 1) * P], mixed[:, 0, :], start=True, stop=False)
            m = T.matmul(o, xt[:, b, at + i * P:at + (i + 1) * P], mixed[:, 1, :], start=False, stop=True)
        m = st.pe.after(m)
        wait(A, m, m_value_free.get(g - NB))
        m_gate[g] = ring.free[slot] = st.act.after(A.activation(gate[:, g % NB, :], core.ps[:, bank, :], ACT_FN.Sigmoid))
        normalise(g + 2)
        if g:
            value_and_add(g - 1)
        if g > 1:
            take_statistics(core, st, g - 2, m_added[g - 2])
    value_and_add(GROUPS - 1)
    for g in (GROUPS - 2, GROUPS - 1):
        take_statistics(core, st, g, m_added[g])
    st.close()


def project_group(core, st, ring, heads_out, ready, group, weights, bias_rows, scratch, scratch_free):
    nc = core.nc
    T, V = nc.tensor, nc.vector
    slot, bank, free = ring.take()
    wait(T, free, ready)
    for i in range(TPG):
        m = T.transpose(core.ps[:, bank, i * P:(i + 1) * P], heads_out[:, i, :], core.ident[:, :])
    m_read = m = st.pe.after(m)
    wait(V, m, scratch_free)
    m = ring.free[slot] = st.dve.after(V.tensor_copy(scratch, core.ps[:, bank, :]))
    yield PRODUCT
    slot, bank, free = ring.take()
    wait(T, free, m)
    for i in range(TPG):
        m = T.matmul(core.ps[:, bank, i * P:(i + 1) * P], scratch[:, i * P:(i + 1) * P], weights, start=True, stop=True)
    m_scratch = m = st.pe.after(m)
    xg = core.x[:, group * TPG:(group + 1) * TPG, :]
    wait(V, m)
    m = ring.free[slot] = st.dve.after(V.tensor_tensor(
        xg, xg, core.ps[:, bank, :].rearrange("p (t c) -> p t c", t=TPG), ALU.add))
    wait(nc.gpsimd, m)
    m_added = st.pool.after(nc.gpsimd.tensor_tensor(xg, xg, bias_rows[:, None, :].broadcast_to([P, TPG, DIM]), ALU.add))
    return m_read, m_scratch, m_added


def load_stacks(core, signal, parts, qk, stack):
    for s in range(2):
        for row, part in enumerate(K_PARTS if qk else Q_PARTS):
            src = parts[qk, part].rearrange("(r s d) t -> s d r t", s=2, d=HD)[s]
            rows = slice(s * STACK + row * HD, s * STACK + (row + 1) * HD)
            m = signal.after(core.nc.sync.dma_start(stack[rows, s, :, :] if qk else stack[rows, :, :], src), 16)
    return m


def softmax_attention(core, w, dram):
    nc = core.nc
    T, V, A, G, S = nc.tensor, nc.vector, nc.scalar, nc.gpsimd, nc.sync
    st = Stage(core, "attn")
    VW = HD + 1
    HALVES = SEQ // BANK
    PAUSE = 4
    LAG, NP = 2, 3
    HEAD_GROUPS = HEADS // HEADS_PER_GROUP
    SCORE_BANKS, PV_BANK, AUX_BANKS = ((0, 1), (2, 3), (4, 5)), 6, (7,)
    qs = st.sbuf("q_stack", [P, 2, PAIRS, SEQ], BF16)
    ks = st.sbuf("k_stack", [P, 2, 2, PAIRS, SEQ], BF16)
    v = st.sbuf("v", [P, 2, TPB, HEADS, VW])
    probs = st.sbuf("probs", [P, NP, HEADS_PER_GROUP * BANK])
    xn = st.sbuf("xn", [P, TPG, DIM])
    xt = st.sbuf("xt", [P, SEQ])
    t_cos, t_sin = (st.sbuf(k, [P, BANK]) for k in ("t_cos", "t_sin"))
    roped, square = (st.sbuf(k, [P, 2, BANK]) for k in ("roped", "square"))
    parts = st.sbuf("parts", [P, 2, 3, BANK], BF16)
    k_norms = st.sbuf("k_norms", [P, HALVES])
    k_top, k_of = st.sbuf("k_top", [P, 1]), st.sbuf("k_of", [P, HEADS])
    q_norm = st.sbuf("q_norm", [P, TPB, HEADS])
    upper, lower, width, neg_max = (st.sbuf(k, [P, HEADS, TPB]) for k in ("upper", "lower", "width", "neg_max"))
    lowest = st.sbuf("lowest", [P, 1])
    wide = st.sbuf("wide", [P, BATCH], I32)
    half_max = st.sbuf("half_max", [P, HEADS, TPB, HALVES])
    max_parts = st.sbuf("max_parts", [P, 2, P], BF16)
    sums = st.sbuf("sums", [P, 2, BANK])
    inv = st.sbuf("inv", [P, 2, TPG, HEADS_PER_GROUP])
    heads_out = st.sbuf("heads_out", [P, HALVES, TPG, DIM])
    scratch = st.sbuf("proj_in", [P, BANK])
    parts_dma = [st.dma_signal(f"parts_store{i}") for i in range(2)]
    stack_dma = [st.dma_signal(f"stack_load{i}") for i in range(2)]
    max_store, max_load = st.dma_signal("max_store"), st.dma_signal("max_load")

    m_v_one = st.pool.after(G.memset(v[:, :, :, :, HD:VW], 1.0))
    m_factors = norm_factors(core, st)
    wait(V, core.m_rope)

    def blank_stacks(buffer, k_by_act=False):
        ones = float(np.frombuffer(np.array([0x3F80, 0x3F80], np.uint16).tobytes(), np.float32)[0])

        def fill(rows, stacks, value):
            m = st.pool.after(G.memset(stacks[rows].rearrange("p r t -> p (r t)").bitcast(F32), value))
            wait(G, m)
            return m

        def copy(rows, stacks, source):
            out = stacks[rows].rearrange("p r t -> p (r t)").bitcast(F32).rearrange("p (n k) -> p n k", k=P // 2)
            return st.act.after(A.activation(out, source[rows, None, :].broadcast_to(out.shape), ACT_FN.Copy))

        m_q = fill(slice(0, P), qs[:, buffer, :, :], 0.0)
        for s in range(2):
            other, shift = slice((1 - s) * STACK, (2 - s) * STACK), slice(s * STACK + 32, (s + 1) * STACK)
            stacks = ks[:, buffer, s, :, :]
            if k_by_act:
                copy(other, stacks, core.zeros[:, 0:P // 2])
                m_k = copy(shift, stacks, core.ones_bf[:, :].bitcast(F32))
            else:
                fill(other, stacks, 0.0)
                m_k = fill(shift, stacks, ones)
        return m_q, m_k

    m_blank = {0: blank_stacks(0, k_by_act=True)}

    ring = Ring(range(8))
    PIECES = (slice(0, BANK // 2), slice(BANK // 2, BANK))
    own_head = core.own_block[:, :].rearrange("p (h c) -> p h c", c=HD + 1)[:, :, 0]
    m_stack_free, m_v_free = [None, None], [None, None]
    m_stack, m_v, m_max, m_xt = {}, {}, {}, {}
    m_xn_read, m_xt_read, m_squared, m_parts_stored = {}, None, [None, None], [None, None]
    m_norms = None

    def rows_in(b):
        for half in range(HALVES):
            g = HALVES * b + half
            m = normalised(core, st, g, xn[:, :, :], m_factors, m_xn_read.get(g - 1))
            yield PRODUCT
            wait(V, m_xt_read)
            m_xn_read[g], m_xt[b, half] = to_channels(core, st, ring, xn[:, :, :], m,
                                                      xt[:, half * BANK:(half + 1) * BANK], "dve")

    def project(b):
        turns = [(qk, half) for qk in range(2) for half in range(HALVES)]
        m_rotated, m_square = {}, {}

        def rotate(i):
            nonlocal m_xt_read
            qk, half = turns[i]
            cols = slice(half * BANK, (half + 1) * BANK)
            for which in range(2):
                yield PRODUCT
                slot, bank, free = ring.take()
                wait(T, free, m_xt[b, half])
                for piece in PIECES:
                    if piece.start:
                        yield SAME_BANK
                    m = m_xt_read = st.pe.after(T.matmul(core.ps[:, bank, piece], w["qk"][:, 2 * qk + which, :],
                                                         xt[:, cols][:, piece], start=True, stop=True))
                wait(V, m, m_rotated.get(i - 1))
                table, dst = ((core.cos, t_cos), (core.sin, t_sin))[which]
                m = ring.free[slot] = st.dve.after(V.scalar_tensor_tensor(
                    dst[:, :], core.ps[:, bank, :], w["qk_bias"][:, 2 * qk + which:2 * qk + which + 1],
                    table[:, cols], ALU.add, ALU.mult))
            wait(G, m)
            m_rotated[i] = st.pool.after(G.tensor_tensor(roped[:, i % 2, :], t_cos[:, :], t_sin[:, :], ALU.add))

        def split(i):
            qk, half = turns[i]
            cols = slice(half * BANK, (half + 1) * BANK)
            k = i % 2
            wait(V, m_rotated[i], m_squared[k])
            m = m_square[i] = st.dve.after(V.tensor_tensor(square[:, k, :], roped[:, k, :], roped[:, k, :], ALU.mult))
            wait(V, m, m_parts_stored[k])
            for part in range(3):
                m = st.dve.after(V.tensor_copy(parts[:, k, part, :], roped[:, k, :]))
                wait(V, m)
                if part < 2:
                    m = st.dve.after(V.tensor_tensor(roped[:, k, :], roped[:, k, :], parts[:, k, part, :], ALU.subtract))
                    wait(V, m)
            wait(S, m, m_stack.get(b - 2))
            m_parts_stored[k] = parts_dma[k].after(
                S.dma_start(dram["parts"][b % 2, qk, :, :, cols].rearrange("k p t -> p k t"), parts[:, k, :, :]), 16)

        def norms(i):
            nonlocal m_norms
            qk, half = turns[i]
            k = i % 2
            yield PRODUCT
            slot, bank, free = ring.take()
            wait(T, free, m_square[i])
            if qk:
                for piece in PIECES:
                    if piece.start:
                        yield SAME_BANK
                    m = m_squared[k] = st.pe.after(T.matmul(core.ps[:, bank, piece], core.same_head[:, :],
                                                            square[:, k, piece], start=True, stop=True))
                wait(V, m, m_norms)
                m_norms = ring.free[slot] = st.dve.after(V.tensor_reduce(k_norms[:, half:half + 1],
                                                                        core.ps[:, bank, :], AX_X, ALU.max))
                return
            for j in range(TPG):
                m = T.matmul(core.ps[:, bank, j * HEADS:(j + 1) * HEADS], square[:, k, j * P:(j + 1) * P], own_head,
                             start=True, stop=True)
            m = m_squared[k] = st.pe.after(m)
            wait(V, m)
            m_norms = ring.free[slot] = st.dve.after(V.tensor_copy(
                q_norm[:, half * TPG:(half + 1) * TPG, :].rearrange("p t h -> p (t h)"),
                core.ps[:, bank, 0:TPG * HEADS]))

        yield from rotate(0)
        for i in range(len(turns)):
            if i + 1 < len(turns):
                yield from rotate(i + 1)
            yield OTHER
            split(i)
            yield from norms(i)
            if i % HALVES == HALVES - 1:
                fill_stacks(b, turns[i][0])

    def values(b):
        nonlocal m_xt_read
        wait(V, m_v_one)
        for half in range(HALVES):
            yield PRODUCT
            slot, bank, free = ring.take()
            wait(T, free, m_xt[b, half])
            for i in range(TPG):
                if i == TPG // 2:
                    yield SAME_BANK
                at = half * BANK + i * P
                m = T.matmul(core.ps[:, bank, i * P:(i + 1) * P], xt[:, at:at + P], w["v"], start=True, stop=True)
            m_xt_read = m = st.pe.after(m)
            wait(V, m, m_v_free[b % 2])
            m_v[b] = ring.free[slot] = st.dve.after(V.tensor_tensor(
                v[:, b % 2, half * TPG:(half + 1) * TPG, :, 0:HD],
                core.ps[:, bank, :].rearrange("p (t h d) -> p t h d", t=TPG, h=HEADS),
                w["v_bias"].rearrange("p (h d) -> p h d", h=HEADS)[:, None, :, :].broadcast_to([P, TPG, HEADS, HD]),
                ALU.add))

    def fill_stacks(b, qk):
        wait(S, *m_parts_stored, m_stack_free[b % 2], *m_blank[b % 2])
        m_stack[b] = load_stacks(core, stack_dma[b % 2], dram["parts"][b % 2], qk,
                                 (ks[:, b % 2, :, :, :] if qk else qs[:, b % 2, :, :]))

    def true_maxima(b):
        pe, dve = Signal(nc, core.ctx, f"max_pe{b}"), Signal(nc, core.ctx, f"max_dve{b}")
        products, reductions = Queue(), Queue()
        turns = [(pair, qt, s, half) for pair in range(PAIRS) for qt in range(TPB) for s in range(2)
                 for half in range(HALVES)]
        m_reduced = {}
        for i, (pair, qt, s, half) in enumerate(turns):
            rows = slice(s * STACK, s * STACK + QK_ROWS)
            bank = AUX_BANKS[i % len(AUX_BANKS)]
            wait(products, m_reduced.get(i - len(AUX_BANKS)))
            m = pe.after(products.matmul(core.ps[:, bank, :], qs[rows, b % 2, pair, qt * P:(qt + 1) * P],
                                         ks[rows, b % 2, s, pair, half * BANK:(half + 1) * BANK], start=True, stop=True))
            wait(reductions, m)
            m_reduced[i] = dve.after(reductions.tensor_reduce(half_max[:, 2 * pair + s, qt, half:half + 1],
                                                              core.ps[:, bank, :], AX_X, ALU.max))
        wait(reductions, m_reduced[len(turns) - 1])
        m = dve.after(reductions.tensor_reduce(
            neg_max[:, :, :].rearrange("p h q -> p (h q)"), half_max[:, :, :, :].rearrange("p h q k -> p (h q) k"),
            AX_X, ALU.max, negate=True))
        wait(products, m)
        return products, reductions

    def chained(instruction):
        m = st.dve.after(instruction)
        wait(V, m)
        return m

    def shifts(b):
        SAMPLE = BANK // (HEADS_PER_GROUP * TPB)
        yield PRODUCT
        wait(V, m_norms)
        chained(V.tensor_reduce(k_top[:, :], k_norms[:, :], AX_X, ALU.max))
        m = chained(V.tensor_scalar(k_of[:, :], own_head, k_top[:, 0:1], 1.0 / HD, ALU.mult, ALU.mult))
        slot, bank, free = ring.take()
        wait(T, free, m)
        m = st.pe.after(T.matmul(core.ps[:, bank, 0:HEADS], core.ones_f[:, :], k_of[:, :], start=True, stop=True))
        wait(V, m)
        ring.free[slot] = chained(V.tensor_tensor(
            upper[:, :, :], core.ps[:, bank, 0:HEADS][:, :, None].broadcast_to([P, HEADS, TPB]),
            q_norm[:, :, :].rearrange("p t h -> p h t"), ALU.add))
        chained(V.tensor_scalar(upper[:, :, :], upper[:, :, :], 0.5, None, ALU.mult))
        for s, first in ((s, first) for s in range(2) for first in range(0, PAIRS, HEADS_PER_GROUP)):
            yield PRODUCT
            slot, bank, free = ring.take()
            wait(T, free, m_stack[b])
            rows = slice(s * STACK, s * STACK + QK_ROWS)
            for j in range(HEADS_PER_GROUP):
                pair = first + j
                for qt in range(TPB):
                    at = (j * TPB + qt) * SAMPLE
                    m = T.matmul(core.ps[:, bank, at:at + SAMPLE], qs[rows, b % 2, pair, qt * P:(qt + 1) * P],
                                 ks[rows, b % 2, s, pair, 0:SAMPLE], start=True, stop=True)
            m = st.pe.after(m)
            wait(V, m)
            ring.free[slot] = chained(V.tensor_reduce(
                lower[:, :, :].rearrange("p (r s) q -> p s r q", s=2)[:, s, first:first + HEADS_PER_GROUP, :],
                core.ps[:, bank, :].rearrange("p (r q k) -> p r q k", q=TPB, k=SAMPLE), AX_X, ALU.max))
        chained(V.tensor_tensor(width[:, :, :], upper[:, :, :], lower[:, :, :], ALU.subtract))
        chained(V.tensor_tensor(neg_max[:, :, :], upper[:, :, :], lower[:, :, :], ALU.add))
        chained(V.tensor_scalar(neg_max[:, :, :], neg_max[:, :, :], -0.5, None, ALU.mult))
        chained(V.tensor_scalar(width[:, :, :], width[:, :, :], 2 * MAX_SCORE * HD ** 0.5, None, ALU.is_lt))
        chained(V.tensor_reduce(lowest[:, :], width[:, :, :].rearrange("p h q -> p (h q)"), AX_X, ALU.min))
        m = chained(V.tensor_scalar(lowest[:, :], lowest[:, :], -1.0, 1.0, ALU.mult, ALU.add))
        yield PRODUCT
        slot, bank, free = ring.take()
        wait(T, free, m)
        m = st.pe.after(T.matmul(core.ps[:, bank, 0:1], core.ones_f[:, :], lowest[:, :], start=True, stop=True))
        wait(V, m)
        m = ring.free[slot] = chained(V.tensor_scalar(wide[:, b:b + 1], core.ps[:, bank, 0:1], 0.5, None, ALU.is_gt))
        yield PRODUCT
        products, reductions = true_maxima(b)
        wait(T, m, *ring.free)
        T.only_if(wide[0:1, b:b + 1], products)
        V.only_if(wide[0:1, b:b + 1], reductions)
        slot, bank, free = ring.take()
        m = st.pe.after(T.transpose(core.ps[:, bank, 0:P], neg_max[:, :, :].rearrange("p h q -> p (h q)"),
                                    core.ident[:, :]))
        wait(V, m, (max_store, max_store.count) if max_store.count else None)
        chained(V.tensor_copy(max_parts[:, 0, :], core.ps[:, bank, 0:P]))
        m = ring.free[slot] = st.dve.after(V.tensor_tensor(max_parts[:, 1, :], core.ps[:, bank, 0:P],
                                                           max_parts[:, 0, :], ALU.subtract))
        wait(S, m)
        m = max_store.after(S.dma_start(dram["maxima"][b].rearrange("k r q -> r k q"), max_parts[:, :, :]), 16)
        wait(S, m)
        for s in range(2):
            first = s * STACK + QK_ROWS
            src = dram["maxima"][b].rearrange("k (r s j) q -> s k r (j q)", s=2, j=TPB)[s]
            m_max[b] = max_load.after(S.dma_start(qs[first:first + MAX_ROWS, b % 2, :, :], src), 16)

    def prepare(b, pause):
        yield from rows_in(b)
        yield from project(b)
        yield from values(b)
        for _ in range(pause):
            yield OTHER
        yield from shifts(b)

    slot_free = [None] * len(SCORE_BANKS)
    m_exp, m_pv = {}, {}
    pv_free, m_sums_read = [None], [None, None]
    m_heads_read, m_scratch = [None, None], [None]

    def scores_and_exp(n, b, group, half, kt):
        if kt == group == half == 0:
            wait(T, m_max[b])
        for e in range(2):
            k = (2 * n + e) % len(SCORE_BANKS)
            pair = 2 * group + e
            wait(T, slot_free[k])
            for s in range(2):
                m = T.matmul(core.ps[:, SCORE_BANKS[k][s], :], ks[:, b % 2, s, pair, kt * P:(kt + 1) * P],
                             qs[:, b % 2, pair, half * BANK:(half + 1) * BANK], start=True, stop=True)
            m = m_stack_free[b % 2] = st.pe.after(m)
            wait(A, m, m_pv.get(n - NP) if e == 0 else None)
            slot_free[k] = st.act.after(A.activation(
                probs[:, n % NP, 2 * e * BANK:2 * (e + 1) * BANK],
                core.ps[:, SCORE_BANKS[k][0]:SCORE_BANKS[k][1] + 1, :].rearrange("p a n -> p (a n)"), ACT_FN.Exp,
                scale=HD ** -0.5))
        m_exp[n] = slot_free[k]

    def weighted_sums(n, b, group, half, kt):
        wait(T, m_exp[n], *((m_v[b], pv_free[0]) if kt == 0 else ()))
        for j in range(HEADS_PER_GROUP):
            m = T.matmul(core.ps[32 * j:32 * j + VW, PV_BANK, :], v[:, b % 2, kt, HEADS_PER_GROUP * group + j, :],
                         probs[:, n % NP, j * BANK:(j + 1) * BANK], start=kt == 0, stop=kt == TPB - 1)
        m_pv[n] = m_v_free[b % 2] = st.pe.after(m)
        if kt == TPB - 1:
            side.add(divide(m_pv[n], b, group, half), first=True)

    def divide(m, b, group, half):
        k = (HALVES * group + half) % 2
        wait(V, m, m_sums_read[k])
        m = pv_free[0] = st.dve.after(V.tensor_copy(sums[:, k, :], core.ps[:, PV_BANK, :]))
        yield PRODUCT
        slot, bank, free = ring.take()
        wait(T, m, free)
        for i in range(TPG):
            m = T.transpose(core.ps[:, bank, i * P:(i + 1) * P], sums[:, k, i * P:(i + 1) * P], core.ident[:, :])
        m = m_sums_read[k] = st.pe.after(m)
        got = core.ps[:, bank, :].rearrange("p (t j c) -> p t j c", t=TPG, j=HEADS_PER_GROUP)
        wait(V, m)
        m = st.dve.after(V.reciprocal(inv[:, k, :, :], got[:, :, :, HD]))
        wait(V, m, m_heads_read[half] if group == 0 else None)
        out = heads_out[:, half, :, group * 32:(group + 1) * 32].rearrange("p t (j d) -> p t j d", d=HD)
        m = ring.free[slot] = st.dve.after(V.tensor_tensor(
            out, got[:, :, :, 0:HD], inv[:, k, :, :, None].broadcast_to([P, TPG, HEADS_PER_GROUP, HD]), ALU.mult))
        if group == HEAD_GROUPS - 1:
            yield PRODUCT
            g = HALVES * b + half
            m_heads_read[half], m_scratch[0], m = yield from project_group(
                core, st, ring, heads_out[:, half, :, :], m, g, w["proj"], w["proj_bias"], scratch[:, :], m_scratch[0])
            yield OTHER
            yield OTHER
            take_statistics(core, st, g, m)

    for _ in prepare(0, 0):
        pass
    ring.narrow(T, V, AUX_BANKS)
    m_pv_zero = st.dve.after(V.memset(core.ps[:, PV_BANK, :], 0.0))
    wait(T, m_pv_zero)
    m_blank[1] = blank_stacks(1)
    side, ahead = Side(), None
    steps = [(b, group, half, kt) for b in range(BATCH) for group in range(HEAD_GROUPS) for half in range(HALVES)
             for kt in range(TPB)]
    for n in range(len(steps) + LAG):
        if n < len(steps):
            if steps[n][1:] == (0, 0, 0):
                side.finish(ahead)
                b = steps[n][0]
                ahead = side.add(prepare(b + 1, PAUSE)) if b + 1 < BATCH else None
            scores_and_exp(n, *steps[n])
        side.run()
        if n >= LAG:
            weighted_sums(n - LAG, *steps[n - LAG])
    side.finish_all()
    st.close()


def experts(core, name, w, dram, result=None):
    nc = core.nc
    T, V, A, G, S = nc.tensor, nc.vector, nc.scalar, nc.gpsimd, nc.sync
    st = Stage(core, name)
    SCORE = 7
    ring = Ring(range(SCORE))
    m_factors = norm_factors(core, st, with_rms=True)
    xl, xr = st.sbuf("xl", [P, TILES, DIM]), st.sbuf("xr", [P, TILES, DIM])
    token_dma = st.dma_signal("token_store")
    rows = dram["tokens"].rearrange("(t p) c -> p t c", p=P)
    NX = 3
    xrt = st.sbuf("xrt", [P, NX, BANK])
    m_xl, m_xrt, m_score = {}, {}, {}

    def router(g):
        wait(T, m_xrt[g])
        for i in range(TPG):
            at = (g * TPG + i) * EXPERTS
            m = T.matmul(core.ps[:, SCORE, at:at + EXPERTS], xrt[:, g % NX, i * P:(i + 1) * P], w["router"],
                         start=True, stop=True)
        m_score[g] = st.pe.after(m)

    def normalise(g):
        if g < GROUPS:
            m_xl[g] = normalised(core, st, g, xl[:, g * TPG:(g + 1) * TPG, :], m_factors)

    normalise(0)
    normalise(1)
    for g in range(GROUPS):
        tiles = slice(g * TPG, (g + 1) * TPG)
        normalise(g + 2)
        wait(A, m_xl[g])
        for t in range(g * TPG, (g + 1) * TPG):
            m = st.act.after(A.activation(xr[:, t, :], xl[:, t, :], ACT_FN.Copy, scale=st.scale_rms[:, t:t + 1]))
        wait(S, m)
        m_tokens = token_dma.after(S.dma_start(rows[:, tiles, :], xr[:, tiles, :]), 16)
        if g > 1:
            router(g - 2)
        wait(V, m_score.get(g - NX))
        _, m_xrt[g] = to_channels(core, st, ring, xr[:, tiles, :], m, xrt[:, g % NX, :], "dve")
    router(GROUPS - 2)
    router(GROUPS - 1)
    m = m_score[GROUPS - 1]

    N8, N2 = [P, TILES, EXPERTS], [P, TILES, TOPK]

    def wide(k, dtype=F32):
        return st.sbuf(k, N8, dtype)

    def bc(narrow):
        return narrow[:, :, None].broadcast_to(N8)

    def v_(instruction):
        m = st.dve.after(instruction)
        wait(V, m)
        return m

    score, key, scored2 = wide("score"), wide("key"), wide("scored2")
    hot = [wide("hot1"), wide("hot2")]
    top = st.sbuf("top", [P, 2, TILES])
    pick = st.sbuf("pick", [P, TILES])
    wait(V, m)
    v_(V.tensor_copy(score[:, :, :].rearrange("p t e -> p (t e)"), core.ps[:, SCORE, 0:TILES * EXPERTS]))
    rev = core.rev_expert[:, None, :].broadcast_to(N8)
    for c, src in enumerate((score, scored2)):
        v_(V.tensor_reduce(top[:, c, :], src[:, :, :], AX_X, ALU.max))
        v_(V.tensor_tensor(key[:, :, :], src[:, :, :], bc(top[:, c, :]), ALU.is_equal))
        v_(V.tensor_tensor(key[:, :, :], key[:, :, :], rev, ALU.mult))
        v_(V.tensor_reduce(pick[:, :], key[:, :, :], AX_X, ALU.max))
        v_(V.tensor_tensor(hot[c][:, :, :], rev, bc(pick[:, :]), ALU.is_equal))
        if c == 0:
            v_(V.scalar_tensor_tensor(scored2[:, :, :], hot[0][:, :, :], -3.0e38, score[:, :, :], ALU.mult, ALU.add))
    weight = st.sbuf("weight", N2)
    gap = st.sbuf("gap", [P, TILES])
    m = v_(V.tensor_tensor(gap[:, :], top[:, 1, :], top[:, 0, :], ALU.subtract))
    wait(A, m)
    m_gap = st.act.after(A.activation(gap[:, :], gap[:, :], ACT_FN.Exp))

    both = wide("both", BF16)
    m = v_(V.tensor_tensor(both[:, :, :], hot[0][:, :, :], hot[1][:, :, :], ALU.add))
    flat = both[:, :, :].rearrange("p t e -> p (t e)")
    slot_a, bank_a, free_a = ring.take()
    slot_b, bank_b, free_b = ring.take()
    wait(T, m, free_a, free_b)
    T.matmul(core.ps[:, bank_a, 0:TILES * EXPERTS], core.before[:, :], flat, start=True, stop=True)
    m = st.pe.after(T.matmul(core.ps[:, bank_b, 0:TILES * EXPERTS], core.ones_bf[:, :], flat, start=True, stop=True))
    E8 = [P, EXPERTS, TILES]
    total, running, base = (st.sbuf(k, E8) for k in ("total", "running", "base"))
    per_e = {k: st.sbuf(k, [P, EXPERTS]) for k in ("count", "tiles", "first")}
    count_i = st.sbuf("count_i", [P, EXPERTS], I32)
    ends = st.sbuf("ends", [P, EXPERTS])
    zero = core.zeros
    wait(V, m)
    v_(V.tensor_copy(total[:, :, :], core.ps[:, bank_b, 0:TILES * EXPERTS].rearrange("p (t e) -> p e t", e=EXPERTS)))
    v_(V.tensor_tensor_scan(running[:, :, :].rearrange("p e t -> p (e t)"), total[:, :, :].rearrange("p e t -> p (e t)"),
                            zero[:, 0:TILES * EXPERTS], 0.0, ALU.add, ALU.add))
    v_(V.tensor_tensor(base[:, :, :], running[:, :, :], total[:, :, :], ALU.subtract))
    v_(V.tensor_tensor(per_e["count"][:, :], running[:, :, TILES - 1], base[:, :, 0], ALU.subtract))
    v_(V.tensor_scalar(count_i[:, :], per_e["count"][:, :], float(P - 1), None, ALU.add))
    v_(V.tensor_scalar(count_i[:, :], count_i[:, :], 7, None, ALU.arith_shift_right))
    v_(V.tensor_copy(per_e["tiles"][:, :], count_i[:, :]))
    v_(V.tensor_tensor_scan(ends[:, :], per_e["tiles"][:, :], zero[:, 0:EXPERTS], 0.0, ALU.add, ALU.add))
    v_(V.tensor_tensor(per_e["first"][:, :], ends[:, :], per_e["tiles"][:, :], ALU.subtract))
    v_(V.tensor_scalar(per_e["first"][:, :], per_e["first"][:, :], float(P), None, ALU.mult))
    v_(V.tensor_tensor(per_e["first"][:, :], per_e["first"][:, :], base[:, :, 0], ALU.subtract))
    v_(V.tensor_tensor(base[:, :, :], base[:, :, :], per_e["first"][:, :, None].broadcast_to(E8), ALU.add))
    place = wide("place")
    v_(V.tensor_tensor(place[:, :, :], core.ps[:, bank_a, 0:TILES * EXPERTS].rearrange("p (t e) -> p t e", e=EXPERTS),
                       base[:, :, :].rearrange("p e t -> p t e"), ALU.add))

    T8 = [P, SLOT_TILES, EXPERTS]
    ended = st.sbuf("ended", T8)
    offsets = st.sbuf("offsets", [P, SLOT_TILES], I32)
    wait(G, st.dve.after(V.tensor_tensor(ended[:, :, :], core.slot_tile[:, :, None].broadcast_to(T8),
                                         ends[:, None, :].broadcast_to(T8), ALU.is_ge)))
    half = EXPERTS // 2
    while half:
        wait(G, st.pool.after(G.tensor_tensor(ended[:, :, 0:half], ended[:, :, 0:half], ended[:, :, half:2 * half],
                                              ALU.add)))
        half //= 2
    m_offsets = st.pool.after(G.tensor_scalar(offsets[:, :], ended[:, :, 0], float(EXPERTS - 1), float(EXPERT_COLS),
                                              ALU.min, ALU.mult))

    slot_f = st.sbuf("slot_f", N2)
    slot_i, slot_t = (st.sbuf(k, N2, I32) for k in ("slot_i", "slot_t"))
    row_f, tile_f = (st.sbuf(k, N2) for k in ("row_f", "tile_f"))
    for c in range(TOPK):
        v_(V.tensor_tensor(key[:, :, :], place[:, :, :], hot[c][:, :, :], ALU.mult))
        v_(V.tensor_reduce(slot_f[:, :, c], key[:, :, :], AX_X, ALU.add))
    v_(V.tensor_copy(slot_i[:, :, :], slot_f[:, :, :]))
    v_(V.tensor_scalar(slot_t[:, :, :], slot_i[:, :, :], 7, None, ALU.arith_shift_right))
    v_(V.tensor_copy(tile_f[:, :, :], slot_t[:, :, :]))
    v_(V.tensor_scalar(slot_i[:, :, :], slot_i[:, :, :], P - 1, None, ALU.bitwise_and))
    v_(V.tensor_copy(row_f[:, :, :], slot_i[:, :, :]))
    wait(V, m_gap)
    v_(V.tensor_scalar(weight[:, :, 0], gap[:, :], 1.0, None, ALU.add))
    v_(V.reciprocal(weight[:, :, 0], weight[:, :, 0]))
    v_(V.tensor_scalar(weight[:, :, 0], weight[:, :, 0], 0.5, None, ALU.mult))
    v_(V.tensor_tensor(weight[:, :, 1], weight[:, :, 0], gap[:, :], ALU.mult))

    CHUNK = 16
    row_hot = st.sbuf("row_hot", [P, 2, CHUNK, P])
    tile_hot = st.sbuf("tile_hot", [P, 2, CHUNK, SLOT_TILES])
    tile_value = st.sbuf("tile_value", [P, 2, CHUNK, 2, SLOT_TILES])
    slot_l, bank_l, free_l = ring.take()
    m_l = {}
    flat_of = [a[:, :, :].rearrange("p t c -> p (t c)") for a in (row_f, tile_f, weight)]
    CR, CT = [P, CHUNK, P], [P, CHUNK, SLOT_TILES]
    for k in range(TILES * TOPK // CHUNK):
        row_c, tile_c, weight_c = (a[:, k * CHUNK:(k + 1) * CHUNK] for a in flat_of)
        wait(V, m_l.get(k - 2))
        m_hot = st.dve.after(V.tensor_tensor(tile_hot[:, k % 2, :, :], core.slot_tile[:, None, :].broadcast_to(CT),
                                             tile_c[:, :, None].broadcast_to(CT), ALU.is_equal))
        wait(G, m_hot, m_l.get(k - 2))
        st.pool.after(G.tensor_tensor(
            tile_value[:, k % 2, :, 0, :], tile_hot[:, k % 2, :, :],
            core.number1[:, k * CHUNK:(k + 1) * CHUNK][:, :, None].broadcast_to(CT), ALU.mult))
        m_row = st.dve.after(V.tensor_tensor(row_hot[:, k % 2, :, :], core.iota_p[:, None, :].broadcast_to(CR),
                                             row_c[:, :, None].broadcast_to(CR), ALU.is_equal))
        m_weight = st.pool.after(G.tensor_tensor(tile_value[:, k % 2, :, 1, :], tile_hot[:, k % 2, :, :],
                                                 weight_c[:, :, None].broadcast_to(CT), ALU.mult))
        wait(T, m_row, m_weight, free_l if k == 0 else None)
        for i in range(CHUNK):
            n = k * CHUNK + i
            m = T.matmul(core.ps[:, bank_l, 0:2 * SLOT_TILES], row_hot[:, k % 2, i, :],
                         tile_value[:, k % 2, i, :, :].rearrange("p a t -> p (a t)"),
                         start=n == 0, stop=n == TILES * TOPK - 1)
        m_l[k] = st.pe.after(m)
    listed = st.sbuf("listed", [P, 2, SLOT_TILES])
    empty, number = (st.sbuf(k, [P, SLOT_TILES]) for k in ("empty", "number"))
    number_i, tile_i = (st.sbuf(k, [P, SLOT_TILES], I32) for k in ("number_i", "tile_i"))
    src_i, dst_i = (st.sbuf(k, [P, SLOT_TILES], U32) for k in ("src_i", "dst_i"))
    wait(V, m_l[k])
    v_(V.tensor_copy(listed[:, :, :].rearrange("p a t -> p (a t)"), core.ps[:, bank_l, 0:2 * SLOT_TILES]))
    v_(V.tensor_scalar(number[:, :], listed[:, 0, :], -1.0, 0.0, ALU.add, ALU.max))
    v_(V.tensor_copy(number_i[:, :], number[:, :]))
    v_(V.tensor_scalar(tile_i[:, :], number_i[:, :], 8, 7, ALU.arith_shift_right, ALU.logical_shift_left))
    v_(V.tensor_scalar(number_i[:, :], number_i[:, :], P - 1, None, ALU.bitwise_and))
    m_sources = v_(V.tensor_tensor(src_i[:, :], tile_i[:, :], number_i[:, :], ALU.add))
    v_(V.tensor_scalar(empty[:, :], listed[:, 0, :], 0.0, None, ALU.is_equal))
    v_(V.tensor_tensor(empty[:, :], empty[:, :], core.spare_row[:, :], ALU.mult))
    m_lists = v_(V.tensor_tensor(dst_i[:, :], number[:, :], empty[:, :], ALU.add))

    ring = Ring(())
    NG, NB = 6, 3
    gathered = st.sbuf("gathered", [P, NG, DIM])
    gt = st.sbuf("gt", [P, NB, DIM])
    silu, h = (st.sbuf(k, [P, NB, HIDDEN]) for k in ("silu", "h"))
    ht = st.sbuf("ht", [P, NB, HIDDEN])
    y = st.sbuf("y", [P, NG, DIM])
    gather_dma = [st.dma_signal(f"gather{i}") for i in range(NG)]
    scatter_dma = [st.dma_signal(f"scatter{i}") for i in range(NG)]
    XT, UP, HT, DOWN = (0, 1), (2, 3), (4, 5), (6, 7)
    m_g, m_xt, m_gt, m_up, m_silu, m_h, m_htp, m_ht, m_down, m_y = ({} for _ in range(10))
    wait(G, m_sources, m_tokens)
    wait(T, m_offsets, m_lists, m_gap, w["ready"])
    wait(A, m_lists)

    def gather(j):
        wait(G, m_xt.get(j - NG))
        m_g[j] = gather_dma[j % NG].after(G.indirect_dma_start(
            out=gathered[:, j % NG, :], out_offset=None, in_=dram["tokens"],
            in_offset=bass.IndirectOffsetOnAxis(ap=src_i[:, j:j + 1], axis=0)), 16)

    def turn(j):
        wait(T, m_g[j], m_gt.get(j - 2))
        m_xt[j] = st.pe.after(T.transpose(core.ps[:, XT[j % 2], 0:P], gathered[:, j % NG, :], core.ident[:, :]))
        wait(V, m_xt[j], m_up.get(j - NB))
        m_gt[j] = st.dve.after(V.tensor_copy(gt[:, j % NB, :], core.ps[:, XT[j % 2], 0:P]))

    def up(j):
        wait(T, m_gt[j], m_h.get(j - 2), m_silu.get(j - 2))
        bank = UP[j % 2]
        m_up[j] = st.pe.after(T.matmul_by_expert(core.ps[:, bank, :], gt[:, j % NB, :], w["all"], 2 * HIDDEN, j))
        wait(A, m_up[j], m_h.get(j - NB))
        m_silu[j] = st.act.after(A.activation(silu[:, j % NB, :], core.ps[:, bank, HIDDEN:2 * HIDDEN], ACT_FN.Silu))
        wait(V, m_silu[j], m_htp.get(j - NB))
        m_h[j] = st.dve.after(V.tensor_tensor(h[:, j % NB, :], core.ps[:, bank, 0:HIDDEN], silu[:, j % NB, :], ALU.mult))

    def turn_hidden(j):
        wait(T, m_h[j], m_ht.get(j - 2))
        bank = HT[j % 2]
        for k in range(2):
            m = T.transpose(core.ps[:, bank, k * P:(k + 1) * P], h[:, j % NB, k * P:(k + 1) * P], core.ident[:, :])
        m_htp[j] = st.pe.after(m)
        wait(A, m_htp[j], m_down.get(j - NB))
        m_ht[j] = st.act.after(A.activation(ht[:, j % NB, :], core.ps[:, bank, 0:HIDDEN], ACT_FN.Copy))

    def down(j):
        wait(T, m_ht[j], m_y.get(j - 2))
        bank = DOWN[j % 2]
        for k in range(2):
            m = T.matmul_by_expert(core.ps[:, bank, 0:DIM], ht[:, j % NB, k * P:(k + 1) * P],
                                   w["all"][:, 2 * HIDDEN + k * DIM:], DIM, j, start=k == 0, stop=k == 1)
        m_down[j] = st.pe.after(m)
        free = (scatter_dma[j % NG], scatter_dma[j % NG].count) if j >= NG else None
        wait(A, m_down[j], free)
        m_y[j] = st.act.after(A.activation(y[:, j % NG, :], core.ps[:, bank, 0:DIM], ACT_FN.Copy,
                                           scale=listed[:, 1, j:j + 1]))

    def scatter(j):
        wait(G, m_y[j])
        scatter_dma[j % NG].after(G.indirect_dma_start(
            out=dram["routed"], out_offset=bass.IndirectOffsetOnAxis(ap=dst_i[:, j:j + 1], axis=0),
            in_=y[:, j % NG, :], in_offset=None), 16)

    AHEAD = 4
    for j in range(min(AHEAD, SLOT_TILES)):
        gather(j)
    m_half = {}
    wait(G, m_lists)
    for j in range(SLOT_TILES + 4):
        if j < SLOT_TILES:
            T.load_offset(j, offsets[0:1, j:j + 1])
            turn(j)
        if 0 <= j - 1 < SLOT_TILES:
            up(j - 1)
        if 0 <= j - 2 < SLOT_TILES:
            turn_hidden(j - 2)
        if 0 <= j - 3 < SLOT_TILES:
            down(j - 3)
        if j + AHEAD < SLOT_TILES:
            gather(j + AHEAD)
        if 0 <= j - 3 < SLOT_TILES:
            scatter(j - 3)
        if j % 8 == 7 and j // 8 < GROUPS:
            g = j // 8
            tiles = slice(g * TPG, (g + 1) * TPG)
            m_half[g] = st.dve.after(V.scalar_tensor_tensor(core.x[:, tiles, :], xl[:, tiles, :], 0.5,
                                                            core.x[:, tiles, :], ALU.mult, ALU.add))

    for s in scatter_dma:
        wait(S, (s, s.count))
    NK = 4
    back = st.sbuf("back", [P, NK, TPG * TOPK, DIM])
    back_dma = [st.dma_signal(f"back{i}") for i in range(NK)]
    routed = dram["routed"][0:TOKENS * TOPK, :].rearrange("(n p) c -> p n c", p=P)
    m_back, m_read = {}, {}
    result_dma = st.dma_signal("result")
    for g in range(GROUPS):
        wait(S, m_read.get(g - NK))
        m_back[g] = back_dma[g % NK].after(S.dma_start(back[:, g % NK, :, :],
                                                       routed[:, g * TPG * TOPK:(g + 1) * TPG * TOPK, :]), 16)
        bk = back[:, g % NK, :, :].rearrange("p (t c) d -> p t c d", c=TOPK)
        xg = core.x[:, g * TPG:(g + 1) * TPG, :]
        wait(V, m_back[g], m_half[g])
        v_(V.tensor_tensor(xg, xg, bk[:, :, 0, :], ALU.add))
        m_read[g] = v_(V.tensor_tensor(xg, xg, bk[:, :, 1, :], ALU.add))
        if result is None:
            take_statistics(core, st, g, None)
        else:
            wait(A, m_read[g])
            result_dma.after(A.dma_start(result[:, g * TPG:(g + 1) * TPG, :], xg), 16)
    st.close()


def linear_attention(core, w, dram):
    nc = core.nc
    T, V, A, G, S = nc.tensor, nc.vector, nc.scalar, nc.gpsimd, nc.sync
    st = Stage(core, "lin")
    VW, PAD = HD + 1, P // HEADS_PER_GROUP
    HEAD_GROUPS = HEADS // HEADS_PER_GROUP
    SCORE_BANKS, OUT_BANKS, AUX_BANKS = (0, 1, 2, 3), (4, 5), (6, 7)
    NQ, NS = 3, 5
    qs = st.sbuf("q_stack", [P, NQ, PAIRS, BANK], BF16)
    ks = st.sbuf("k_stack", [P, NQ, 2, PAIRS, BANK], BF16)
    q = st.sbuf("q", [P, NQ, BANK])
    k = st.sbuf("k", [P, 2, BANK])
    k_tok = st.sbuf("k_tok", [P, NQ, TPG, DIM])
    v = st.sbuf("v", [P, NQ, TPG, HEADS, VW])
    xn, xt = st.sbuf("xn", [P, 2, TPG, DIM]), st.sbuf("xt", [P, 2, BANK])
    z, e, ln, rest = (st.sbuf(n, [P, 2, BANK]) for n in ("z", "e", "ln", "rest"))
    parts = st.sbuf("parts", [P, 2, 3, BANK], BF16)
    scores = st.sbuf("scores", [P, NS, BANK])
    state, update = st.sbuf("state", [P, 2, HEADS, VW]), st.sbuf("update", [P, 2, HEADS, VW])
    sums = st.sbuf("sums", [P, 2, BANK])
    inv = st.sbuf("inv", [P, 2, HEADS])
    heads_out = st.sbuf("heads_out", [P, 2, TPG, DIM])
    scratch = st.sbuf("proj_in", [P, BANK])
    parts_dma = [st.dma_signal(f"parts_store{i}") for i in range(2)]
    stack_dma = [st.dma_signal(f"stack_load{i}") for i in range(NQ)]

    m_v_one = st.pool.after(G.memset(v[:, :, :, :, HD:VW], 1.0))
    def blank_stacks(n):
        G.memset(ks[:, n, :, :, :].rearrange("p s r t -> p (s r t)").bitcast(F32), 0.0)
        return st.pool.after(G.memset(qs[:, n, :, :].rearrange("p r t -> p (r t)").bitcast(F32), 0.0))

    m_blank = {0: blank_stacks(0)}
    for bank in OUT_BANKS:
        m_zero_out = st.dve.after(V.memset(core.ps[:, bank, :], 0.0))
    wait(T, m_zero_out)
    m_factors = norm_factors(core, st)
    hide = st.sbuf("hide", [P, P], BF16)
    later = st.sbuf("later", [P, HEADS_PER_GROUP, P], BF16)
    V.tensor_scalar(hide[:, :], core.ident[:, :], -3.0e38, None, ALU.mult)
    m_hide = st.dve.after(V.tensor_scalar(
        later[:, :, :], core.causal[:, None, :].broadcast_to([P, HEADS_PER_GROUP, P]), -1.0, 1.0, ALU.mult, ALU.add))
    wait(T, m_hide)

    ring = Ring(AUX_BANKS)
    m_xn_read, m_xt_read, m_rest_read, m_k_read, m_parts = {}, {}, {}, {}, {}
    m_q, m_v, m_ktok, m_stack = {}, {}, {}, {}
    m_parts_made = {}
    m_group_scored = {}
    m_group_end = {}

    def prepare(g):
        n = g % NQ
        m = normalised(core, st, g, xn[:, g % 2, :, :], m_factors, m_xn_read.get(g - 2))
        yield PRODUCT
        wait(A, m_xt_read.get(g - 2))
        m_xn_read[g], m_xt = to_channels(core, st, ring, xn[:, g % 2, :, :], m, xt[:, g % 2, :], "act")
        yield PRODUCT
        m_e = []
        for i in range(2):
            slot, bank, free = ring.take()
            wait(T, free, m_xt)
            m = st.pe.after(T.matmul(core.ps[:, bank, :], w["qkvo"][:, i, :], xt[:, g % 2, :], start=True, stop=True))
            bias = w["qk_bias"][:, i:i + 1]
            wait(V, m, m_rest_read.get((g - 1, i)))
            m = ring.free[slot] = st.dve.after(V.tensor_scalar(z[:, i, :], core.ps[:, bank, :], bias, None, ALU.add))
            wait(A, m)
            m = st.act.after(A.activation(e[:, i, :], z[:, i, :], ACT_FN.Abs))
            yield OTHER
            wait(A, m)
            m_e.append(st.act.after(A.activation(e[:, i, :], e[:, i, :], ACT_FN.Exp, scale=-1.0)))
            yield PRODUCT
        slot, bank, free = ring.take()
        wait(T, free)
        for i in range(TPG):
            m = T.matmul(core.ps[:, bank, i * P:(i + 1) * P], xt[:, g % 2, i * P:(i + 1) * P], w["qkvo"][:, 2, :],
                         start=True, stop=True)
        m_xt_read[g] = m = st.pe.after(m)
        wait(V, m, m_v_one, m_group_end.get(g - NQ))
        m_v[g] = ring.free[slot] = st.dve.after(V.tensor_tensor(
            v[:, n, :, :, 0:HD], core.ps[:, bank, :].rearrange("p (t h d) -> p t h d", t=TPG, h=HEADS),
            w["v_bias"].rearrange("p (h d) -> p h d", h=HEADS)[:, None, :, :].broadcast_to([P, TPG, HEADS, HD]), ALU.add))
        yield OTHER
        dst = (q[:, n, :], k[:, g % 2, :])
        engine, done = (G, V), (st.pool, st.dve)
        m_rest, m_value, m_part = {}, {}, {}
        for i in (1, 0):
            wait(A, m_e[i])
            m = st.act.after(A.activation(ln[:, i, :], e[:, i, :], ACT_FN.Ln, bias=1.0))
            wait(V, m_e[i], m_parts_made.get((g - 1, i)))
            mm = st.dve.after(V.tensor_scalar(rest[:, i, :], e[:, i, :], 1.0, -1.0, ALU.add, ALU.add))
            wait(V, mm)
            mm = st.dve.after(V.tensor_tensor(rest[:, i, :], e[:, i, :], rest[:, i, :], ALU.subtract))
            m_rest[i] = (m, mm)
            yield OTHER
        for i in (1, 0):
            wait(engine[i], *m_rest[i])
            m = done[i].after(engine[i].tensor_tensor(rest[:, i, :], ln[:, i, :], rest[:, i, :], ALU.add))
            wait(V, m, m_group_end.get(g - NQ) if i == 0 else m_k_read.get(g - 2))
            m_value[i] = m_rest_read[g, i] = st.dve.after(V.scalar_tensor_tensor(
                dst[i], z[:, i, :], 0.0, rest[:, i, :], ALU.max, ALU.add))
            yield OTHER
        m_q[g] = m_value[0]

        def rounded(i, part):
            if part == 0:
                wait(A, (parts_dma[i], parts_dma[i].count) if parts_dma[i].count else None)
            wait(A, m_value[i])
            m_part[i] = st.act.after(A.activation(parts[:, i, part, :], rest[:, i, :] if part else dst[i], ACT_FN.Copy))

        def less(i, part):
            wait(engine[i], m_part[i], m_rest_read[g, i])
            m_value[i] = done[i].after(engine[i].tensor_tensor(
                rest[:, i, :], rest[:, i, :] if part else dst[i], parts[:, i, part, :], ALU.subtract))

        def stored(i):
            m_parts_made[g, i] = m_part[i]
            wait(S, m_part[i], m_stack.get(g - NQ))
            m_parts[g, i] = parts_dma[i].after(S.dma_start(dram["lin_parts"][n, i].rearrange("k p t -> p k t"),
                                                           parts[:, i, :, :]), 16)

        rounded(1, 0)
        yield OTHER
        less(1, 0)
        rounded(0, 0)
        yield PRODUCT
        slot, bank, free = ring.take()
        wait(T, free, m_rest_read[g, 1])
        for i in range(TPG):
            m = T.transpose(core.ps[:, bank, i * P:(i + 1) * P], k[:, g % 2, i * P:(i + 1) * P], core.ident[:, :])
        m_k_read[g] = m = st.pe.after(m)
        rounded(1, 1)
        less(0, 0)
        yield OTHER
        wait(A, m, m_group_end.get(g - NQ))
        m_ktok[g] = ring.free[slot] = st.act.after(A.activation(
            k_tok[:, n, :, :].rearrange("p t c -> p (t c)"), core.ps[:, bank, :], ACT_FN.Copy))
        less(1, 1)
        yield OTHER
        rounded(1, 2)
        stored(1)
        rounded(0, 1)
        yield OTHER
        less(0, 1)
        yield OTHER
        yield OTHER
        rounded(0, 2)
        stored(0)
        fill_stacks(g)

    def fill_stacks(g):
        wait(S, m_parts[g, 0], m_parts[g, 1], m_group_scored.get(g - NQ), m_blank[g % NQ])
        n = g % NQ
        for qk, stack in ((0, qs[:, n, :, :]), (1, ks[:, n, :, :, :])):
            m_stack[g] = load_stacks(core, stack_dma[n], dram["lin_parts"][n], qk, stack)

    m_masked, m_av, m_inter, m_state = {}, {}, {}, {}
    score_free, out_free = [None] * len(SCORE_BANKS), [None] * 2

    def own_scores(n, g, c, gr):
        bank = SCORE_BANKS[n % len(SCORE_BANKS)]
        wait(T, score_free[n % len(SCORE_BANKS)], m_stack[g] if c == gr == 0 else None)
        by_act = n % 2
        tokens = slice(c * P, (c + 1) * P)
        if by_act:
            T.matmul(core.ps[:, bank, :], hide[:, :], later[:, :, :].rearrange("p j t -> p (j t)"), start=True, stop=False)
        for j in range(HEADS_PER_GROUP):
            pair, s = divmod(gr * HEADS_PER_GROUP + j, 2)
            m = T.matmul(core.ps[:, bank, j * P:(j + 1) * P], ks[:, g % NQ, s, pair, tokens], qs[:, g % NQ, pair, tokens],
                         start=not by_act, stop=not by_act or j == HEADS_PER_GROUP - 1)
        m = st.pe.after(m)
        if c == TPG - 1 and gr == HEAD_GROUPS - 1:
            m_group_scored[g] = m
        engine = A if by_act else V
        wait(engine, m, m_av.get(n - NS))
        if by_act:
            m = st.act.after(A.activation(scores[:, n % NS, :], core.ps[:, bank, :], ACT_FN.Relu))
        else:
            m = st.dve.after(V.tensor_tensor(
                scores[:, n % NS, :].rearrange("p (j t) -> p j t", j=HEADS_PER_GROUP),
                core.ps[:, bank, :].rearrange("p (j t) -> p j t", j=HEADS_PER_GROUP),
                core.causal[:, None, :].broadcast_to([P, HEADS_PER_GROUP, P]), ALU.mult))
        m_masked[n] = score_free[n % len(SCORE_BANKS)] = m

    def weighted_sums(n, g, c, gr):
        u = g * TPG + c
        out = core.ps[:, OUT_BANKS[u % 2], gr * P:(gr + 1) * P]
        first = u % TPB == 0
        wait(T, out_free[u % 2] if gr == 0 else None, None if first else m_state[u], m_q[g])
        if not first:
            for j in range(HEADS_PER_GROUP):
                m = T.matmul(out[PAD * j:PAD * j + VW, :], state[:, u % 2, gr * HEADS_PER_GROUP + j, :],
                             q[:, g % NQ, c * P:(c + 1) * P], start=True, stop=False)
            m_inter[u] = st.pe.after(m)
        wait(T, m_masked[n], m_v[g])
        for j in range(HEADS_PER_GROUP):
            m = T.matmul(out[PAD * j:PAD * j + VW, :], v[:, g % NQ, c, gr * HEADS_PER_GROUP + j, :],
                         scores[:, n % NS, j * P:(j + 1) * P], start=first, stop=True)
        m_av[n] = m_group_end[g] = st.pe.after(m)

    def next_state(u):
        g, c = divmod(u, TPG)
        if (u + 1) % TPB == 0:
            return
        slot, bank, free = ring.take()
        wait(T, m_ktok[g], m_v[g], free)
        m = st.pe.after(T.matmul(core.ps[:, bank, 0:HEADS * VW], k_tok[:, g % NQ, c, :],
                                 v[:, g % NQ, c, :, :].rearrange("p h c -> p (h c)"), start=True, stop=True))
        new = state[:, (u + 1) % 2, :, :]
        own = new if u % TPB == 0 else update[:, u % 2, :, :]
        wait(V, m, m_inter.get(u - 1), m_state.get(u - 1))
        m = ring.free[slot] = st.dve.after(V.tensor_tensor(
            own, core.ps[:, bank, 0:HEADS * VW].rearrange("p (h c) -> p h c", c=VW),
            core.own_block[:, :].rearrange("p (h c) -> p h c", c=VW), ALU.mult))
        if u % TPB:
            wait(G, m, m_state[u], m_inter.get(u - 1))
            m = st.pool.after(G.tensor_tensor(new, state[:, u % 2, :, :], own, ALU.add))
        m_state[u + 1] = m

    m_sums_read, m_heads_read, m_scratch, m_added = {}, {}, [None], {}

    def finish(u, n):
        g, c = divmod(u, TPG)
        wait(V, m_av[n], m_sums_read.get(u - 2))
        m = out_free[u % 2] = st.dve.after(V.tensor_copy(sums[:, u % 2, :], core.ps[:, OUT_BANKS[u % 2], :]))
        yield PRODUCT
        slot, bank, free = ring.take()
        wait(T, m, free)
        for i in range(HEAD_GROUPS):
            mm = T.transpose(core.ps[:, bank, i * P:(i + 1) * P], sums[:, u % 2, i * P:(i + 1) * P], core.ident[:, :])
        m = m_sums_read[u] = st.pe.after(mm)
        got = core.ps[:, bank, :].rearrange("p (h c) -> p h c", c=PAD)
        wait(V, m)
        m = st.dve.after(V.reciprocal(inv[:, u % 2, :], got[:, :, HD]))
        wait(V, m, m_heads_read.get(g - 2))
        m = ring.free[slot] = st.dve.after(V.tensor_tensor(
            heads_out[:, g % 2, c, :].rearrange("p (h d) -> p h d", h=HEADS), got[:, :, 0:HD],
            inv[:, u % 2, :, None].broadcast_to([P, HEADS, HD]), ALU.mult))
        if c == TPG - 1:
            yield PRODUCT
            marks = yield from project_group(core, st, ring, heads_out[:, g % 2, :, :], m, g, w["qkvo"][:, 3, :],
                                             w["o_bias"], scratch[:, :], m_scratch[0])
            m_heads_read[g], m_scratch[0], m_added[g] = marks
            yield OTHER
            yield OTHER
            take_statistics(core, st, g, m_added[g])

    first, second = prepare(0), prepare(1)
    while 0 not in m_q:
        next(first)
    for _ in first:
        next(second)
    for n in range(1, NQ):
        m_blank[n] = blank_stacks(n)
    for _ in second:
        pass
    steps = [(g, c, gr) for g in range(GROUPS) for c in range(TPG) for gr in range(HEAD_GROUPS)]
    LAG, START = 3, 1
    side, ahead = Side(), None
    for n in range(len(steps) + LAG):
        if n < len(steps):
            g, c, gr = steps[n]
            if (c, gr) == (START, 0):
                side.finish(ahead)
                ahead = side.add(prepare(g + 2)) if g + 2 < GROUPS else None
            own_scores(n, g, c, gr)
            if gr == HEAD_GROUPS - 1:
                next_state(g * TPG + c)
        side.run()
        if n >= LAG:
            g, c, gr = steps[n - LAG]
            weighted_sums(n - LAG, g, c, gr)
            if gr == HEAD_GROUPS - 1:
                side.add(finish(g * TPG + c, n - LAG), first=True)
    side.finish_all()
    st.close()


def macaron_kernel(bass_nc, t):
    nc = Program(bass_nc)
    with ExitStack() as ctx:
        core = Core(nc, ctx)
        S, V, G = nc.sync, nc.vector, nc.gpsimd
        core.x = core.sbuf("x", [P, TILES, DIM])
        core.ps = ctx.enter_context(nc.psum_tensor("ps", [P, 8, BANK], F32))
        load = Stage(core, "load")
        done = load.dma_signal("in")

        def loaded(name, shape, dtype=F32):
            buf = core.sbuf("c_" + name, shape, dtype)
            done.after(nc.scalar.dma_start(buf[:], t[name]), 16)
            return buf

        tiles = t["x"].rearrange("(n p) c -> p n c", p=P)
        m_x = []
        for g in range(GROUPS):
            at = slice(g * TPG, (g + 1) * TPG)
            m_x.append(load.dma_signal(f"x{g}").after(S.dma_start(core.x[:, at, :], tiles[:, at, :]), 16))
        core.ident = loaded("ident", [P, P])
        mix_w = loaded("mix_w", [P, 3, DIM])
        mus = loaded("mus", [P, 2])
        core.causal = loaded("causal", [P, P])
        core.own_block = loaded("own_block", [P, HEADS * (HD + 1)])
        core.slot_tile = loaded("slot_tile", [P, SLOT_TILES])
        core.spare_row = loaded("spare_row", [P, SLOT_TILES])
        core.iota_p = loaded("iota_p", [P, P])
        core.same_head = loaded("same_head", [P, P])
        core.rev_expert = loaded("rev_expert", [P, EXPERTS])
        core.number1 = loaded("number1", [P, TILES * TOPK])
        scale = loaded("norm_scale", [P, 1])
        qkv_w = loaded("qk_w", [P, 4, DIM])
        attn_vo = loaded("attn_vo", [P, 2, DIM])
        attn_b = loaded("attn_b", [P, 4])
        attn_rows = loaded("attn_rows", [P, 2, DIM])
        lin_w = loaded("lin_w", [P, 4, DIM])
        lin_b = loaded("lin_b", [P, 2])
        lin_rows = loaded("lin_rows", [P, 2, DIM])
        before_f = loaded("before", [P, P])
        router = loaded("router", [P, EXPERTS])
        core.before = core.sbuf("before_bf", [P, P], BF16)
        core.ones_bf = core.sbuf("ones_bf", [P, P], BF16)
        core.ones_f = core.sbuf("ones_f", [P, P])
        load.pool.after(G.memset(core.ones_f[:, :], 1.0))
        core.stats = core.sbuf("stats", [P, TILES, 6])
        core.moments = core.sbuf("moments", [P, TILES, 2])
        core.zeros = core.sbuf("zeros", [P, TILES * EXPERTS])
        load.pool.after(G.memset(core.zeros[:, :], 0.0))
        load.pool.after(G.memset(core.ones_bf[:, :], 1.0))
        for g in range(GROUPS):
            take_statistics(core, load, g, m_x[g])
        wait(V, (done, done.count))
        load.dve.after(V.tensor_copy(core.before[:, :], before_f[:, :]))
        load.dve.after(V.tensor_scalar(router[:, :], router[:, :], scale[:, 0:1], None, ALU.mult))
        load.close()

        dram = {
            "parts": nc.dram_tensor("qk_parts", [2, 2, 3, P, SEQ], BF16, kind="Internal").ap(),
            "lin_parts": nc.dram_tensor("lin_qk_parts", [3, 2, 3, P, BANK], BF16, kind="Internal").ap(),
            "maxima": nc.dram_tensor("row_maxima", [BATCH, 2, P, P], BF16, kind="Internal").ap(),
            "tokens": nc.dram_tensor("tokens", [TOKENS, DIM], F32, kind="Internal").ap(),
            "routed": nc.dram_tensor("routed", [TOKENS * TOPK + SLOTS, DIM], F32, kind="Internal").ap(),
        }
        mix = [mix_w[:, i, :] for i in range(3)]

        with ExitStack() as rope_ctx:
            core.cos = rope_ctx.enter_context(nc.sbuf_tensor("cos", [P, SEQ], F32))
            core.sin = rope_ctx.enter_context(nc.sbuf_tensor("sin", [P, SEQ], F32))
            rope = Signal(nc, ctx, "rope_in")
            rope.after(S.dma_start(core.cos[:, :], t["cos"]), 16)
            core.m_rope = rope.after(S.dma_start(core.sin[:, :], t["sin"]), 16)
            channel_mix(core, "mix1", mix, mus[:, 0:1], mus[:, 1:2])
            softmax_attention(core, {
                "qk": qkv_w[:, :, :], "qk_bias": attn_b[:, :], "v": attn_vo[:, 0, :], "v_bias": attn_rows[:, 0, :],
                "proj": attn_vo[:, 1, :], "proj_bias": attn_rows[:, 1, :]}, dram)
        with ExitStack() as late:
            expert_w = late.enter_context(nc.sbuf_tensor("expert_w", [P, EXPERTS, EXPERT_COLS], F32))
            expert_in, expert_ready = Signal(nc, ctx, "expert_in"), Signal(nc, ctx, "expert_ready")
            wait(S, core.m_rope)
            m = expert_in.after(S.dma_start(expert_w[:, :, :], t["expert_w"]), 16)
            channel_mix(core, "mix2", mix, mus[:, 0:1], mus[:, 1:2])
            wait(G, m)
            m = expert_ready.after(G.tensor_scalar(expert_w[:, :, 0:2 * HIDDEN], expert_w[:, :, 0:2 * HIDDEN],
                                                   scale[:, 0:1], None, ALU.mult))
            moe_w = {"router": router[:, :], "all": expert_w[:, :, :].rearrange("p e c -> p (e c)"), "ready": m}
            experts(core, "moe1", moe_w, dram)
            linear_attention(core, {"qkvo": lin_w[:, :, :], "qk_bias": lin_b[:, :], "v_bias": lin_rows[:, 0, :],
                                    "o_bias": lin_rows[:, 1, :]}, dram)
            experts(core, "moe2", moe_w, dram, t["out"].rearrange("(n p) c -> p n c", p=P))
        nc.build(bass_nc)


def constants():
    ar = np.arange
    inv_freq = (np.float32(1.0) / np.float32(10000.0) ** (ar(0, HD, 2, dtype=np.float32) / np.float32(HD))).astype(np.float32)
    freqs = ar(SEQ, dtype=np.float32)[:, None] * inv_freq[None, :]
    emb = np.concatenate([freqs, freqs], axis=-1).astype(np.float32)
    cos, sin = np.cos(emb), np.sin(emb)
    sign = np.where(ar(HD) % 2 == 0, -1.0, 1.0).astype(np.float32)
    head = ar(P) // HD
    own = (head[:, None] == ar(HEADS)[None, :]).astype(np.float32)
    spare = TOKENS * TOPK + ar(SLOT_TILES)[None, :] * P + ar(P)[:, None]
    f = np.float32
    return {
        "cos": np.tile(cos.T, (HEADS, 1)).astype(f), "sin": np.tile((sin * sign).T, (HEADS, 1)).astype(f),
        "ident": np.eye(P, dtype=f),
        "causal": (ar(P)[:, None] <= ar(P)[None, :]).astype(f),
        "before": (ar(P)[:, None] < ar(P)[None, :]).astype(f),
        "own_block": np.repeat(own, HD + 1, axis=1).astype(f),
        "slot_tile": np.tile(ar(SLOT_TILES, dtype=f), (P, 1)), "spare_row": spare.astype(f),
        "iota_p": np.tile(ar(P, dtype=f), (P, 1)),
        "number1": (ar(TILES * TOPK)[None, :] * P + ar(P)[:, None] + 1).astype(f),
        "same_head": (head[:, None] == head[None, :]).astype(f),
        "rev_expert": np.tile(ar(EXPERTS, 0, -1, dtype=f), (P, 1)),
    }


def layout(i):
    c = np.ascontiguousarray
    swap = np.arange(DIM) ^ 1
    qkv, qb = np.asarray(i["L0_attn_qkv_w"]), np.asarray(i["L0_attn_qkv_b"])
    a = {k: np.asarray(v) for k, v in i.items()}

    def cols(*ws):
        return c(np.stack([w.T for w in ws], axis=1))

    def rows(*bs):
        return c(np.broadcast_to(np.stack(bs)[None], (P, len(bs), DIM)))

    q, k, v = qkv[:DIM], qkv[DIM:2 * DIM], qkv[2 * DIM:]
    bq, bk, bv = qb[:DIM], qb[DIM:2 * DIM], qb[2 * DIM:]
    up = a["L1_ffn_w_up"].transpose(2, 0, 1)
    down = a["L1_ffn_w_down"].transpose(2, 0, 1).reshape(2, P, EXPERTS, DIM)
    return {
        "x": c(a["L0_attn_x"].reshape(TOKENS, DIM)),
        "mix_w": cols(a["L0_ffn_W_r"], a["L0_ffn_W_k"], a["L0_ffn_W_v"]),
        "mus": c(np.stack([a["L0_ffn_mu_r"], a["L0_ffn_mu_k"]], axis=1)),
        "qk_w": cols(q, q[swap], k, k[swap]), "attn_vo": cols(v, a["L0_attn_proj_w"]),
        "attn_b": c(np.stack([bq, bq[swap], bk, bk[swap]], axis=1)), "attn_rows": rows(bv, a["L0_attn_proj_b"]),
        "lin_w": cols(a["L1_attn_Wq"], a["L1_attn_Wk"], a["L1_attn_Wv"], a["L1_attn_Wo"]),
        "lin_b": c(np.stack([a["L1_attn_bq"], a["L1_attn_bk"]], axis=1)), "lin_rows": rows(a["L1_attn_bv"], a["L1_attn_bo"]),
        "norm_scale": c(a["L1_ffn_norm_scale"][:, None]), "router": c(a["L1_ffn_w_router"].T),
        "expert_w": c(np.concatenate([up, down[0], down[1]], axis=2)),
    }


def kernel(**inputs):
    import concourse.bacc as _bacc
    from concourse.bass_utils import run_bass_kernel_spmd as _run

    nc = _bacc.Bacc("TRN2", target_bir_lowering=False, num_devices=1)
    arrays = {**layout(inputs), **constants()}
    t = {n: nc.dram_tensor("in_" + n, a.shape, mybir.dt.from_np(a.dtype), kind="ExternalInput").ap()
         for n, a in arrays.items()}
    t["out"] = nc.dram_tensor("out_0", (TOKENS, DIM), F32, kind="ExternalOutput").ap()
    macaron_kernel(nc, t)
    r = _run(nc, [{"in_" + n: a for n, a in arrays.items()}], core_ids=[0])
    return r.results[0]["out_0"].reshape(BATCH, SEQ, DIM)
```
